# Optimizing a Trainium2 kernel written in Bass

```python
import numpy as np
import jax
import jax.numpy as jnp

def _softmax(x, axis=-1):
    return jax.nn.softmax(x, axis=axis)

def _gelu(x):
    return jax.nn.gelu(x, approximate=True)

def _silu(x):
    return jax.nn.silu(x)

def _sigmoid(x):
    return jax.nn.sigmoid(x)

def _layernorm(x, axis=-1, eps=1e-05):
    m = jnp.mean(x, axis=axis, keepdims=True)
    v = jnp.var(x, axis=axis, keepdims=True)
    return (x - m) / jnp.sqrt(v + eps)

def _scatter_add(tgt, idx, src, axis=0):
    return tgt.at[idx].add(src)

def _segment_sum(src, seg, n):
    return jax.ops.segment_sum(src, seg, n)
kernel_name = 'mk_decoder_preln_d2_seqx_r8_fcd771'

def setup_inputs(seed: int=0):
    np.random.seed(seed)
    _w = jnp.asarray

    def _rec_inputs():
        import jax
        import jax.numpy as jnp
        _rk = jax.random.key(seed)
        x = -0.0002928 + 1 * jax.random.normal(jax.random.fold_in(_rk, 1), (4, 512, 128), jnp.float32)
        _lenS = 512 - jax.random.randint(jax.random.fold_in(_rk, 7), (4,), 0, max(1, 512 // 4) + 1, jnp.int32)
        _lenS2 = 77 - jax.random.randint(jax.random.fold_in(_rk, 8), (4,), 0, max(1, 77 // 4) + 1, jnp.int32)
        _ctx_1024P = jax.random.normal(jax.random.fold_in(_rk, 11), (4, 16, 128), jnp.float32)
        _ctx_1024c = jax.random.dirichlet(jax.random.fold_in(_rk, 511), 0.3 * jnp.ones((16,), jnp.float32), (4, 77))
        _ctx_1024t = jnp.einsum('bsk,bkd->bsd', _ctx_1024c, _ctx_1024P)
        _ctx_1024t = _ctx_1024t * jax.lax.rsqrt(jnp.mean(jnp.square(_ctx_1024t)) + 1e-12) * 0.953939
        ctx_1024 = -1.78809e-06 + 0.0312453 * (_ctx_1024t + 0.3 * jax.random.normal(jax.random.fold_in(_rk, 611), (4, 77, 128), jnp.float32))
        return (x, ctx_1024)
    x, ctx_1024 = _rec_inputs()

    def _L0_attn_setup():
        import math
        import jax, jax.numpy as jnp
        import numpy as np
        N_HEAD = 16

        def _reference_tuple_inner(x, W_dq, W_uq, W_dkv, W_uk, W_uv, W_o):
            B, T, C = x.shape
            nh = N_HEAD
            hs = C // nh
            kvl = W_dkv.shape[0]
            k_eff = (W_dq.T @ W_uq.T @ W_uk).reshape(nh, hs, kvl)
            v_eff = (W_uv.T @ W_o.T).reshape(kvl, nh, hs).transpose(1, 0, 2)
            c_kv = x @ W_dkv.T
            q = (x @ W_dq.T @ W_uq.T).reshape(B, T, nh, hs).transpose(0, 2, 1, 3)
            q_lat = jnp.einsum('bhtd,hdl->bhtl', q, k_eff)
            attn = jnp.einsum('bhtl,bsl->bhts', q_lat, c_kv) / math.sqrt(hs)
            causal_mask = jnp.triu(jnp.ones((T, T), bool), k=1)
            attn = jnp.where(causal_mask[None, None], -jnp.inf, attn)
            attn = jax.nn.softmax(attn, axis=-1)
            ctx = jnp.einsum('bhts,bsl->bhtl', attn, c_kv)
            y = jnp.einsum('bhtl,hld->bhtd', ctx, v_eff).transpose(0, 2, 1, 3).reshape(B, T, C)
            return (y, c_kv)
        key = jax.random.key(seed)
        ks = jax.random.split(key, 7)
        B, T, C = (4, 256, 128)
        QL, KVL = (32, 32)
        s = 0.02
        return {'x': jax.random.normal(ks[0], (B, T, C), jnp.float32), 'W_dq': jax.random.normal(ks[1], (QL, C), jnp.float32) * s, 'W_uq': jax.random.normal(ks[2], (C, QL), jnp.float32) * s, 'W_dkv': jax.random.normal(ks[3], (KVL, C), jnp.float32) * s, 'W_uk': jax.random.normal(ks[4], (C, KVL), jnp.float32) * s, 'W_uv': jax.random.normal(ks[5], (C, KVL), jnp.float32) * s, 'W_o': jax.random.normal(ks[6], (C, C), jnp.float32) * s}
    _L0_attn_all = _L0_attn_setup()
    _L0_attn_in = {k: v for k, v in _L0_attn_all.items() if k in ('W_dq', 'W_uq', 'W_dkv', 'W_uk', 'W_uv', 'W_o')}
    del _L0_attn_all

    def _L0_xattn_setup():
        import jax, jax.numpy as jnp
        import numpy as np
        E, TPE, H, F = (64, 64, 128, 128)
        key = jax.random.key(seed)
        k1, k2, k3, k4 = jax.random.split(key, 4)
        scale = 1.0 / np.sqrt(H)
        return {'x': jax.random.normal(k1, (E, TPE, H), dtype=jnp.float32), 'w1': jax.random.normal(k2, (E, F, H), dtype=jnp.float32) * scale, 'v1': jax.random.normal(k3, (E, F, H), dtype=jnp.float32) * scale, 'w2': jax.random.normal(k4, (E, F, H), dtype=jnp.float32) * scale}
    _L0_xattn_all = _L0_xattn_setup()
    _L0_xattn_in = {k: v for k, v in _L0_xattn_all.items() if k in ()}
    del _L0_xattn_all

    def _L0_ffn_setup():
        import jax, jax.numpy as jnp
        import numpy as np
        B, S, H, F, E = (8, 256, 128, 512, 8)
        INIT_LAMBDA = 0.2
        key = jax.random.key(seed)
        ks = jax.random.split(key, 12)
        std = 0.02
        return {'hidden_states': jax.random.normal(ks[0], (B, S, H), jnp.float32), 'gate_w1': jax.random.normal(ks[1], (H, H), jnp.float32) * 0.01, 'gate_b1': jnp.zeros((H,), jnp.float32), 'gate_w2': jax.random.normal(ks[2], (E, H), jnp.float32) * 0.01, 'gate_b2': jnp.full((E,), INIT_LAMBDA, jnp.float32), 'W1': jax.random.normal(ks[3], (F, H), jnp.float32) * std, 'b1': jax.random.normal(ks[4], (F,), jnp.float32) * std, 'W2': jax.random.normal(ks[5], (H, F), jnp.float32) * std, 'b2': jax.random.normal(ks[6], (H,), jnp.float32) * std, 'TW1': jax.random.normal(ks[7], (E, F, H), jnp.float32) * std, 'Tb1': jax.random.normal(ks[8], (E, F), jnp.float32) * std, 'TW2': jax.random.normal(ks[9], (E, H, F), jnp.float32) * std, 'Tb2': jax.random.normal(ks[10], (E, H), jnp.float32) * std}
    _L0_ffn_all = _L0_ffn_setup()
    _L0_ffn_in = {k: v for k, v in _L0_ffn_all.items() if k in ('gate_w1', 'gate_b1', 'gate_w2', 'gate_b2', 'W1', 'b1', 'W2', 'b2', 'TW1', 'Tb1', 'TW2', 'Tb2')}
    del _L0_ffn_all

    def _L1_attn_setup():
        import jax, jax.numpy as jnp
        import numpy as np
        from jax import lax
        DIM = 128
        EXP = 2
        GMLP_EXP = 2
        K = 4
        HID = DIM * EXP
        GHID = DIM * GMLP_EXP
        ALPHA_LOG_SCALE = -8.0

        def init_forget_gate(size, a=0.001, b=0.1, lo=-9.0, hi=-4.323):
            x = np.log(np.expm1(np.linspace(a, b, size, dtype=np.float64)))
            x = (x - x.min()) / (x.max() - x.min())
            x = x * abs(hi - lo) + lo
            return jnp.asarray(x, dtype=jnp.float32)

        def _rmsnorm(x, gamma):
            n = jnp.sqrt(jnp.sum(x * x, axis=-1, keepdims=True))
            return gamma * jnp.sqrt(jnp.float32(x.shape[-1])) * (x / n)

        def _linear_recurrence(alpha, x):

            def combine(e1, e2):
                a1, b1 = e1
                a2, b2 = e2
                return (a1 * a2, a2 * b1 + b2)
            _, h = lax.associative_scan(combine, (alpha, x), axis=1)
            return h

        def _hawk_block(x, W_in, conv_w, conv_b, W_gates, b_gates, forget_base, W_out, gamma1, gamma2, W_grow, W_shrink):
            B, T, _ = x.shape
            xn = _rmsnorm(x, gamma1)
            z = xn @ W_in.T
            gate, xc = (z[..., :HID], z[..., HID:])
            xc_t = jnp.pad(xc.transpose(0, 2, 1), ((0, 0), (0, 0), (K - 1, 0)))
            xc = lax.conv_general_dilated(xc_t, conv_w, window_strides=(1,), padding='VALID', dimension_numbers=('NCH', 'OIH', 'NCH'), feature_group_count=HID)
            xc = (xc + conv_b[None, :, None]).transpose(0, 2, 1)
            g = xc @ W_gates.T + b_gates
            forget, inp = (g[..., :HID], g[..., HID:])
            alpha = jnp.exp(ALPHA_LOG_SCALE * jax.nn.softplus(forget_base) * jax.nn.sigmoid(forget))
            beta = jnp.sqrt(1.0 - alpha ** 2 + 1e-06)
            xs = beta * jax.nn.sigmoid(inp) * xc
            h = _linear_recurrence(alpha, xs)
            rglru_out = jax.nn.gelu(gate, approximate=False) * h @ W_out.T
            x = x + rglru_out
            xn2 = _rmsnorm(x, gamma2)
            gz = xn2 @ W_grow.T
            mgate, mx = (gz[..., :GHID], gz[..., GHID:])
            mlp_out = jax.nn.gelu(mgate, approximate=False) * mx @ W_shrink.T
            return x + mlp_out
        key = jax.random.key(seed)
        ks = jax.random.split(key, 10)
        B, T = (4, 256)
        x = jax.random.normal(ks[0], (B, T, DIM), dtype=jnp.float32)
        W_in = jax.random.normal(ks[1], (2 * HID, DIM), dtype=jnp.float32) * DIM ** (-0.5)
        conv_w = jax.random.normal(ks[2], (HID, 1, K), dtype=jnp.float32) * (1.0 / K) ** 0.5
        conv_b = jnp.zeros((HID,), dtype=jnp.float32)
        W_gates = jax.random.normal(ks[3], (2 * HID, HID), dtype=jnp.float32) * HID ** (-0.5)
        b_gates = jnp.zeros((2 * HID,), dtype=jnp.float32)
        forget_base = init_forget_gate(HID)
        W_out = jax.random.normal(ks[4], (DIM, HID), dtype=jnp.float32) * HID ** (-0.5)
        gamma1 = jnp.ones((DIM,), dtype=jnp.float32)
        gamma2 = jnp.ones((DIM,), dtype=jnp.float32)
        W_grow = jax.random.normal(ks[5], (2 * GHID, DIM), dtype=jnp.float32) * DIM ** (-0.5)
        W_shrink = jax.random.normal(ks[6], (DIM, GHID), dtype=jnp.float32) * GHID ** (-0.5)
        return {'x': x, 'W_in': W_in, 'conv_w': conv_w, 'conv_b': conv_b, 'W_gates': W_gates, 'b_gates': b_gates, 'forget_base': forget_base, 'W_out': W_out, 'gamma1': gamma1, 'gamma2': gamma2, 'W_grow': W_grow, 'W_shrink': W_shrink}
    _L1_attn_all = _L1_attn_setup()
    _L1_attn_in = {k: v for k, v in _L1_attn_all.items() if k in ('W_in', 'conv_w', 'conv_b', 'W_gates', 'b_gates', 'forget_base', 'W_out', 'gamma1', 'gamma2', 'W_grow', 'W_shrink')}
    del _L1_attn_all

    def _L1_xattn_setup():
        import jax, jax.numpy as jnp
        import numpy as np
        D1, D2, D3 = (128, 128, 128)
        key = jax.random.key(seed)
        k1, k2, kw, kb = jax.random.split(key, 4)
        x1 = jax.random.normal(k1, (8, 256, D1), dtype=jnp.float32)
        x2 = jax.random.normal(k2, (8, 256, D2), dtype=jnp.float32)
        bound = 1.0 / np.sqrt(D1 + D2)
        W = jax.random.uniform(kw, (D3, D1 + D2), minval=-bound, maxval=bound, dtype=jnp.float32)
        b = jax.random.uniform(kb, (D3,), minval=-bound, maxval=bound, dtype=jnp.float32)
        return {'x1': x1, 'x2': x2, 'W': W, 'b': b}
    _L1_xattn_all = _L1_xattn_setup()
    _L1_xattn_in = {k: v for k, v in _L1_xattn_all.items() if k in ('W', 'b')}
    del _L1_xattn_all

    def _L1_ffn_setup():
        import jax, jax.numpy as jnp
        import numpy as np
        B, S, D, F, E = (2, 256, 128, 512, 8)
        LN_EPS = 1e-05

        def _xavier(key, shape, fan_in, fan_out):
            a = np.sqrt(6.0 / (fan_in + fan_out))
            return jax.random.uniform(key, shape, jnp.float32, -a, a)
        key = jax.random.key(seed)
        ks = jax.random.split(key, 8)
        tgt = jax.random.normal(ks[0], (B, S, D), jnp.float32)
        router_w = _xavier(ks[1], (E, D), D, E)
        router_b = jnp.zeros((E,), jnp.float32)
        w1 = _xavier(ks[2], (E, D, F), D, F)
        b1 = jnp.zeros((E, F), jnp.float32)
        w2 = _xavier(ks[3], (E, F, D), F, D)
        b2 = jnp.zeros((E, D), jnp.float32)
        gamma = jnp.ones((D,), jnp.float32)
        beta = jnp.zeros((D,), jnp.float32)
        return {'tgt': tgt, 'router_w': router_w, 'router_b': router_b, 'w1': w1, 'b1': b1, 'w2': w2, 'b2': b2, 'gamma': gamma, 'beta': beta}
    _L1_ffn_all = _L1_ffn_setup()
    _L1_ffn_in = {k: v for k, v in _L1_ffn_all.items() if k in ('router_w', 'router_b', 'w1', 'b1', 'w2', 'b2', 'gamma', 'beta')}
    del _L1_ffn_all
    return {'x': x, 'ctx_1024': ctx_1024, 'L0_attn_W_dq': _L0_attn_in['W_dq'], 'L0_attn_W_uq': _L0_attn_in['W_uq'], 'L0_attn_W_dkv': _L0_attn_in['W_dkv'], 'L0_attn_W_uk': _L0_attn_in['W_uk'], 'L0_attn_W_uv': _L0_attn_in['W_uv'], 'L0_attn_W_o': _L0_attn_in['W_o'], 'L0_ffn_gate_w1': _L0_ffn_in['gate_w1'], 'L0_ffn_gate_b1': _L0_ffn_in['gate_b1'], 'L0_ffn_gate_w2': _L0_ffn_in['gate_w2'], 'L0_ffn_gate_b2': _L0_ffn_in['gate_b2'], 'L0_ffn_W1': _L0_ffn_in['W1'], 'L0_ffn_b1': _L0_ffn_in['b1'], 'L0_ffn_W2': _L0_ffn_in['W2'], 'L0_ffn_b2': _L0_ffn_in['b2'], 'L0_ffn_TW1': _L0_ffn_in['TW1'], 'L0_ffn_Tb1': _L0_ffn_in['Tb1'], 'L0_ffn_TW2': _L0_ffn_in['TW2'], 'L0_ffn_Tb2': _L0_ffn_in['Tb2'], 'L1_attn_W_in': _L1_attn_in['W_in'], 'L1_attn_conv_w': _L1_attn_in['conv_w'], 'L1_attn_conv_b': _L1_attn_in['conv_b'], 'L1_attn_W_gates': _L1_attn_in['W_gates'], 'L1_attn_b_gates': _L1_attn_in['b_gates'], 'L1_attn_forget_base': _L1_attn_in['forget_base'], 'L1_attn_W_out': _L1_attn_in['W_out'], 'L1_attn_gamma1': _L1_attn_in['gamma1'], 'L1_attn_gamma2': _L1_attn_in['gamma2'], 'L1_attn_W_grow': _L1_attn_in['W_grow'], 'L1_attn_W_shrink': _L1_attn_in['W_shrink'], 'L1_xattn_W': _L1_xattn_in['W'], 'L1_xattn_b': _L1_xattn_in['b'], 'L1_ffn_router_w': _L1_ffn_in['router_w'], 'L1_ffn_router_b': _L1_ffn_in['router_b'], 'L1_ffn_w1': _L1_ffn_in['w1'], 'L1_ffn_b1': _L1_ffn_in['b1'], 'L1_ffn_w2': _L1_ffn_in['w2'], 'L1_ffn_b2': _L1_ffn_in['b2'], 'L1_ffn_gamma': _L1_ffn_in['gamma'], 'L1_ffn_beta': _L1_ffn_in['beta']}

def reference(x, ctx_1024, L0_attn_W_dq, L0_attn_W_uq, L0_attn_W_dkv, L0_attn_W_uk, L0_attn_W_uv, L0_attn_W_o, L0_ffn_gate_w1, L0_ffn_gate_b1, L0_ffn_gate_w2, L0_ffn_gate_b2, L0_ffn_W1, L0_ffn_b1, L0_ffn_W2, L0_ffn_b2, L0_ffn_TW1, L0_ffn_Tb1, L0_ffn_TW2, L0_ffn_Tb2, L1_attn_W_in, L1_attn_conv_w, L1_attn_conv_b, L1_attn_W_gates, L1_attn_b_gates, L1_attn_forget_base, L1_attn_W_out, L1_attn_gamma1, L1_attn_gamma2, L1_attn_W_grow, L1_attn_W_shrink, L1_xattn_W, L1_xattn_b, L1_ffn_router_w, L1_ffn_router_b, L1_ffn_w1, L1_ffn_b1, L1_ffn_w2, L1_ffn_b2, L1_ffn_gamma, L1_ffn_beta):
    import jax
    import jax.numpy as jnp

    def _L0_attn_ref(x, W_dq, W_uq, W_dkv, W_uk, W_uv, W_o):
        import math
        import jax, jax.numpy as jnp
        import numpy as np
        N_HEAD = 16

        def _reference_tuple_inner(x, W_dq, W_uq, W_dkv, W_uk, W_uv, W_o):
            B, T, C = x.shape
            nh = N_HEAD
            hs = C // nh
            kvl = W_dkv.shape[0]
            k_eff = (W_dq.T @ W_uq.T @ W_uk).reshape(nh, hs, kvl)
            v_eff = (W_uv.T @ W_o.T).reshape(kvl, nh, hs).transpose(1, 0, 2)
            c_kv = x @ W_dkv.T
            q = (x @ W_dq.T @ W_uq.T).reshape(B, T, nh, hs).transpose(0, 2, 1, 3)
            q_lat = jnp.einsum('bhtd,hdl->bhtl', q, k_eff)
            attn = jnp.einsum('bhtl,bsl->bhts', q_lat, c_kv) / math.sqrt(hs)
            causal_mask = jnp.triu(jnp.ones((T, T), bool), k=1)
            attn = jnp.where(causal_mask[None, None], -jnp.inf, attn)
            attn = jax.nn.softmax(attn, axis=-1)
            ctx = jnp.einsum('bhts,bsl->bhtl', attn, c_kv)
            y = jnp.einsum('bhtl,hld->bhtd', ctx, v_eff).transpose(0, 2, 1, 3).reshape(B, T, C)
            return (y, c_kv)
        return _reference_tuple_inner(x, W_dq, W_uq, W_dkv, W_uk, W_uv, W_o)[0]

    def _L0_xattn_ref(x, w1, v1, w2):
        import jax, jax.numpy as jnp
        import numpy as np
        E, TPE, H, F = (64, 64, 128, 128)
        h1 = jnp.einsum('eth,efh->etf', x, w1)
        h2 = jnp.einsum('eth,efh->etf', x, v1)
        g = jax.nn.gelu(h1, approximate=False) * h2
        return jnp.einsum('etf,efh->eth', g, w2)

    def _L0_ffn_ref(hidden_states, gate_w1, gate_b1, gate_w2, gate_b2, W1, b1, W2, b2, TW1, Tb1, TW2, Tb2):
        import jax, jax.numpy as jnp
        import numpy as np
        B, S, H, F, E = (8, 256, 128, 512, 8)
        INIT_LAMBDA = 0.2
        x = hidden_states
        h = jax.nn.relu(jnp.einsum('bsh,oh->bso', x, gate_w1) + gate_b1)
        g = jnp.einsum('bso,eo->bse', h, gate_w2) + gate_b2
        g = g.mean(axis=1)
        mW1 = W1 + jnp.einsum('be,efh->bfh', g, TW1)
        mb1 = b1 + g @ Tb1
        mW2 = W2 + jnp.einsum('be,ehf->bhf', g, TW2)
        mb2 = b2 + g @ Tb2
        u = jax.nn.gelu(jnp.einsum('bsh,bfh->bsf', x, mW1) + mb1[:, None, :])
        out = jnp.einsum('bsf,bhf->bsh', u, mW2) + mb2[:, None, :]
        return out

    def _L1_attn_ref(x, W_in, conv_w, conv_b, W_gates, b_gates, forget_base, W_out, gamma1, gamma2, W_grow, W_shrink):
        import jax, jax.numpy as jnp
        import numpy as np
        from jax import lax
        DIM = 128
        EXP = 2
        GMLP_EXP = 2
        K = 4
        HID = DIM * EXP
        GHID = DIM * GMLP_EXP
        ALPHA_LOG_SCALE = -8.0

        def init_forget_gate(size, a=0.001, b=0.1, lo=-9.0, hi=-4.323):
            x = np.log(np.expm1(np.linspace(a, b, size, dtype=np.float64)))
            x = (x - x.min()) / (x.max() - x.min())
            x = x * abs(hi - lo) + lo
            return jnp.asarray(x, dtype=jnp.float32)

        def _rmsnorm(x, gamma):
            n = jnp.sqrt(jnp.sum(x * x, axis=-1, keepdims=True))
            return gamma * jnp.sqrt(jnp.float32(x.shape[-1])) * (x / n)

        def _linear_recurrence(alpha, x):

            def combine(e1, e2):
                a1, b1 = e1
                a2, b2 = e2
                return (a1 * a2, a2 * b1 + b2)
            _, h = lax.associative_scan(combine, (alpha, x), axis=1)
            return h

        def _hawk_block(x, W_in, conv_w, conv_b, W_gates, b_gates, forget_base, W_out, gamma1, gamma2, W_grow, W_shrink):
            B, T, _ = x.shape
            xn = _rmsnorm(x, gamma1)
            z = xn @ W_in.T
            gate, xc = (z[..., :HID], z[..., HID:])
            xc_t = jnp.pad(xc.transpose(0, 2, 1), ((0, 0), (0, 0), (K - 1, 0)))
            xc = lax.conv_general_dilated(xc_t, conv_w, window_strides=(1,), padding='VALID', dimension_numbers=('NCH', 'OIH', 'NCH'), feature_group_count=HID)
            xc = (xc + conv_b[None, :, None]).transpose(0, 2, 1)
            g = xc @ W_gates.T + b_gates
            forget, inp = (g[..., :HID], g[..., HID:])
            alpha = jnp.exp(ALPHA_LOG_SCALE * jax.nn.softplus(forget_base) * jax.nn.sigmoid(forget))
            beta = jnp.sqrt(1.0 - alpha ** 2 + 1e-06)
            xs = beta * jax.nn.sigmoid(inp) * xc
            h = _linear_recurrence(alpha, xs)
            rglru_out = jax.nn.gelu(gate, approximate=False) * h @ W_out.T
            x = x + rglru_out
            xn2 = _rmsnorm(x, gamma2)
            gz = xn2 @ W_grow.T
            mgate, mx = (gz[..., :GHID], gz[..., GHID:])
            mlp_out = jax.nn.gelu(mgate, approximate=False) * mx @ W_shrink.T
            return x + mlp_out
        return _hawk_block(x, W_in, conv_w, conv_b, W_gates, b_gates, forget_base, W_out, gamma1, gamma2, W_grow, W_shrink)

    def _L1_xattn_ref(x1, x2, W, b):
        import jax, jax.numpy as jnp
        import numpy as np
        D1, D2, D3 = (128, 128, 128)
        d1 = x1.shape[-1]
        W1 = W[:, :d1]
        W2 = W[:, d1:]
        part1 = jnp.einsum('bld,ed->ble', x1, W1)
        part2 = jnp.einsum('bld,ed->be', x2, W2) / x2.shape[1]
        return part1 + part2[:, None, :] + b

    def _L1_ffn_ref(tgt, router_w, router_b, w1, b1, w2, b2, gamma, beta):
        import jax, jax.numpy as jnp
        import numpy as np
        B, S, D, F, E = (2, 256, 128, 512, 8)
        LN_EPS = 1e-05

        def _xavier(key, shape, fan_in, fan_out):
            a = np.sqrt(6.0 / (fan_in + fan_out))
            return jax.random.uniform(key, shape, jnp.float32, -a, a)
        logits = jnp.einsum('bsd,ed->bse', tgt, router_w) + router_b
        rw = jax.nn.softmax(logits, axis=-1)
        rw = jnp.zeros_like(rw).at[..., 0].set(1.0)
        h = jax.nn.relu(jnp.einsum('bsd,edf->besf', tgt, w1) + b1[None, :, None, :])
        eo = jnp.einsum('besf,efd->besd', h, w2) + b2[None, :, None, :]
        tgt2 = jnp.einsum('besd,bse->bsd', eo, rw)
        x = tgt + tgt2
        mean = jnp.mean(x, axis=-1, keepdims=True)
        var = jnp.mean(jnp.square(x - mean), axis=-1, keepdims=True)
        return (x - mean) * jax.lax.rsqrt(var + LN_EPS) * gamma + beta
    x = x + _L0_attn_ref(_layernorm(x, axis=-1), L0_attn_W_dq, L0_attn_W_uq, L0_attn_W_dkv, L0_attn_W_uk, L0_attn_W_uv, L0_attn_W_o)
    x = x + _L0_xattn_ref(_layernorm(x, axis=-1), ctx_1024, ctx_1024, ctx_1024)
    x = x + _L0_ffn_ref(_layernorm(x, axis=-1), L0_ffn_gate_w1, L0_ffn_gate_b1, L0_ffn_gate_w2, L0_ffn_gate_b2, L0_ffn_W1, L0_ffn_b1, L0_ffn_W2, L0_ffn_b2, L0_ffn_TW1, L0_ffn_Tb1, L0_ffn_TW2, L0_ffn_Tb2)
    x = x + _L1_attn_ref(_layernorm(x, axis=-1), L1_attn_W_in, L1_attn_conv_w, L1_attn_conv_b, L1_attn_W_gates, L1_attn_b_gates, L1_attn_forget_base, L1_attn_W_out, L1_attn_gamma1, L1_attn_gamma2, L1_attn_W_grow, L1_attn_W_shrink)
    x = x + _L1_xattn_ref(_layernorm(x, axis=-1), ctx_1024, L1_xattn_W, L1_xattn_b)
    x = x + _L1_ffn_ref(_layernorm(x, axis=-1), L1_ffn_router_w, L1_ffn_router_b, L1_ffn_w1, L1_ffn_b1, L1_ffn_w2, L1_ffn_b2, L1_ffn_gamma, L1_ffn_beta)
    return x

_drawn_inputs = setup_inputs


def setup_inputs(seed=0):
    import zlib

    import numpy as np

    out = dict(_drawn_inputs(seed))
    spreads = {'L0_ffn_gate_b1': (0.0, 0.8),
     'L0_ffn_gate_b2': (0.20000000298023224, 0.6),
     'L1_attn_conv_b': (0.0, 0.1),
     'L1_attn_b_gates': (0.0, 0.583),
     'L1_attn_gamma1': (1.0, 0.2),
     'L1_attn_gamma2': (1.0, 0.2),
     'L1_ffn_router_b': (0.0, 0.1),
     'L1_ffn_b1': (0.0, 0.33),
     'L1_ffn_b2': (0.0, 0.287),
     'L1_ffn_gamma': (1.0, 0.2),
     'L1_ffn_beta': (0.0, 0.37)}
    factors = {'L0_attn_W_dq': 8.0,
     'L0_attn_W_uq': 8.0,
     'L0_attn_W_dkv': 8.0,
     'L0_attn_W_uk': 8.0,
     'L0_attn_W_uv': 8.0,
     'L0_attn_W_o': 8.0,
     'L0_ffn_gate_w1': 8.0,
     'L0_ffn_gate_w2': 8.0,
     'L0_ffn_b1': 4.223,
     'L0_ffn_Tb1': 8.0,
     'L1_xattn_b': 3.684,
     'L0_ffn_b2': 4.246}
    for name, (base, spread) in spreads.items():
        noise = np.random.default_rng([zlib.crc32(name.encode()), seed]).standard_normal(out[name].shape)
        drawn = base * np.exp(spread * noise) if base else spread * noise
        out[name] = jnp.asarray(drawn.astype(out[name].dtype))
    for name, factor in factors.items():
        out[name] = (out[name] * factor).astype(out[name].dtype)
    return out
```

```python
import numpy as np
from contextlib import ExitStack

import concourse.bass as bass
from concourse import mybir

P = 128
B = 4
T = 512
NT = T // P
NH = 16
HS = P // NH
NG = 4
HG = NH // NG
LAT = 32
VW = 32
CTX = 77
NE = 8
FC = 4
HC = 2
KCONV = 4
GW = HG * (T + 384 + 256 + 128)
UNIT = 1024
NU = GW // UNIT
EPS = 1e-5
NEG = -1e30

F32 = mybir.dt.float32
F32R = mybir.dt.float32r
BF16 = mybir.dt.bfloat16
ALU = mybir.AluOpType
ACT = mybir.ActivationFunctionType
AX = mybir.AxisListType

ATTN_PARTS = [("wdq", LAT, P), ("wuqT", LAT, P), ("wdkv", LAT, P), ("wuk", P, LAT), ("wuv", P, LAT),
              ("woT", P, P), ("ident", P, P), ("mask", P, P), ("kone", P, 1), ("headcol", P, HG)]
SELECTIONS = ("selqh", "selql", "selkh", "selkl")
REST_PARTS = [("gw1T", P, P), ("gb1", P, 1), ("gw2T", P, NE), ("gb2", NE, 1), ("W1T", P, FC * P),
              ("b1", P, FC), ("W2T", P, FC * P), ("tb2x", NE + 1, P), ("Tb1", P, FC * NE),
              ("winT", P, 4 * P), ("gamma1", P, 1), ("convw", P, HC * KCONV), ("convb", P, HC),
              ("wgT", P, HC * 4 * P), ("bg", P, 4), ("fb", P, HC), ("woutT", P, HC * P),
              ("gamma2", P, 1), ("growT", P, 4 * P), ("shrinkT", P, HC * P),
              ("x1T", P, P), ("x2T", P, P), ("xb", 1, P),
              ("m1", P, FC * P), ("mb1", P, FC), ("m2", P, FC * P)]


def columns(parts):
    at, out = 0, {}
    for name, rows, width in parts:
        out[name] = (at, rows, width)
        at += width
    return out, at


ATTN_AT, ATTN_W = columns(ATTN_PARTS)
REST_AT, REST_W = columns(REST_PARTS)

def segments(unit):
    width = [512, 384, 256, 128]
    if unit < 2:
        return [(j, 0, 512 * (j % 2), width[0]) for j in (2 * unit, 2 * unit + 1)]
    if unit < 4:
        return [(j, r, 512 * (j % 2) + c, width[r])
                for j in (2 * unit - 4, 2 * unit - 3) for r, c in ((1, 0), (3, 384))]
    return [(j, 2, 256 * j, width[2]) for j in range(HG)]


PER = dict(
    x_loaded=16, ctx_loaded=32,
    ln_var=8, ln_rstd=8, ln_norm=4 * 7, lnT_psum=7, lnT_ready=7,
    qkv_psum=3, split_hi=2, split_lo=2, v_ready=1,
    stack_psum=4, kstack_ready=4, qstack_ready=4, kmask_ready=16,
    s_psum=NG * NU, max_done=NG * NU, e_psum=NG * NU, exp_done=NG * NU, sel_done=NG * NU,
    m_psum=4, mstack_ready=4, av_psum=4, av_ready=4, avT_psum=4, av_norm=4,
    dve=31, pool=24,
    xa_psum=1, xa_gelu=1, xa_prod=1,
    gate_psum=1, gate_sum=1, gate_bcast=1, g_psum=1, g_ready=1,
    mix1_done=1, mix2_done=1, mb1_done=1, u_psum=4, u_ready=4,
    z_psum=4, zg_gelu=1, conv0=2, conv_done=1, gates_psum=4, gates_tanh=4, alpha_done=1,
    asq_done=1, beta_done=1, hm_done=1, hx_done=1, grow_psum=4, mg_gelu=1, mm_done=1,
    h_psum=4, h_ready=4, p2_psum=1, p2_ready=1, csum_ready=1,
    res_psum=6, res_done=6, side_done=4, out_ready=1, out_stored=16, batch_done=1,
)


def decoder_kernel(nc, x, ctxn, ctxT, attnw, selw, restw, rowsw, tw1, tw2, gb2row, out):
    es = ExitStack()
    with es:
        def sb(name, shape, dt=F32):
            return es.enter_context(nc.sbuf_tensor(name, shape, dt))

        aw = sb("aw", [P, ATTN_W])
        rw = sb("rw", [P, REST_W])
        rows = sb("rows", [P, 3 * P])
        tw1_sb = sb("tw1_sb", [P, NE, FC * P])
        tw2_sb = sb("tw2_sb", [P, NE, FC * P])
        gb2_sb = sb("gb2_sb", [P, NE])

        def wa(name):
            c, r, w = ATTN_AT[name]
            return aw[0:r, c:c + w]

        def wr(name):
            c, r, w = REST_AT[name]
            return rw[0:r, c:c + w]

        ident_r = sb("ident_r", [P, P], F32R)
        ident_b = sb("ident_b", [P, P], BF16)
        mask_b = sb("mask_b", [P, P], BF16)
        sel_r = sb("sel_r", [P, 4, NG, P], F32R)
        wq_T = sb("wq_T", [P, P])
        wk_T = sb("wk_T", [P, P])
        wv_T = sb("wv_T", [P, P])
        fold_a = sb("fold_a", [P, P])
        fold_b = sb("fold_b", [LAT, P])
        fold_c = sb("fold_c", [LAT, P])
        ones = sb("ones", [P, P])
        halfpow = sb("halfpow", [P, 2 * NT])
        decay = sb("decay", [P, 12, HC])
        hdecay = sb("hdecay", [P, HC])
        hbg = sb("hbg", [P, 4])
        sqrt_bias = sb("sqrt_bias", [P, 1])

        probs = sb("probs", [P, 2, GW])

        def after_probs(c, n):
            return probs[:].rearrange("p a n -> p (a n)")[:, c:c + n * T].rearrange("p (n t) -> p n t", n=n)

        xin = sb("xin", [P, NT, P])
        ctxn_sb = sb("ctxn_sb", [CTX, P])
        ctxT_sb = sb("ctxT_sb", [P, CTX])
        stats = sb("stats", [P, NT, 6])
        meanvar = sb("meanvar", [P, NT, 2])
        vareps = sb("vareps", [P, 2 * NT])
        rstd = sb("rstd", [P, 2 * NT])
        xn = sb("xn", [P, NT, P])
        xT = sb("xT", [P, T])
        qk_hi = sb("qk_hi", [P, 2, T], F32R)
        qk_lo = sb("qk_lo", [P, 2, T], F32R)
        vx = sb("vx", [P, NT, NH, VW])
        kstack = sb("kstack", [P, NG, T])
        qstack = sb("qstack", [P, NG, T], F32R)
        mstack = sb("mstack", [P, 2, T], F32R)
        km = sb("km", [P, 2 * HG, T], F32R)
        negmax = sb("negmax", [P, NG, NT, P], F32R)
        av_sb = sb("av_sb", [P, T])
        rden = sb("rden", [P, NT * HG])
        y = sb("y", [P, NT, P])
        x1 = sb("x1", [P, NT, P])
        x2 = sb("x2", [P, NT, P])
        x3 = sb("x3", [P, NT, P])
        x4 = sb("x4", [P, NT, P])
        x5 = sb("x5", [P, NT, P])
        side = sb("side", [P, NT, P])
        side2 = sb("side2", [P, NT, P])
        hsum = sb("hsum", [P, 1])
        hsum_b = sb("hsum_b", [P, P])
        gvec = sb("gvec", [P, NE])
        g9 = sb("g9", [NE + 1, P])
        mw1 = sb("mw1", [P, FC * P])
        mw2 = sb("mw2", [P, FC * P])
        mw2_t = sb("mw2_t", [P, FC * P])
        mb1_t = sb("mb1_t", [P, FC, NE])
        mb1_s = sb("mb1_s", [P, FC])
        mb1_c = sb("mb1_c", [P, FC])
        hid = after_probs(0, 4)
        th = hid
        y3 = y
        gate_g = after_probs(2048, 2)
        xc = after_probs(3072, 2)
        alpha = after_probs(4096, 2)
        asq = after_probs(5120, 2)
        beta = asq
        xa_g = gate_g[0:CTX, 0, :]
        xa_p = gate_g[0:CTX, 1, :]
        junk = xc[:, 0, :]
        rec = after_probs(6144, 2)
        hm = after_probs(7168, 2)
        hx = sb("hx", [P, NT, P])
        sumsq = sb("sumsq", [P, NT])
        csum = sb("csum", [P, 1])
        csum_b = sb("csum_b", [P, P])
        p2 = sb("p2", [P, P])
        o = sb("o", [P, NT, P])
        flag = sb("flag", [P, 1])

        ps = es.enter_context(nc.psum_tensor("ps", [P, 8, 512], F32))

        def bank(i, n=1):
            return ps[:, i, :] if n == 1 else ps[:, i:i + n, :]

        names = list(PER) + ["attnw_loaded", "selw_loaded", "restw_loaded", "fold_psum", "fold_copied", "const_ready",
                             "pool_const", "dve_const", "act_const", "vx_ready"]
        S = {n: es.enter_context(nc.semaphore(n)) for n in names}

        block = es.enter_context(nc.Block())

        x_v = x.rearrange("b (i p) c -> b p i c", p=P)
        out_v = out.rearrange("b (i p) c -> b p i c", p=P)

        def nth(name, b, k):
            return b * PER[name] + k

        order = [("S", 0, u) for u in range(NU)]
        for g in range(1, NG):
            for u in range(NU):
                order += [("S", g, u), ("T", g - 1, u)]
        order += [("T", NG - 1, u) for u in range(NU)]
        place = {k: n for n, k in enumerate(order)}

        def ring_of(kind, g, u):
            return place[(kind, g, u)]

        @block.sync
        def _(sp):
            sp.dma_start(xin[:], x_v[0]).then_inc(S["x_loaded"], 16)
            sp.dma_start(aw[:], attnw).then_inc(S["attnw_loaded"], 16)
            sp.dma_start(probs[:, 0, 0:4 * NG * P], selw).then_inc(S["selw_loaded"], 16)
            sp.dma_start(ctxT_sb[:], ctxT[0]).then_inc(S["ctx_loaded"], 16)
            sp.dma_start(ctxn_sb[:], ctxn[0]).then_inc(S["ctx_loaded"], 16)
            sp.dma_start(rw[:], restw).then_inc(S["restw_loaded"], 16)
            sp.dma_start(gb2_sb[:], gb2row.broadcast_to([P, NE])).then_inc(S["restw_loaded"], 16)
            sp.dma_start(tw1_sb[:], tw1).then_inc(S["restw_loaded"], 16)
            sp.dma_start(tw2_sb[:], tw2).then_inc(S["restw_loaded"], 16)
            sp.dma_start(rows[:], rowsw.broadcast_to([P, 3 * P])).then_inc(S["restw_loaded"], 16)
            with sp.Fori(0, B - 1) as b:
                sp.wait_ge(S["res_done"], nth("res_done", b, 1))
                sp.dma_start(xin[:], x_v[b + 1]).then_inc(S["x_loaded"], 16)
                sp.wait_ge(S["out_ready"], nth("out_ready", b, 1))
                sp.dma_start(out_v[b], o[:]).then_inc(S["out_stored"], 16)
                sp.dma_start(ctxT_sb[:], ctxT[b + 1]).then_inc(S["ctx_loaded"], 16)
                sp.dma_start(ctxn_sb[:], ctxn[b + 1]).then_inc(S["ctx_loaded"], 16)
            sp.wait_ge(S["out_ready"], B)
            sp.dma_start(out_v[B - 1], o[:]).then_inc(S["out_stored"], 16)
            sp.wait_ge(S["out_stored"], 16 * B)

        @block.gpsimd
        def _(pool):
            pool.memset(vx[:], 0.0).then_inc(S["pool_const"], 1)
            pool.wait_ge(S["pool_const"], 1)
            pool.memset(vx[:, :, :, HS:HS + 1], 1.0).then_inc(S["vx_ready"], 1)
            pool.memset(negmax[:].bitcast(F32), 0.0).then_inc(S["pool_const"], 1)
            pool.memset(ones[:], 1.0).then_inc(S["pool_const"], 1)
            pool.memset(g9[:], 1.0).then_inc(S["pool_const"], 1)
            pool.memset(halfpow[:], -0.5).then_inc(S["pool_const"], 1)
            pool.memset(sqrt_bias[:], 1.0 + 1e-6).then_inc(S["pool_const"], 1)

            count = dict(ln=0, side=0, n=0)

            spare = pool.alloc_register("pool_spare")
            pool.reg_mov(spare, 0)

            def wait_apart(sem, value):
                pool.reg_mov(spare, value)
                value = pool.snap(spare)
                pool.wait_ge(S["pool_const"], 6)
                pool.wait_ge(sem, value)

            with pool.Fori(0, B) as b:
                def step(ins, separate=False):
                    ins.then_inc(S["pool"], 1)
                    count["n"] += 1
                    if separate:
                        wait_apart(S["pool"], nth("pool", b, count["n"]))
                    else:
                        pool.wait_ge(S["pool"], nth("pool", b, count["n"]))

                def rstd_of(scale, eps, both=False):
                    wait_apart(S["ln_var"], nth("ln_var", b, count["ln"] + 1))
                    if scale is None:
                        step(pool.tensor_scalar(vareps[:, 0:NT], meanvar[:, :, 1], 1.0, eps, ALU.mult, ALU.add),
                             separate=both)
                        if both:
                            step(pool.tensor_scalar(vareps[:, NT:2 * NT], meanvar[:, :, 1], 1.0, 0.0,
                                                    ALU.mult, ALU.add))
                    else:
                        step(pool.tensor_scalar(vareps[:, 0:NT], sumsq[:], scale, 0.0, ALU.mult, ALU.add))
                    n = 2 * NT if both else NT
                    pool.tensor_tensor(rstd[:, 0:n], vareps[:, 0:n], halfpow[:, 0:n], ALU.pow)\
                        .then_inc(S["ln_rstd"], 1)
                    count["ln"] += 1

                def beside(*args):
                    pool.tensor_tensor(*args).then_inc(S["side_done"], 1)
                    count["side"] += 1

                count.update(ln=0, side=0, n=0)
                pool.wait_ge(S["batch_done"], b + 1)
                rstd_of(None, EPS)
                for g in range(NG):
                    for u in range(NU):
                        wait_apart(S["exp_done"], nth("exp_done", b, g * NU + u + 1))
                        seg = probs[:, g % 2, u * UNIT:(u + 1) * UNIT]
                        if u < 2:
                            v = seg.rearrange("p (j t) -> p j t", j=2)[:, :, 0:P]
                            pat = [[0, 2], [1, P]]
                        elif u < 4:
                            v = seg.rearrange("p (j t) -> p j t", j=2)
                            pool.affine_select(out=v[:, :, 384:512], in_=v[:, :, 384:512], pattern=[[0, 2], [1, P]],
                                               compare_op=ALU.is_ge, fill=0.0, base=0, channel_multiplier=-1)
                            v = v[:, :, 0:P]
                            pat = [[0, 2], [1, P]]
                        else:
                            v = seg.rearrange("p (j t) -> p j t", j=4)[:, :, 0:P]
                            pat = [[0, 4], [1, P]]
                        pool.affine_select(out=v, in_=v, pattern=pat, compare_op=ALU.is_ge, fill=0.0, base=0,
                                           channel_multiplier=-1).then_inc(S["sel_done"], 1)
                rstd_of(None, EPS)
                rstd_of(None, EPS)
                wait_apart(S["g_ready"], nth("g_ready", b, 1))
                for e in range(NE):
                    step(pool.tensor_scalar(mw2_t[:], tw2_sb[:, e, :], gvec[:, e:e + 1], 1.0, ALU.mult, ALU.mult))
                    last = pool.tensor_tensor(mw2[:], wr("W2T") if e == 0 else mw2[:], mw2_t[:], ALU.add)
                    if e < NE - 1:
                        step(last, separate=True)
                last.then_inc(S["mix2_done"], 1)
                rstd_of(None, EPS, both=True)
                pool.wait_ge(S["alpha_done"], nth("alpha_done", b, 1))
                pool.tensor_tensor(asq[:], alpha[:], alpha[:], ALU.mult).then_inc(S["asq_done"], 1)
                pool.wait_ge(S["hx_done"], nth("hx_done", b, 1))
                beside(side[:], x3[:], hx[:], ALU.add)
                rstd_of(1.0 / P, 0.0)
                pool.wait_ge(S["res_done"], nth("res_done", b, 4))
                pool.wait_ge(S["p2_ready"], nth("p2_ready", b, 1))
                for i in range(NT):
                    last = pool.tensor_tensor(side2[:, i, :], x4[:, i, :], p2[:], ALU.add)
                last.then_inc(S["side_done"], 1)
                rstd_of(None, EPS)
                rstd_of(None, EPS)
                pool.wait_ge(S["ln_norm"], nth("ln_norm", b, 4 * 7))
                for i in range(NT):
                    last = pool.tensor_tensor(side[:, i, :], xn[:, i, :], rows[:, 0:P], ALU.add)
                last.then_inc(S["side_done"], 1)
                for i in range(NT):
                    last = pool.tensor_tensor(side2[:, i, :], x5[:, i, :], rows[:, 2 * P:3 * P], ALU.add)
                last.then_inc(S["side_done"], 1)
                rstd_of(None, EPS)
                assert count["n"] == PER["pool"], count["n"]

        @block.scalar
        def _(act):
            act.wait_ge(S["attnw_loaded"], 16)
            act.activation(ident_b[:], wa("ident"), ACT.Copy).then_inc(S["act_const"], 1)
            act.activation(mask_b[:], wa("mask"), ACT.Copy).then_inc(S["act_const"], 1)
            act.activation(ident_r[:], wa("ident"), ACT.Copy).then_inc(S["act_const"], 1)
            act.wait_ge(S["selw_loaded"], 16)
            for n in range(4):
                act.activation(sel_r[:, n, :, :],
                               probs[:, 0, n * NG * P:(n + 1) * NG * P].rearrange("p (g c) -> p g c", g=NG),
                               ACT.Copy).then_inc(S["act_const"], 1)
            act.wait_ge(S["restw_loaded"], 80)
            act.activation(decay[:, 0, :], wr("fb"), ACT.Abs).then_inc(S["act_const"], 1)
            act.wait_ge(S["act_const"], 8)
            act.activation(decay[:, 1, :], decay[:, 0, :], ACT.Exp, scale=-1.0).then_inc(S["act_const"], 1)

            with act.Fori(0, B) as b:
                n_ln = 0

                def evac_lnT():
                    nonlocal n_ln
                    n_ln += 1
                    act.wait_ge(S["lnT_psum"], nth("lnT_psum", b, n_ln))
                    act.activation(xT[:], bank(6), ACT.Copy).then_inc(S["lnT_ready"], 1)

                act.wait_ge(S["batch_done"], b + 1)
                evac_lnT()
                for n in range(2):
                    act.wait_ge(S["qkv_psum"], nth("qkv_psum", b, n + 1))
                    act.activation(qk_hi[:, n, :], bank(n), ACT.Copy).then_inc(S["split_hi"], 1)
                act.wait_ge(S["vx_ready"], 1)
                act.wait_ge(S["qkv_psum"], nth("qkv_psum", b, 3))
                act.activation(vx[:].rearrange("p i h d -> p (i h) d")[:, :, 0:HS],
                               bank(2).rearrange("p (n d) -> p n d", d=HS), ACT.Copy).then_inc(S["v_ready"], 1)
                for g in range(NG):
                    c = 2 * (g % 2)
                    act.wait_ge(S["stack_psum"], nth("stack_psum", b, g + 1))
                    act.activation(kstack[:, g, :], bank(c), ACT.Identity, bias=wa("kone"))\
                       .then_inc(S["kstack_ready"], 1)
                    act.activation(qstack[:, g, :], bank(c + 1), ACT.Copy).then_inc(S["qstack_ready"], 1)

                def mstack_evac(g):
                    act.wait_ge(S["m_psum"], nth("m_psum", b, g + 1))
                    act.activation(mstack[:, g % 2, :], bank(6), ACT.Copy).then_inc(S["mstack_ready"], 1)

                mstack_evac(0)
                for g in range(NG):
                    for u in range(NU):
                        r = ring_of("T", g, u)
                        act.wait_ge(S["e_psum"], nth("e_psum", b, g * NU + u + 1))
                        if g >= 2 and u == 0:
                            act.wait_ge(S["av_psum"], nth("av_psum", b, g - 1))
                        act.activation(probs[:, g % 2, u * UNIT:(u + 1) * UNIT].rearrange("p (a n) -> p a n", a=2),
                                       bank(2 * (r % 3), 2), ACT.Exp, scale=float(HS) ** -0.5)\
                           .then_inc(S["exp_done"], 1)
                    act.wait_ge(S["av_psum"], nth("av_psum", b, g + 1))
                    act.activation(av_sb[:], bank(7), ACT.Copy).then_inc(S["av_ready"], 1)
                    if g + 1 < NG:
                        mstack_evac(g + 1)
                evac_lnT()
                act.wait_ge(S["xa_psum"], nth("xa_psum", b, 1))
                act.activation(xa_g[:], ps[0:CTX, 0, :], ACT.Gelu).then_inc(S["xa_gelu"], 1)
                evac_lnT()
                act.wait_ge(S["gate_psum"], nth("gate_psum", b, 1))
                act.activation(junk[:], bank(0), ACT.Relu, bias=wr("gb1"), accum_out=hsum[:])\
                   .then_inc(S["gate_sum"], 1)
                act.wait_ge(S["mb1_done"], nth("mb1_done", b, 1))
                for f in range(FC):
                    act.wait_ge(S["u_psum"], nth("u_psum", b, f + 1))
                    act.activation(hid[:, f, :], bank(f), ACT.Gelu_apprx_tanh, bias=mb1_c[:, f:f + 1])\
                       .then_inc(S["u_ready"], 1)
                evac_lnT()
                act.wait_ge(S["z_psum"], nth("z_psum", b, 2))
                act.activation(gate_g[:], bank(0, 2), ACT.Gelu).then_inc(S["zg_gelu"], 1)
                for c in range(HC):
                    act.wait_ge(S["z_psum"], nth("z_psum", b, 3 + c))
                    act.activation(xc[:, c, :], bank(2 + c), ACT.Identity, bias=wr("convb")[:, c:c + 1],
                                   scale=wr("convw")[:, c * KCONV + 3:c * KCONV + 4]).then_inc(S["conv0"], 1)
                for n in range(4):
                    act.wait_ge(S["gates_psum"], nth("gates_psum", b, n + 1))
                    act.activation(th[:, n, :], bank(4 + n if n < 2 else n - 2), ACT.Tanh, scale=0.5,
                                   bias=hbg[:, n:n + 1]).then_inc(S["gates_tanh"], 1)
                act.wait_ge(S["gates_tanh"], nth("gates_tanh", b, 4))
                for c in range(HC):
                    last = act.activation(alpha[:, c, :], th[:, c, :], ACT.Exp, scale=hdecay[:, c:c + 1],
                                          bias=hdecay[:, c:c + 1])
                last.then_inc(S["alpha_done"], 1)
                act.wait_ge(S["asq_done"], nth("asq_done", b, 1))
                act.activation(beta[:], asq[:], ACT.Sqrt, scale=-1.0, bias=sqrt_bias[:]).then_inc(S["beta_done"], 1)
                evac_lnT()
                act.wait_ge(S["grow_psum"], nth("grow_psum", b, 2))
                act.activation(gate_g[:], bank(0, 2), ACT.Gelu).then_inc(S["mg_gelu"], 1)
                evac_lnT()
                evac_lnT()
                for f in range(FC):
                    act.wait_ge(S["h_psum"], nth("h_psum", b, f + 1))
                    act.activation(hid[:, f, :], bank(f), ACT.Relu, bias=wr("mb1")[:, f:f + 1])\
                       .then_inc(S["h_ready"], 1)

        @block.vector
        def _(dve):
            spare = dve.alloc_register("vector_spare")
            dve.reg_mov(spare, 0)
            dve.wait_ge(S["restw_loaded"], 80)
            dve.wait_ge(S["act_const"], 9)
            n_const = 0

            def const(ins):
                nonlocal n_const
                ins.then_inc(S["dve_const"], 1)
                n_const += 1
                dve.wait_ge(S["dve_const"], n_const)

            e, d2, z, z2, acc = (decay[:, n, :] for n in (1, 2, 3, 4, 5))
            const(dve.tensor_scalar(d2, e, 2.0, None, ALU.add))
            const(dve.reciprocal(d2, d2))
            const(dve.tensor_tensor(z, e, d2, ALU.mult))
            const(dve.tensor_tensor(z2, z, z, ALU.mult))
            const(dve.tensor_scalar(acc, z2, 1.0 / 19, None, ALU.mult))
            for k in range(17, 1, -2):
                const(dve.scalar_tensor_tensor(acc, acc, 1.0 / k, z2, ALU.add, ALU.mult))
            const(dve.scalar_tensor_tensor(acc, acc, 1.0, z, ALU.add, ALU.mult))
            const(dve.tensor_scalar(decay[:, 6, :], wr("fb"), 0.0, -4.0, ALU.max, ALU.mult))
            const(dve.scalar_tensor_tensor(hdecay[:], acc, -8.0, decay[:, 6, :], ALU.mult, ALU.add))
            const(dve.tensor_scalar(hbg[:], wr("bg"), 0.5, None, ALU.mult))
            const(dve.tensor_scalar(wr("winT"), wr("winT"), wr("gamma1"), None, ALU.mult))
            const(dve.tensor_scalar(wr("growT"), wr("growT"), wr("gamma2"), None, ALU.mult))
            for n, (dst, r) in enumerate(((fold_a, P), (wq_T, P), (fold_b, LAT), (fold_c, LAT), (wk_T, P), (wv_T, P))):
                dve.wait_ge(S["fold_psum"], n + 1)
                dve.tensor_copy(dst[:], ps[0:r, n, 0:P]).then_inc(S["fold_copied"], 1)
            dve.wait_ge(S["pool_const"], 6)
            dve.wait_ge(S["fold_copied"], 6)
            dve.tensor_copy(flag[:], ones[:, 0:1]).then_inc(S["batch_done"], 1)

            with dve.Fori(0, B) as b:
                n_dve = 0
                n_ln = n_norm = 0

                def step(ins):
                    nonlocal n_dve
                    ins.then_inc(S["dve"], 1)
                    n_dve += 1

                def steps_done():
                    dve.wait_ge(S["dve"], nth("dve", b, n_dve))

                def variance(src):
                    nonlocal n_ln
                    for i in range(NT):
                        last = dve.bn_stats(stats[:, i, :], src[:, i, :])
                    step(last)
                    dve.reg_mov(spare, nth("dve", b, n_dve))
                    done = dve.snap(spare)
                    dve.wait_ge(S["fold_copied"], 6)
                    dve.wait_ge(S["dve"], done)
                    for i in range(NT):
                        last = dve.bn_aggr(meanvar[:, i, :], stats[:, i, :])
                    last.then_inc(S["ln_var"], 1)
                    n_ln += 1
                    dve.wait_ge(S["ln_rstd"], nth("ln_rstd", b, n_ln))

                def normalise(src, dst=xn, scales=0):
                    nonlocal n_norm
                    for i in range(NT):
                        dve.tensor_scalar(dst[:, i, :], src[:, i, :], meanvar[:, i, 0:1],
                                          rstd[:, scales + i:scales + i + 1], ALU.subtract, ALU.mult)\
                           .then_inc(S["ln_norm"], 1)

                def residual(dst, base, product, src_bank, n):
                    dve.wait_ge(S["res_psum"], nth("res_psum", b, product))
                    dve.tensor_tensor(dst[:], bank(src_bank).rearrange("p (i c) -> p i c", i=NT), base[:], ALU.add)\
                       .then_inc(S["res_done"], 1)
                    dve.wait_ge(S["res_done"], nth("res_done", b, n))

                dve.wait_ge(S["batch_done"], b + 1)
                dve.wait_ge(S["ctx_loaded"], nth("ctx_loaded", b, 32))
                step(dve.tensor_reduce(csum[:], ctxT_sb[:], AX.X, ALU.add))
                steps_done()
                dve.tensor_scalar(csum_b[:], ones[:], csum[:], 1.0 / CTX, ALU.mult, ALU.mult)\
                   .then_inc(S["csum_ready"], 1)
                dve.wait_ge(S["x_loaded"], nth("x_loaded", b, 16))
                variance(xin)
                normalise(xin)
                for n in range(2):
                    dve.wait_ge(S["split_hi"], nth("split_hi", b, n + 1))
                    dve.tensor_tensor(qk_lo[:, n, :], bank(n), qk_hi[:, n, :].bitcast(F32), ALU.subtract)\
                       .then_inc(S["split_lo"], 1)

                def head_keys(g):
                    if g >= 2:
                        dve.wait_ge(S["e_psum"], nth("e_psum", b, (g - 1) * NU))
                    dve.wait_ge(S["kstack_ready"], nth("kstack_ready", b, g + 1))
                    for j in range(HG):
                        dve.tensor_scalar(km[:, (g % 2) * HG + j, :], kstack[:, g, :], wa("headcol")[:, j:j + 1], None,
                                          ALU.mult).then_inc(S["kmask_ready"], 1)

                def maxima(g, u):
                    dve.wait_ge(S["s_psum"], nth("s_psum", b, g * NU + u + 1))
                    s = bank(2 * (ring_of("S", g, u) % 3), 2)
                    neg = negmax[:, g, :, :].rearrange("p i (j r) -> p i j r", j=HG)
                    if u < 2:
                        last = dve.tensor_reduce(neg[:, 3, 2 * u:2 * u + 2, 24], s, AX.X, ALU.max, negate=True)
                    elif u < 4:
                        j = 2 * u - 4
                        dve.tensor_reduce(neg[:, 2, j:j + 2, 24], s[:, :, 0:384], AX.X, ALU.max, negate=True)
                        last = dve.tensor_reduce(neg[:, 0, j:j + 2, 24], s[:, :, 384:512], AX.X, ALU.max, negate=True)
                    else:
                        last = dve.tensor_reduce(neg[:, 1, :, 24], s.rearrange("p a (h n) -> p (a h) n", h=2),
                                                 AX.X, ALU.max, negate=True)
                    last.then_inc(S["max_done"], 1)

                def divide(g):
                    dve.wait_ge(S["avT_psum"], nth("avT_psum", b, g + 1))
                    v = bank(7).rearrange("p (i j r) -> p (i j) r", i=NT, j=HG)
                    step(dve.reciprocal(rden[:], v[:, :, HS]))
                    steps_done()
                    for i in range(NT):
                        last = dve.tensor_tensor(
                            y[:, i, g * HG * HS:(g + 1) * HG * HS].rearrange("p (j d) -> p j d", j=HG),
                            v[:, i * HG:(i + 1) * HG, 0:HS],
                            rden[:, i * HG:(i + 1) * HG].unsqueeze(2).broadcast_to([P, HG, HS]), ALU.mult)
                    last.then_inc(S["av_norm"], 1)

                head_keys(0)
                for g in range(NG):
                    for u in range(NU):
                        maxima(g, u)
                    if g + 1 < NG:
                        head_keys(g + 1)
                    if g >= 1:
                        divide(g - 1)
                divide(NG - 1)
                dve.wait_ge(S["av_norm"], nth("av_norm", b, NG))
                dve.tensor_tensor(x1[:], xin[:], y[:], ALU.add).then_inc(S["res_done"], 1)
                dve.wait_ge(S["res_done"], nth("res_done", b, 1))
                dve.wait_ge(S["p2_psum"], nth("p2_psum", b, 1))
                dve.tensor_copy(p2[:], ps[:, 5, 0:P]).then_inc(S["p2_ready"], 1)
                variance(x1)
                normalise(x1)
                dve.wait_ge(S["xa_gelu"], nth("xa_gelu", b, 1))
                dve.tensor_tensor(xa_p[:], ps[0:CTX, 0, :], xa_g[:], ALU.mult).then_inc(S["xa_prod"], 1)
                residual(x2, x1, 1, 1, 2)
                variance(x2)
                normalise(x2)
                dve.wait_ge(S["gate_sum"], nth("gate_sum", b, 1))
                dve.tensor_scalar(hsum_b[:], ones[:], hsum[:], 1.0 / T, ALU.mult, ALU.mult)\
                   .then_inc(S["gate_bcast"], 1)
                dve.wait_ge(S["g_psum"], nth("g_psum", b, 1))
                dve.tensor_tensor(gvec[:], ps[:, 1, 0:NE], gb2_sb[:], ALU.add)
                dve.tensor_scalar(g9[0:NE, :], ps[0:NE, 2, 0:P], wr("gb2"), None, ALU.add).then_inc(S["g_ready"], 1)
                dve.wait_ge(S["g_ready"], nth("g_ready", b, 1))
                tb1 = wr("Tb1").rearrange("p (f e) -> p f e", f=FC)
                for f in range(FC):
                    last = dve.tensor_tensor(mb1_t[:, f, :], tb1[:, f, :], gvec[:], ALU.mult)
                step(last)
                steps_done()
                step(dve.tensor_reduce(mb1_s[:], mb1_t[:], AX.X, ALU.add))
                steps_done()
                dve.tensor_tensor(mb1_c[:], mb1_s[:], wr("b1"), ALU.add).then_inc(S["mb1_done"], 1)
                for e in range(NE):
                    last = dve.scalar_tensor_tensor(mw1[:], tw1_sb[:, e, :], gvec[:, e:e + 1],
                                                    wr("W1T") if e == 0 else mw1[:], ALU.mult, ALU.add)
                    if e < NE - 1:
                        step(last)
                        steps_done()
                last.then_inc(S["mix1_done"], 1)
                residual(x3, x2, 2, 4, 3)
                variance(x3)
                for i in range(NT):
                    dve.tensor_scalar(y3[:, i, :], x3[:, i, :], meanvar[:, i, 0:1], rstd[:, i:i + 1],
                                      ALU.subtract, ALU.mult)
                normalise(x3, scales=NT)
                for c in range(HC):
                    dve.wait_ge(S["conv0"], nth("conv0", b, c + 1))
                    for k in range(1, KCONV):
                        last = dve.scalar_tensor_tensor(
                            xc[:, c, k:T], ps[:, 2 + c, 0:T - k],
                            wr("convw")[:, c * KCONV + 3 - k:c * KCONV + 4 - k], xc[:, c, k:T], ALU.mult, ALU.add)
                        if k < KCONV - 1 or c < HC - 1:
                            step(last)
                            steps_done()
                last.then_inc(S["conv_done"], 1)
                dve.wait_ge(S["conv_done"], nth("conv_done", b, 1))
                dve.wait_ge(S["gates_tanh"], nth("gates_tanh", b, 4))
                step(dve.scalar_tensor_tensor(rec[:], th[:, 2:4, :], 1.0, xc[:], ALU.add, ALU.mult))
                steps_done()
                dve.wait_ge(S["beta_done"], nth("beta_done", b, 1))
                step(dve.scalar_tensor_tensor(xc[:], rec[:], 0.5, beta[:], ALU.mult, ALU.mult))
                steps_done()
                for c in range(HC):
                    last = dve.tensor_tensor_scan(rec[:, c, :], alpha[:, c, :], xc[:, c, :], 0.0, ALU.mult, ALU.add)
                step(last)
                steps_done()
                dve.wait_ge(S["zg_gelu"], nth("zg_gelu", b, 1))
                dve.tensor_tensor(hm[:], rec[:], gate_g[:], ALU.mult).then_inc(S["hm_done"], 1)
                dve.wait_ge(S["res_psum"], nth("res_psum", b, 3))
                dve.tensor_tensor(hx[:], bank(2).rearrange("p (i c) -> p i c", i=NT), y3[:], ALU.add)\
                   .then_inc(S["hx_done"], 1)
                dve.wait_ge(S["hx_done"], nth("hx_done", b, 1))
                for i in range(NT):
                    last = dve.scalar_tensor_tensor(junk[:, i * P:(i + 1) * P], hx[:, i, :], 1.0, hx[:, i, :],
                                                    ALU.mult, ALU.mult, accum_out=sumsq[:, i:i + 1])
                last.then_inc(S["ln_var"], 1)
                n_ln += 1
                dve.wait_ge(S["ln_rstd"], nth("ln_rstd", b, n_ln))
                for i in range(NT):
                    dve.tensor_scalar(xn[:, i, :], hx[:, i, :], rstd[:, i:i + 1], None, ALU.mult)\
                       .then_inc(S["ln_norm"], 1)
                dve.wait_ge(S["mg_gelu"], nth("mg_gelu", b, 1))
                dve.wait_ge(S["grow_psum"], nth("grow_psum", b, 4))
                dve.tensor_tensor(hm[:], bank(2, 2), gate_g[:], ALU.mult).then_inc(S["mm_done"], 1)
                dve.wait_ge(S["side_done"], nth("side_done", b, 1))
                residual(x4, side, 4, 4, 4)
                variance(x4)
                normalise(x4)
                dve.wait_ge(S["side_done"], nth("side_done", b, 2))
                residual(x5, side2, 5, 0, 5)
                variance(x5)
                normalise(x5)
                dve.wait_ge(S["side_done"], nth("side_done", b, 3))
                residual(x1, side, 6, 4, 6)
                variance(x1)
                for i in range(NT):
                    last = dve.tensor_scalar(x2[:, i, :], x1[:, i, :], meanvar[:, i, 0:1], rstd[:, i:i + 1],
                                             ALU.subtract, ALU.mult)
                step(last)
                steps_done()
                for i in range(NT):
                    last = dve.tensor_tensor(x3[:, i, :], x2[:, i, :], rows[:, P:2 * P], ALU.mult)
                step(last)
                steps_done()
                dve.wait_ge(S["side_done"], nth("side_done", b, 4))
                dve.tensor_tensor(o[:], x3[:], side2[:], ALU.add).then_inc(S["out_ready"], 1)
                dve.wait_ge(S["out_ready"], b + 1)
                dve.wait_ge(S["out_stored"], nth("out_stored", b, 16))
                dve.tensor_copy(flag[:], ones[:, 0:1]).then_inc(S["batch_done"], 1)
                assert n_dve == PER["dve"], n_dve

        @block.tensor
        def _(pe):
            pe.wait_ge(S["attnw_loaded"], 16)

            def fold(n, lhsT, rhs, r, after):
                if after:
                    pe.wait_ge(S["fold_copied"], after)
                pe.matmul(ps[0:r, n, 0:P], lhsT, rhs, start=True, stop=True).then_inc(S["fold_psum"], 1)

            fold(0, wa("wuqT"), wa("wdq"), P, 0)
            fold(1, wa("wdq"), wa("wuqT"), P, 0)
            fold(2, wa("wuk"), fold_a[:], LAT, 1)
            fold(3, wa("wuv"), wa("woT"), LAT, 0)
            fold(4, wa("wdkv"), fold_b[:], P, 3)
            fold(5, wa("wdkv"), fold_c[:], P, 4)
            pe.wait_ge(S["act_const"], 7)

            with pe.Fori(0, B) as b:
                n_ln = 0
                n_norm = 0

                def norm_T():
                    nonlocal n_ln
                    for i in range(NT):
                        pe.wait_ge(S["ln_norm"], nth("ln_norm", b, n_ln * NT + i + 1))
                        last = pe.transpose(bank(6)[:, i * P:(i + 1) * P], xn[:, i, :], wa("ident"))
                    last.then_inc(S["lnT_psum"], 1)
                    n_ln += 1
                    pe.wait_ge(S["lnT_ready"], nth("lnT_ready", b, n_ln))

                def natural(src_bank, terms, n):
                    for i in range(NT):
                        for m, (lhsT, rhs) in enumerate(terms(i)):
                            last = pe.matmul(bank(src_bank)[:, i * P:(i + 1) * P], lhsT, rhs,
                                             start=(m == 0), stop=(m == len(terms(i)) - 1))
                    last.then_inc(S["res_psum"], 1)

                pe.wait_ge(S["batch_done"], b + 1)
                norm_T()
                pe.matmul(bank(0), wq_T[:], xT[:], start=True, stop=True).then_inc(S["qkv_psum"], 1)
                pe.matmul(bank(1), wk_T[:], xT[:], start=True, stop=True).then_inc(S["qkv_psum"], 1)
                for i in range(NT):
                    last = pe.matmul(bank(2)[:, i * P:(i + 1) * P], xT[:, i * P:(i + 1) * P], wv_T[:],
                                     start=True, stop=True)
                last.then_inc(S["qkv_psum"], 1)
                pe.wait_ge(S["split_lo"], nth("split_lo", b, 2))
                pe.wait_ge(S["v_ready"], nth("v_ready", b, 1))

                def q_parts(dst, g, stop):
                    pe.matmul(dst, sel_r[:, 0, g, :], qk_hi[:, 0, :], start=True, stop=False)
                    return pe.matmul(dst, sel_r[:, 1, g, :], qk_lo[:, 0, :], start=False, stop=stop)

                for g in range(NG):
                    c = 2 * (g % 2)
                    if g >= 2:
                        pe.wait_ge(S["qstack_ready"], nth("qstack_ready", b, g - 1))
                    pe.matmul(bank(c), sel_r[:, 2, g, :], qk_hi[:, 1, :], start=True, stop=False)
                    pe.matmul(bank(c), sel_r[:, 3, g, :], qk_lo[:, 1, :], start=False, stop=True)
                    q_parts(bank(c + 1), g, True).then_inc(S["stack_psum"], 1)
                pe.wait_ge(S["qstack_ready"], nth("qstack_ready", b, NG))

                def slot_free(r):
                    if r < 3:
                        return
                    kind, g, u = order[r - 3]
                    name = "max_done" if kind == "S" else "exp_done"
                    pe.wait_ge(S[name], nth(name, b, g * NU + u + 1))

                def s_unit(g, u):
                    r = ring_of("S", g, u)
                    slot_free(r)
                    s = bank(2 * (r % 3), 2).rearrange("p a n -> p (a n)")
                    for j, rank, c, w in segments(u):
                        i = NT - 1 - rank
                        if u in (0, 1, 2):
                            pe.wait_ge(S["kmask_ready"], nth("kmask_ready", b, g * HG + j + 1))
                        pe.matmul(s[:, c:c + w], qstack[:, g, i * P:(i + 1) * P], km[:, (g % 2) * HG + j, 0:w],
                                  start=True, stop=False)
                        last = pe.matmul(s[:, c + w - P:c + w], ident_b[:], mask_b[:], start=False, stop=True)
                    last.then_inc(S["s_psum"], 1)

                def t_unit(g, u):
                    r = ring_of("T", g, u)
                    slot_free(r)
                    if u == 0:
                        pe.wait_ge(S["mstack_ready"], nth("mstack_ready", b, g + 1))
                    s = bank(2 * (r % 3), 2).rearrange("p a n -> p (a n)")
                    for j, i, c, w in segments(u):
                        last = pe.matmul(s[:, c:c + w], km[:, (g % 2) * HG + j, i * P:(i + 1) * P],
                                         mstack[:, g % 2, T - w:T], start=True, stop=True)
                    last.then_inc(S["e_psum"], 1)

                def max_rows(g):
                    pe.wait_ge(S["max_done"], nth("max_done", b, (g + 1) * NU))
                    if g >= 1:
                        pe.wait_ge(S["mstack_ready"], nth("mstack_ready", b, g))
                    q_parts(bank(6), g, False)
                    for i in range(NT):
                        last = pe.matmul(bank(6)[:, i * P:(i + 1) * P], negmax[:, g, i, :], ident_r[:],
                                         start=False, stop=(i == NT - 1))
                    last.then_inc(S["m_psum"], 1)

                def values(g):
                    pe_probs = probs[:, g % 2, :]
                    if g >= 1:
                        pe.wait_ge(S["av_norm"], nth("av_norm", b, g))
                    for i, units in ((0, (0, 1)), (1, (2, 3)), (3, (2, 3)), (2, (4,))):
                        pe.wait_ge(S["sel_done"], nth("sel_done", b, g * NU + units[-1] + 1))
                        for j in range(HG):
                            u, c, w = next((u, c, w) for u in units for jj, r, c, w in segments(u)
                                           if jj == j and r == i)
                            last = pe.matmul(ps[j * VW:(j + 1) * VW, 7, T - w:T], vx[:, i, g * HG + j, :],
                                             pe_probs[:, u * UNIT + c:u * UNIT + c + w],
                                             start=(i == 0), stop=(i == 2),
                                             tile_position=(0, j * VW))
                    last.then_inc(S["av_psum"], 1)

                def tokens_first(g):
                    pe.wait_ge(S["av_ready"], nth("av_ready", b, g + 1))
                    for i in range(NT):
                        last = pe.transpose(bank(7)[:, i * P:(i + 1) * P], av_sb[:, i * P:(i + 1) * P], wa("ident"))
                    last.then_inc(S["avT_psum"], 1)

                for u in range(NU):
                    s_unit(0, u)
                max_rows(0)
                for g in range(1, NG):
                    for u in range(NU):
                        s_unit(g, u)
                        t_unit(g - 1, u)
                    values(g - 1)
                    tokens_first(g - 1)
                    max_rows(g)
                for u in range(NU):
                    t_unit(NG - 1, u)
                values(NG - 1)
                tokens_first(NG - 1)
                pe.wait_ge(S["exp_done"], nth("exp_done", b, NG * NU))
                pe.wait_ge(S["csum_ready"], nth("csum_ready", b, 1))
                pe.matmul(ps[:, 5, 0:P], csum_b[:], wr("x2T"), start=True, stop=False)
                pe.matmul(ps[:, 5, 0:P], ones[0:1, :], wr("xb"), start=False, stop=True).then_inc(S["p2_psum"], 1)
                norm_T()
                pe.matmul(ps[0:CTX, 0, :], ctxT_sb[:], xT[:], start=True, stop=True).then_inc(S["xa_psum"], 1)
                pe.wait_ge(S["xa_prod"], nth("xa_prod", b, 1))
                natural(1, lambda i: [(xa_p[:, i * P:(i + 1) * P], ctxn_sb[:])], 1)
                norm_T()
                pe.matmul(bank(0), wr("gw1T"), xT[:], start=True, stop=True).then_inc(S["gate_psum"], 1)
                pe.wait_ge(S["gate_bcast"], nth("gate_bcast", b, 1))
                pe.matmul(ps[:, 1, 0:NE], hsum_b[:], wr("gw2T"), start=True, stop=True)
                pe.matmul(ps[0:NE, 2, 0:P], wr("gw2T"), hsum_b[:], start=True, stop=True).then_inc(S["g_psum"], 1)
                pe.wait_ge(S["mix1_done"], nth("mix1_done", b, 1))
                for f in range(FC):
                    pe.matmul(bank(f), mw1[:, f * P:(f + 1) * P], xT[:], start=True, stop=True)\
                      .then_inc(S["u_psum"], 1)
                pe.wait_ge(S["mix2_done"], nth("mix2_done", b, 1))
                pe.wait_ge(S["u_ready"], nth("u_ready", b, 4))
                natural(4, lambda i: [(hid[:, f, i * P:(i + 1) * P], mw2[:, f * P:(f + 1) * P]) for f in range(FC)]
                        + [(g9[:], wr("tb2x"))], 2)
                norm_T()
                for n in range(4):
                    pe.matmul(bank(n), wr("winT")[:, n * P:(n + 1) * P], xT[:], start=True, stop=True)\
                      .then_inc(S["z_psum"], 1)
                pe.wait_ge(S["conv_done"], nth("conv_done", b, 1))
                pe.wait_ge(S["zg_gelu"], nth("zg_gelu", b, 1))
                wg = wr("wgT").rearrange("p (c n) -> p c n", c=HC)
                for n in range(4):
                    for c in range(HC):
                        last = pe.matmul(bank(4 + n if n < 2 else n - 2), wg[:, c, n * P:(n + 1) * P], xc[:, c, :],
                                         start=(c == 0), stop=(c == HC - 1))
                    last.then_inc(S["gates_psum"], 1)
                pe.wait_ge(S["hm_done"], nth("hm_done", b, 1))
                natural(2, lambda i: [(hm[:, c, i * P:(i + 1) * P], wr("woutT")[:, c * P:(c + 1) * P])
                                      for c in range(HC)], 3)
                norm_T()
                for n in range(4):
                    pe.matmul(bank(n), wr("growT")[:, n * P:(n + 1) * P], xT[:], start=True, stop=True)\
                      .then_inc(S["grow_psum"], 1)
                pe.wait_ge(S["mm_done"], nth("mm_done", b, 1))
                natural(4, lambda i: [(hm[:, c, i * P:(i + 1) * P], wr("shrinkT")[:, c * P:(c + 1) * P])
                                      for c in range(HC)], 4)
                norm_T()
                natural(0, lambda i: [(xT[:, i * P:(i + 1) * P], wr("x1T"))], 5)
                norm_T()
                pe.wait_ge(S["res_done"], nth("res_done", b, 5))
                for f in range(FC):
                    pe.matmul(bank(f), wr("m1")[:, f * P:(f + 1) * P], xT[:], start=True, stop=True)\
                      .then_inc(S["h_psum"], 1)
                pe.wait_ge(S["h_ready"], nth("h_ready", b, 4))
                natural(4, lambda i: [(hid[:, f, i * P:(i + 1) * P], wr("m2")[:, f * P:(f + 1) * P])
                                      for f in range(FC)], 6)


def kernel(**inputs):
    import numpy as _np
    import concourse.bacc as _bacc
    from concourse.bass_utils import run_bass_kernel_spmd as _run

    a = {k: _np.asarray(v) for k, v in inputs.items()}

    def chunked(w):
        n = w.shape[0] // P
        return w.reshape(n, P, w.shape[1]).transpose(1, 0, 2).reshape(P, -1)

    def per_chunk(v):
        return v.reshape(-1, P).T

    part = {"selqh": (0, 2), "selql": (1,), "selkh": (0, 1), "selkl": (2,)}
    sel = {n: _np.zeros((P, NG, HG, 4, HS), _np.float32) for n in part}
    for n, places in part.items():
        for h in range(NH):
            for d in range(HS):
                for pl in places:
                    sel[n][h * HS + d, h // HG, h % HG, pl, d] = 1.0
    row = _np.arange(P)
    attn = {
        "wdq": a["L0_attn_W_dq"], "wuqT": a["L0_attn_W_uq"].T, "wdkv": a["L0_attn_W_dkv"],
        "wuk": a["L0_attn_W_uk"], "wuv": a["L0_attn_W_uv"], "woT": a["L0_attn_W_o"].T,
        "ident": _np.eye(P, dtype=_np.float32),
        "mask": _np.where(row[None, :] > row[:, None], NEG, 0.0).astype(_np.float32),
        "kone": (row % 32 == 24).astype(_np.float32)[:, None],
        "headcol": (row[:, None] // 32 == _np.arange(HG)[None, :]).astype(_np.float32),
    }
    rest = {
        "gw1T": a["L0_ffn_gate_w1"].T, "gb1": a["L0_ffn_gate_b1"][:, None], "gw2T": a["L0_ffn_gate_w2"].T,
        "gb2": a["L0_ffn_gate_b2"][:, None], "W1T": a["L0_ffn_W1"].T, "b1": per_chunk(a["L0_ffn_b1"]),
        "W2T": chunked(a["L0_ffn_W2"].T),
        "tb2x": _np.concatenate([a["L0_ffn_Tb2"], a["L0_ffn_b2"][None]], 0),
        "Tb1": a["L0_ffn_Tb1"].reshape(NE, FC, P).transpose(2, 1, 0).reshape(P, -1),
        "winT": a["L1_attn_W_in"].T, "gamma1": a["L1_attn_gamma1"][:, None],
        "convw": a["L1_attn_conv_w"].reshape(HC, P, KCONV).transpose(1, 0, 2).reshape(P, -1),
        "convb": per_chunk(a["L1_attn_conv_b"]), "wgT": chunked(a["L1_attn_W_gates"].T),
        "bg": per_chunk(a["L1_attn_b_gates"]), "fb": per_chunk(a["L1_attn_forget_base"]),
        "woutT": chunked(a["L1_attn_W_out"].T), "gamma2": a["L1_attn_gamma2"][:, None],
        "growT": a["L1_attn_W_grow"].T, "shrinkT": chunked(a["L1_attn_W_shrink"].T),
        "x1T": a["L1_xattn_W"][:, :P].T, "x2T": a["L1_xattn_W"][:, P:].T, "xb": a["L1_xattn_b"][None],
        "m1": a["L1_ffn_w1"][0], "mb1": per_chunk(a["L1_ffn_b1"][0]), "m2": chunked(a["L1_ffn_w2"][0]),
    }

    def packed(parts, at, width, values):
        m = _np.zeros((P, width), _np.float32)
        for name, r, w in parts:
            c = at[name][0]
            assert values[name].shape == (r, w), (name, values[name].shape)
            m[0:r, c:c + w] = values[name]
        return m

    arrays = {
        "x": a["x"], "ctxn": a["ctx_1024"], "ctxT": _np.ascontiguousarray(a["ctx_1024"].transpose(0, 2, 1)),
        "attnw": packed(ATTN_PARTS, ATTN_AT, ATTN_W, attn),
        "selw": _np.concatenate([sel[n].reshape(P, -1) for n in SELECTIONS], 1),
        "restw": packed(REST_PARTS, REST_AT, REST_W, rest),
        "rowsw": _np.concatenate([a["L1_ffn_b2"][0], a["L1_ffn_gamma"], a["L1_ffn_beta"]])[None],
        "tw1": _np.ascontiguousarray(a["L0_ffn_TW1"].transpose(2, 0, 1)),
        "tw2": _np.ascontiguousarray(a["L0_ffn_TW2"].reshape(NE, P, FC, P).transpose(3, 0, 2, 1).reshape(P, NE, -1)),
        "gb2row": a["L0_ffn_gate_b2"][None],
    }
    nc = _bacc.Bacc("TRN2", target_bir_lowering=False, num_devices=1)
    args, sent = [], {}
    for name, v in arrays.items():
        v = _np.ascontiguousarray(v)
        sent["in_" + name] = v
        args.append(nc.dram_tensor("in_" + name, v.shape, mybir.dt.from_np(v.dtype), kind="ExternalInput").ap())
    args.append(nc.dram_tensor("out_0", (B, T, P), F32, kind="ExternalOutput").ap())
    decoder_kernel(nc, *args)
    r = _run(nc, [sent], core_ids=[0])
    return r.results[0]["out_0"]
```

```python
import numpy as np
from contextlib import ExitStack

import concourse.bass as bass
from concourse import mybir

P = 128
B = 4
T = 512
NT = T // P
NH = 16
HS = P // NH
NG = 4
HG = NH // NG
LAT = 32
VW = 32
CTX = 77
NE = 8
FC = 4
HC = 2
KCONV = 4
GW = HG * (T + 384 + 256 + 128)
UNIT = 1024
NU = GW // UNIT
EPS = 1e-5
NEG = -1e30

F32 = mybir.dt.float32
F32R = mybir.dt.float32r
BF16 = mybir.dt.bfloat16
ALU = mybir.AluOpType
ACT = mybir.ActivationFunctionType
AX = mybir.AxisListType

ATTN_PARTS = [("wdq", LAT, P), ("wuqT", LAT, P), ("wdkv", LAT, P), ("wuk", P, LAT), ("wuv", P, LAT),
              ("woT", P, P), ("ident", P, P), ("mask", P, P), ("kone", P, 1), ("headcol", P, HG)]
SELECTIONS = ("selqh", "selql", "selkh", "selkl")
REST_PARTS = [("gw1T", P, P), ("gb1", P, 1), ("gw2T", P, NE), ("gb2", NE, 1), ("W1T", P, FC * P),
              ("b1", P, FC), ("W2T", P, FC * P), ("tb2x", NE + 1, P), ("Tb1", P, FC * NE),
              ("winT", P, 4 * P), ("gamma1", P, 1), ("convw", P, HC * KCONV), ("convb", P, HC),
              ("wgT", P, HC * 4 * P), ("bg", P, 4), ("fb", P, HC), ("woutT", P, HC * P),
              ("gamma2", P, 1), ("growT", P, 4 * P), ("shrinkT", P, HC * P),
              ("x1T", P, P), ("x2T", P, P), ("xb", 1, P),
              ("m1", P, FC * P), ("mb1", P, FC), ("m2", P, FC * P)]


def columns(parts):
    at, out = 0, {}
    for name, rows, width in parts:
        out[name] = (at, rows, width)
        at += width
    return out, at


ATTN_AT, ATTN_W = columns(ATTN_PARTS)
REST_AT, REST_W = columns(REST_PARTS)

def segments(unit):
    width = [512, 384, 256, 128]
    if unit < 2:
        return [(j, 0, 512 * (j % 2), width[0]) for j in (2 * unit, 2 * unit + 1)]
    if unit < 4:
        return [(j, r, 512 * (j % 2) + c, width[r])
                for j in (2 * unit - 4, 2 * unit - 3) for r, c in ((1, 0), (3, 384))]
    return [(j, 2, 256 * j, width[2]) for j in range(HG)]


def slot(kind, g, u):
    return (g * 2 * NU + 2 * u + (kind == "keys")) % 3


def decoder_kernel(nc, x, ctxn, ctxT, attnw, selw, restw, rowsw, tw1, tw2, gb2row, out):
    es = ExitStack()
    with es:
        def sb(name, shape, dt=F32, stack=es):
            return stack.enter_context(nc.sbuf_tensor(name, shape, dt))

        aw = sb("aw", [P, ATTN_W])
        rw = sb("rw", [P, REST_W])
        rows = sb("rows", [P, 3 * P])
        tw1_sb = sb("tw1_sb", [P, NE, FC * P])
        tw2_sb = sb("tw2_sb", [P, NE, FC * P])
        gb2_sb = sb("gb2_sb", [P, NE])

        def wa(name):
            c, r, w = ATTN_AT[name]
            return aw[0:r, c:c + w]

        def wr(name):
            c, r, w = REST_AT[name]
            return rw[0:r, c:c + w]

        ones = sb("ones", [P, P])
        halfpow = sb("halfpow", [P, 2 * NT])
        decay = sb("decay", [P, 7, HC])
        ndecay = sb("ndecay", [P, HC])
        sqrt_bias = sb("sqrt_bias", [P, 1])
        flag = sb("flag", [P, 1])

        xs = sb("xs", [P, B, NT, P])
        y = sb("y", [P, B, NT, P])
        ctxn_sb = sb("ctxn_sb", [CTX, B, P])
        ctxT_sb = sb("ctxT_sb", [P, B, CTX])

        att = ExitStack()
        ident_r = sb("ident_r", [P, P], F32R, att)
        ident_b = sb("ident_b", [P, P], BF16, att)
        mask_b = sb("mask_b", [P, P], BF16, att)
        sel_r = sb("sel_r", [P, 4, NG, P], F32R, att)
        wq_T = sb("wq_T", [P, P], F32, att)
        wk_T = sb("wk_T", [P, P], F32, att)
        wv_T = sb("wv_T", [P, P], F32, att)
        a_stats = sb("a_stats", [P, NT, 6], F32, att)
        a_meanvar = sb("a_meanvar", [P, NT, 2], F32, att)
        a_vareps = sb("a_vareps", [P, NT], F32, att)
        a_rstd = sb("a_rstd", [P, NT], F32, att)
        a_xn = sb("a_xn", [P, NT, P], F32, att)
        a_xT = sb("a_xT", [P, T], F32, att)
        qk_hi = sb("qk_hi", [P, B, 2, T], F32R, att)
        qk_lo = sb("qk_lo", [P, B, 2, T], F32R, att)
        v_all = sb("v_all", [P, T], F32, att)
        vx = sb("vx", [P, NT, NH, VW], F32, att)
        kstack = sb("kstack", [P, T], F32, att)
        qstack = sb("qstack", [P, 2, T], F32R, att)
        mstack = sb("mstack", [P, 2, T], F32R, att)
        km = sb("km", [P, 2 * HG, T], F32R, att)
        negmax = sb("negmax", [P, 2, NT, P], F32R, att)
        probs = sb("probs", [P, 2, GW], F32, att)
        av_sb = sb("av_sb", [P, T], F32, att)
        fold_a = av_sb[:, 0:P]
        fold_b = av_sb[0:LAT, P:2 * P]
        fold_c = av_sb[0:LAT, 2 * P:3 * P]
        rden = sb("rden", [P, NT * HG], F32, att)
        att.close()

        stats = sb("stats", [P, B, NT, 6])
        meanvar = sb("meanvar", [P, B, NT, 2])
        vareps = sb("vareps", [P, B, 2 * NT])
        rstd = sb("rstd", [P, B, 2 * NT])
        xn = sb("xn", [P, B, NT, P])
        xT = sb("xT", [P, B, T])
        side = sb("side", [P, B, NT, P])
        hsum = sb("hsum", [P, B])
        hsum_b = sb("hsum_b", [P, B, P])
        gvec = sb("gvec", [P, B, NE])
        g9 = sb("g9", [NE + 1, B, P])
        mw1 = sb("mw1", [P, 2, FC * P])
        mw2 = sb("mw2", [P, 2, FC * P])
        mb1_t = sb("mb1_t", [P, B, FC, NE])
        mb1_s = sb("mb1_s", [P, B, FC])
        mb1_c = sb("mb1_c", [P, B, FC])
        hid = sb("hid", [P, 2, FC, T])
        gate_g = sb("gate_g", [P, 2, HC, T])
        xc = sb("xc", [P, 2, HC, T])
        alpha = sb("alpha", [P, 2, HC, T])
        beta = sb("beta", [P, 2, HC, T])
        rec = sb("rec", [P, 2, HC, T])
        sumsq = sb("sumsq", [P, B, NT])
        csum = sb("csum", [P, B])
        csum_b = sb("csum_b", [P, B, P])
        p2 = sb("p2", [P, B, P])
        sq = sb("sq", [P, P])

        ps = es.enter_context(nc.psum_tensor("ps", [P, 8, 512], F32))

        def bank(i, n=1):
            return ps[:, i, :] if n == 1 else ps[:, i:i + n, :]

        names = """x_loaded xs_loaded attnw_loaded selw_loaded restw_loaded ctx_loaded fold_psum fold_copied
            act_const pool_const dve_const pool_step dve_step
            a_ln_var a_ln_rstd a_ln_norm a_lnT_psum a_lnT_ready a_stats_done a_eps_done
            q_psum k_psum v_psum q_hi k_hi q_lo k_lo v_ready vx_ready
            kstack_psum qstack_psum kstack_ready qstack_ready kmask_ready
            s_psum max_done e_psum exp_done sel_done m_psum mstack_ready
            av_psum av_ready avT_psum av_den av_norm
            ln_var ln_rstd ln_norm lnT_psum lnT_ready eps_done
            xa_psum xa_gelu xa_prod gate_psum gate_sum gate_bcast g_psum g_ready mix1_done mix2_done
            mixed_terms mix2_half mb1_done u_psum u_ready z_psum zg_gelu conv0 conv_done gates_psum gates_sig
            alpha_done beta_done sx_done xs_done hm_done hx_done hx_side grow_psum mg_gelu mm_done
            h_psum h_ready p2_psum p2_ready csum_ready res_psum res_done p2_side b2_side beta_side
            gain_done out_ready out_stored""".split()
        S = {n: es.enter_context(nc.semaphore(n)) for n in names}

        block = es.enter_context(nc.Block())

        x_v = x.rearrange("b (i p) c -> b p i c", p=P)
        out_v = out.rearrange("b (i p) c -> b p i c", p=P)

        XA, FFN, REC, RMS, XA2, EXPERT, LAST = range(7)

        @block.sync
        def _(sp):
            sp.dma_start(xs[:, 0], x_v[0]).then_inc(S["x_loaded"], 16)
            sp.dma_start(aw[:], attnw).then_inc(S["attnw_loaded"], 16)
            sp.dma_start(probs[:, 0, 0:4 * NG * P], selw).then_inc(S["selw_loaded"], 16)
            for b in range(1, B):
                sp.dma_start(xs[:, b], x_v[b]).then_inc(S["xs_loaded"], 16)
            sp.dma_start(rw[:], restw).then_inc(S["restw_loaded"], 16)
            sp.dma_start(ctxT_sb[:], ctxT).then_inc(S["ctx_loaded"], 16)
            sp.dma_start(ctxn_sb[:], ctxn).then_inc(S["ctx_loaded"], 16)
            sp.dma_start(gb2_sb[:], gb2row.broadcast_to([P, NE])).then_inc(S["restw_loaded"], 16)
            sp.dma_start(rows[:], rowsw.broadcast_to([P, 3 * P])).then_inc(S["restw_loaded"], 16)
            sp.dma_start(tw1_sb[:], tw1).then_inc(S["restw_loaded"], 16)
            sp.dma_start(tw2_sb[:], tw2).then_inc(S["restw_loaded"], 16)
            for b in range(B):
                sp.wait_ge(S["out_ready"], b + 1)
                sp.dma_start(out_v[b], xn[:, b]).then_inc(S["out_stored"], 16)
            sp.wait_ge(S["out_stored"], 16 * B)

        @block.gpsimd
        def _(pool):
            spare = pool.alloc_register("pool_spare")

            def wait_apart(sem, value):
                if isinstance(value, int):
                    pool.wait_ge(sem, value)
                    return
                pool.reg_mov(spare, value)
                value = pool.snap(spare)
                pool.wait_ge(S["pool_const"], 6)
                pool.wait_ge(sem, value)

            pool.memset(halfpow[:], -0.5).then_inc(S["pool_const"], 1)
            pool.memset(ones[:], 1.0).then_inc(S["pool_const"], 1)
            pool.memset(vx[:], 0.0).then_inc(S["pool_const"], 1)
            pool.memset(negmax[:].bitcast(F32), 0.0).then_inc(S["pool_const"], 1)
            pool.memset(sqrt_bias[:], 1.0 + 1e-6).then_inc(S["pool_const"], 1)
            pool.wait_ge(S["pool_const"], 5)
            pool.memset(vx[:, :, :, HS:HS + 1], 1.0).then_inc(S["pool_const"], 1)
            pool.wait_ge(S["pool_const"], 6)

            def attention_rstd(b):
                wait_apart(S["a_ln_var"], b + 1)
                pool.tensor_scalar(a_vareps[:], a_meanvar[:, :, 1], 1.0, EPS, ALU.mult, ALU.add)\
                    .then_inc(S["a_eps_done"], 1)
                pool.wait_ge(S["a_eps_done"], b + 1)
                pool.tensor_tensor(a_rstd[:], a_vareps[:], halfpow[:, 0:NT], ALU.pow).then_inc(S["a_ln_rstd"], 1)

            def value_operand(b):
                wait_apart(S["v_ready"], b + 1)
                pool.tensor_copy(vx[:].rearrange("p i h d -> p (i h) d")[:, :, 0:HS],
                                 v_all[:].rearrange("p (n d) -> p n d", d=HS)).then_inc(S["vx_ready"], 1)

            def causal(G, g, u):
                wait_apart(S["exp_done"], G * NU + u + 1)
                seg = probs[:, g % 2, u * UNIT:(u + 1) * UNIT]
                n = 4 if u == 4 else 2
                v = seg.rearrange("p (j t) -> p j t", j=n)
                if u in (2, 3):
                    pool.affine_select(out=v[:, :, 384:512], in_=v[:, :, 384:512], pattern=[[0, 2], [1, P]],
                                       compare_op=ALU.is_ge, fill=0.0, base=0, channel_multiplier=-1)
                pool.affine_select(out=v[:, :, 0:P], in_=v[:, :, 0:P], pattern=[[0, n], [1, P]],
                                   compare_op=ALU.is_ge, fill=0.0, base=0, channel_multiplier=-1)\
                    .then_inc(S["sel_done"], 1)

            def batch(b, last):
                for g in range(NG):
                    for u in range(NU):
                        causal(b * NG + g, g, u)
                        if g == 0 and u == 0 and not last:
                            attention_rstd(b + 1)
                if not last:
                    pool.wait_ge(S["av_psum"], (b + 1) * NG)
                    value_operand(b + 1)

            attention_rstd(0)
            value_operand(0)
            with pool.Fori(0, B - 1) as b:
                batch(b, False)
            batch(B - 1, True)

            pool.wait_ge(S["avT_psum"], B * NG)
            pool.memset(g9[:], 1.0).then_inc(S["pool_const"], 1)
            n_eps = 0

            def norm_rstd(k, b, both=False):
                nonlocal n_eps
                pool.wait_ge(S["ln_var"], k * B + b + 1)
                n = NT
                if k == RMS:
                    last = pool.tensor_scalar(vareps[:, b, 0:NT], sumsq[:, b, :], 1.0 / P, 0.0, ALU.mult, ALU.add)
                else:
                    last = pool.tensor_scalar(vareps[:, b, 0:NT], meanvar[:, b, :, 1], 1.0, EPS, ALU.mult, ALU.add)
                if both:
                    n = 2 * NT
                    last = pool.tensor_scalar(vareps[:, b, NT:n], meanvar[:, b, :, 1], 1.0, 0.0, ALU.mult, ALU.add)
                last.then_inc(S["eps_done"], 1)
                n_eps += 1
                pool.wait_ge(S["eps_done"], n_eps)
                pool.tensor_tensor(rstd[:, b, 0:n], vareps[:, b, 0:n], halfpow[:, 0:n], ALU.pow)\
                    .then_inc(S["ln_rstd"], 1)

            def hx_side_sum(b):
                pool.wait_ge(S["hx_done"], b + 1)
                pool.tensor_tensor(side[:, b], xs[:, b], y[:, b], ALU.add).then_inc(S["hx_side"], 1)

            for b in range(B):
                norm_rstd(XA, b)
            for b in range(B):
                norm_rstd(FFN, b)
            n_step = 0
            for b in range(B):
                if b >= 2:
                    pool.wait_ge(S["res_psum"], B + b - 1)
                for e in range(NE // 2):
                    pool.wait_ge(S["mixed_terms"], b * (NE // 2) + e + 1)
                    if e:
                        pool.wait_ge(S["pool_step"], n_step)
                    last = pool.tensor_tensor(mw2[:, b % 2], wr("W2T") if e == 0 else mw2[:, b % 2],
                                              hid[:, b % 2, e, :], ALU.add)
                    if e < NE // 2 - 1:
                        last.then_inc(S["pool_step"], 1)
                        n_step += 1
                last.then_inc(S["mix2_half"], 1)
            for b in range(B):
                norm_rstd(REC, b, both=True)
            for b in range(B):
                pool.wait_ge(S["gates_sig"], 4 * b + 4)
                pool.wait_ge(S["conv_done"], b + 1)
                pool.tensor_tensor(rec[:, b % 2], hid[:, b % 2, 2:4, :], xc[:, b % 2], ALU.mult)\
                    .then_inc(S["sx_done"], 1)
                if b >= 2:
                    hx_side_sum(b - 2)
                    norm_rstd(RMS, b - 2)
            for b in range(2, B):
                hx_side_sum(b)
                norm_rstd(RMS, b)
            for b in range(B):
                pool.wait_ge(S["res_done"], 3 * B + b + 1)
                norm_rstd(XA2, b)
                if b == 0:
                    pool.wait_ge(S["p2_ready"], 1)
                for i in range(NT):
                    last = pool.tensor_tensor(side[:, b, i, :], xs[:, b, i, :], p2[:, b, :], ALU.add)
                last.then_inc(S["p2_side"], 1)
            for b in range(B):
                norm_rstd(EXPERT, b)
                pool.wait_ge(S["ln_norm"], NT * (EXPERT * B + b + 1))
                for i in range(NT):
                    last = pool.tensor_tensor(y[:, b, i, :], xn[:, b, i, :], rows[:, 0:P], ALU.add)
                last.then_inc(S["b2_side"], 1)
                for i in range(NT):
                    last = pool.tensor_tensor(side[:, b, i, :], xs[:, b, i, :], rows[:, 2 * P:3 * P], ALU.add)
                last.then_inc(S["beta_side"], 1)
            for b in range(B):
                norm_rstd(LAST, b)

        @block.scalar
        def _(act):
            act.wait_ge(S["attnw_loaded"], 16)
            act.activation(ident_b[:], wa("ident"), ACT.Copy).then_inc(S["act_const"], 1)
            act.activation(mask_b[:], wa("mask"), ACT.Copy).then_inc(S["act_const"], 1)
            act.activation(ident_r[:], wa("ident"), ACT.Copy).then_inc(S["act_const"], 1)
            act.wait_ge(S["selw_loaded"], 16)
            for n in range(4):
                act.activation(sel_r[:, n, :, :],
                               probs[:, 0, n * NG * P:(n + 1) * NG * P].rearrange("p (g c) -> p g c", g=NG),
                               ACT.Copy).then_inc(S["act_const"], 1)

            def norm_piece(b, src):
                act.wait_ge(S["a_lnT_psum"], b + 1)
                act.activation(a_xT[:], bank(src), ACT.Copy).then_inc(S["a_lnT_ready"], 1)

            def q_piece(b, src):
                act.wait_ge(S["q_psum"], b + 1)
                act.activation(qk_hi[:, b, 0, :], bank(src), ACT.Copy).then_inc(S["q_hi"], 1)

            def k_piece(b, src):
                act.wait_ge(S["k_psum"], b + 1)
                act.activation(qk_hi[:, b, 1, :], bank(src), ACT.Copy).then_inc(S["k_hi"], 1)

            def v_piece(b, src):
                act.wait_ge(S["v_psum"], b + 1)
                act.activation(v_all[:], bank(src), ACT.Copy).then_inc(S["v_ready"], 1)

            def k_stack(G, g, src):
                act.wait_ge(S["kstack_psum"], G + 1)
                if not (isinstance(G, int) and G == 0):
                    act.wait_ge(S["kmask_ready"], G * HG)
                act.activation(kstack[:], bank(src), ACT.Identity, bias=wa("kone"))\
                   .then_inc(S["kstack_ready"], 1)

            def q_stack(G, g, src):
                act.wait_ge(S["qstack_psum"], G + 1)
                act.activation(qstack[:, g % 2, :], bank(src), ACT.Copy).then_inc(S["qstack_ready"], 1)

            def m_stack(G, g):
                act.wait_ge(S["m_psum"], G + 1)
                act.activation(mstack[:, g % 2, :], bank(6), ACT.Copy).then_inc(S["mstack_ready"], 1)

            norm_piece(0, 6)
            q_piece(0, 0)
            k_piece(0, 1)
            v_piece(0, 2)
            k_stack(0, 0, 3)
            q_stack(0, 0, 4)
            k_stack(1, 1, 5)
            q_stack(1, 1, 7)
            m_stack(0, 0)

            def batch(b, last):
                for g in range(NG):
                    G = b * NG + g
                    for u in range(NU):
                        act.wait_ge(S["e_psum"], G * NU + u + 1)
                        act.activation(probs[:, g % 2, u * UNIT:(u + 1) * UNIT].rearrange("p (a n) -> p a n", a=2),
                                       bank(2 * slot("keys", g, u), 2), ACT.Exp, scale=float(HS) ** -0.5)\
                           .then_inc(S["exp_done"], 1)
                        if not (last and g >= NG - 2):
                            if u == 0:
                                k_stack(G + 2, g, 6)
                            if u == 1:
                                q_stack(G + 2, g, 6)
                        if not last:
                            if (g, u) == (0, 3):
                                norm_piece(b + 1, 6)
                            if (g, u) == (1, 2):
                                q_piece(b + 1, 6)
                            if (g, u) == (1, 3):
                                k_piece(b + 1, 6)
                            if (g, u) == (2, 2):
                                v_piece(b + 1, 6)
                    act.wait_ge(S["av_psum"], G + 1)
                    act.activation(av_sb[:], bank(7), ACT.Copy).then_inc(S["av_ready"], 1)
                    if not (last and g == NG - 1):
                        m_stack(G + 1, g + 1)

            with act.Fori(0, B - 1) as b:
                batch(b, False)
            batch(B - 1, True)

            def norm_T(k, b):
                act.wait_ge(S["lnT_psum"], k * B + b + 1)
                act.activation(xT[:, b, :], bank(4 + b), ACT.Copy).then_inc(S["lnT_ready"], 1)

            act.wait_ge(S["restw_loaded"], 80)
            act.activation(decay[:, 0, :], wr("fb"), ACT.Abs).then_inc(S["act_const"], 1)
            act.wait_ge(S["act_const"], 8)
            act.activation(decay[:, 1, :], decay[:, 0, :], ACT.Exp, scale=-1.0).then_inc(S["act_const"], 1)
            for b in range(B):
                norm_T(XA, b)
            for b in range(B):
                act.wait_ge(S["xa_psum"], b + 1)
                act.activation(gate_g[0:CTX, b % 2, b // 2, :], ps[0:CTX, b, :], ACT.Gelu)\
                   .then_inc(S["xa_gelu"], 1)
            for b in range(B):
                norm_T(FFN, b)
            for b in range(B):
                act.wait_ge(S["gate_psum"], b + 1)
                act.activation(rec[:, b // 2, b % 2, :], bank(b), ACT.Relu, bias=wr("gb1"), accum_out=hsum[:, b:b + 1])\
                   .then_inc(S["gate_sum"], 1)

            def mixed_terms(b):
                act.wait_ge(S["g_ready"], b + 1)
                if b >= 2:
                    act.wait_ge(S["res_psum"], B + b - 1)
                for e in range(NE // 2):
                    act.activation(hid[:, b % 2, e, :], tw2_sb[:, e, :], ACT.Copy, scale=gvec[:, b, e:e + 1])\
                       .then_inc(S["mixed_terms"], 1)

            def hidden(b):
                act.wait_ge(S["mb1_done"], b + 1)
                act.wait_ge(S["mix2_half"], b + 1)
                for f in range(FC):
                    act.wait_ge(S["u_psum"], b * FC + f + 1)
                    act.activation(hid[:, b % 2, f, :], bank(f), ACT.Gelu_apprx_tanh, bias=mb1_c[:, b, f:f + 1])\
                       .then_inc(S["u_ready"], 1)

            mixed_terms(0)
            mixed_terms(1)
            hidden(0)
            for b in range(1, B):
                if b + 1 < B:
                    mixed_terms(b + 1)
                hidden(b)
            for b in range(B):
                norm_T(REC, b)

            def gelu_conv(b):
                if b >= 2:
                    act.wait_ge(S["res_psum"], 2 * B + b - 1)
                act.wait_ge(S["z_psum"], 4 * b + 2)
                act.activation(gate_g[:, b % 2], bank(0, 2), ACT.Gelu).then_inc(S["zg_gelu"], 1)
                for c in range(HC):
                    act.wait_ge(S["z_psum"], 4 * b + 3 + c)
                    act.activation(xc[:, b % 2, c, :], bank(2 + c), ACT.Identity, bias=wr("convb")[:, c:c + 1],
                                   scale=wr("convw")[:, c * KCONV + 3:c * KCONV + 4]).then_inc(S["conv0"], 1)

            def gates(b):
                for n in range(4):
                    act.wait_ge(S["gates_psum"], 4 * b + n + 1)
                    act.activation(hid[:, b % 2, n, :], bank(4 + (4 * b + n) % 3), ACT.Sigmoid,
                                   bias=wr("bg")[:, n:n + 1]).then_inc(S["gates_sig"], 1)

            def decays(b):
                act.wait_ge(S["gates_sig"], 4 * b + 4)
                for c in range(HC):
                    last = act.activation(alpha[:, b % 2, c, :], hid[:, b % 2, c, :], ACT.Exp,
                                          scale=ndecay[:, c:c + 1])
                last.then_inc(S["alpha_done"], 1)
                act.wait_ge(S["alpha_done"], b + 1)
                act.activation(beta[:, b % 2], alpha[:, b % 2], ACT.Square).then_inc(S["act_const"], 1)

            def input_scale(b):
                act.wait_ge(S["act_const"], 10 + b)
                act.activation(beta[:, b % 2], beta[:, b % 2], ACT.Sqrt, scale=-1.0, bias=sqrt_bias[:])\
                   .then_inc(S["beta_done"], 1)

            act.wait_ge(S["dve_const"], REC_CONST)
            gelu_conv(0)
            gelu_conv(1)
            gates(0)
            decays(0)
            input_scale(0)
            for b in range(1, B):
                if b + 1 < B:
                    gelu_conv(b + 1)
                gates(b)
                decays(b)
                input_scale(b)
            for b in range(B):
                norm_T(RMS, b)
            for b in range(B):
                act.wait_ge(S["grow_psum"], 4 * b + 2)
                if b >= 2:
                    act.wait_ge(S["mm_done"], b - 1)
                act.activation(gate_g[:, b % 2], bank(0, 2), ACT.Gelu).then_inc(S["mg_gelu"], 1)
            for b in range(B):
                norm_T(XA2, b)
            for b in range(B):
                norm_T(EXPERT, b)
            for b in range(B):
                for f in range(FC):
                    act.wait_ge(S["h_psum"], b * FC + f + 1)
                    if b >= 2 and f == 0:
                        act.wait_ge(S["res_psum"], 5 * B + b - 1)
                    act.activation(hid[:, b % 2, f, :], bank(f), ACT.Relu, bias=wr("mb1")[:, f:f + 1])\
                       .then_inc(S["h_ready"], 1)

        @block.vector
        def _(dve):
            spare = dve.alloc_register("vector_spare")

            def attention_stats(b):
                for i in range(NT):
                    last = dve.bn_stats(a_stats[:, i, :], xs[:, b, i, :])
                last.then_inc(S["a_stats_done"], 1)
                if isinstance(b, int):
                    dve.wait_ge(S["a_stats_done"], b + 1)
                else:
                    dve.reg_mov(spare, b + 1)
                    done = dve.snap(spare)
                    dve.wait_ge(S["fold_copied"], 6)
                    dve.wait_ge(S["a_stats_done"], done)
                for i in range(NT):
                    last = dve.bn_aggr(a_meanvar[:, i, :], a_stats[:, i, :])
                last.then_inc(S["a_ln_var"], 1)

            def attention_norm(b):
                dve.wait_ge(S["a_ln_rstd"], b + 1)
                if not isinstance(b, int):
                    dve.wait_ge(S["a_lnT_psum"], b)
                for i in range(NT):
                    dve.tensor_scalar(a_xn[:, i, :], xs[:, b, i, :], a_meanvar[:, i, 0:1], a_rstd[:, i:i + 1],
                                      ALU.subtract, ALU.mult).then_inc(S["a_ln_norm"], 1)

            def low_part(b, n, src):
                dve.wait_ge(S["qk"[n] + "_hi"], b + 1)
                dve.tensor_tensor(qk_lo[:, b, n, :], bank(src), qk_hi[:, b, n, :].bitcast(F32), ALU.subtract)\
                   .then_inc(S["qk"[n] + "_lo"], 1)

            def head_keys(G, g):
                dve.wait_ge(S["kstack_ready"], G + 1)
                if not (isinstance(G, int) and G < 2):
                    dve.wait_ge(S["e_psum"], (G - 1) * NU)
                for j in range(HG):
                    dve.tensor_scalar(km[:, (g % 2) * HG + j, :], kstack[:], wa("headcol")[:, j:j + 1],
                                      None, ALU.mult).then_inc(S["kmask_ready"], 1)

            def maxima(G, g, u, at):
                dve.wait_ge(S["s_psum"], G * NU + u + 1)
                s = bank(2 * at, 2)
                neg = negmax[:, g % 2, :, :].rearrange("p i (j r) -> p i j r", j=HG)
                if u < 2:
                    last = dve.tensor_reduce(neg[:, 3, 2 * u:2 * u + 2, 24], s, AX.X, ALU.max, negate=True)
                elif u < 4:
                    j = 2 * u - 4
                    dve.tensor_reduce(neg[:, 2, j:j + 2, 24], s[:, :, 0:384], AX.X, ALU.max, negate=True)
                    last = dve.tensor_reduce(neg[:, 0, j:j + 2, 24], s[:, :, 384:512], AX.X, ALU.max, negate=True)
                else:
                    last = dve.tensor_reduce(neg[:, 1, :, 24], s.rearrange("p a (h n) -> p (a h) n", h=2),
                                             AX.X, ALU.max, negate=True)
                last.then_inc(S["max_done"], 1)

            def divide(b, g):
                dve.wait_ge(S["avT_psum"], b * NG + g + 1)
                v = bank(7).rearrange("p (i j r) -> p (i j) r", i=NT, j=HG)
                dve.reciprocal(rden[:], v[:, :, HS]).then_inc(S["av_den"], 1)
                dve.wait_ge(S["av_den"], b * NG + g + 1)
                for i in range(NT):
                    last = dve.tensor_tensor(
                        y[:, b, i, g * HG * HS:(g + 1) * HG * HS].rearrange("p (j d) -> p j d", j=HG),
                        v[:, i * HG:(i + 1) * HG, 0:HS],
                        rden[:, i * HG:(i + 1) * HG].unsqueeze(2).broadcast_to([P, HG, HS]), ALU.mult)
                last.then_inc(S["av_norm"], 1)

            dve.wait_ge(S["x_loaded"], 16)
            attention_stats(0)
            for n, (dst, r) in enumerate(((fold_a, P), (wq_T, P), (fold_b, LAT), (fold_c, LAT), (wk_T, P), (wv_T, P))):
                dve.wait_ge(S["fold_psum"], n + 1)
                dve.tensor_copy(dst if n in (0, 2, 3) else dst[:], ps[0:r, n, 0:P]).then_inc(S["fold_copied"], 1)
            attention_norm(0)
            dve.wait_ge(S["xs_loaded"], 16 * (B - 1))
            dve.wait_ge(S["pool_const"], 6)
            low_part(0, 0, 0)
            low_part(0, 1, 1)
            dve.tensor_copy(flag[:], ones[:, 0:1]).then_inc(S["av_norm"], 1)
            head_keys(0, 0)
            head_keys(1, 1)
            for u in range(NU):
                maxima(0, 0, u, u % 3)

            def batch(b, last):
                for g in range(NG):
                    G = b * NG + g
                    for u in range(NU):
                        if not (last and g == NG - 1):
                            maxima(G + 1, g + 1, u, slot("queries", g, u))
                        if not last:
                            if (g, u) == (0, 0):
                                attention_stats(b + 1)
                            if (g, u) == (0, 2):
                                attention_norm(b + 1)
                            if (g, u) == (1, 2):
                                low_part(b + 1, 0, 6)
                            if (g, u) == (1, 3):
                                low_part(b + 1, 1, 6)
                    if not (last and g >= NG - 2):
                        head_keys(G + 2, g)
                    divide(b, g)

            with dve.Fori(0, B - 1) as b:
                batch(b, False)
            batch(B - 1, True)

            dve.wait_ge(S["restw_loaded"], 80)
            dve.wait_ge(S["act_const"], 9)
            n_const = 0

            def const(ins):
                nonlocal n_const
                ins.then_inc(S["dve_const"], 1)
                n_const += 1
                dve.wait_ge(S["dve_const"], n_const)

            e, d2, z, z2, acc = (decay[:, n, :] for n in (1, 2, 3, 4, 5))
            const(dve.tensor_scalar(d2, e, 2.0, None, ALU.add))
            const(dve.reciprocal(d2, d2))
            const(dve.tensor_tensor(z, e, d2, ALU.mult))
            const(dve.tensor_tensor(z2, z, z, ALU.mult))
            const(dve.tensor_scalar(acc, z2, 1.0 / 19, None, ALU.mult))
            for k in range(17, 1, -2):
                const(dve.scalar_tensor_tensor(acc, acc, 1.0 / k, z2, ALU.add, ALU.mult))
            const(dve.scalar_tensor_tensor(acc, acc, 1.0, z, ALU.add, ALU.mult))
            const(dve.tensor_scalar(decay[:, 6, :], wr("fb"), 0.0, -8.0, ALU.max, ALU.mult))
            const(dve.scalar_tensor_tensor(ndecay[:], acc, -16.0, decay[:, 6, :], ALU.mult, ALU.add))
            const(dve.tensor_scalar(wr("winT"), wr("winT"), wr("gamma1"), None, ALU.mult))
            const(dve.tensor_scalar(wr("growT"), wr("growT"), wr("gamma2"), None, ALU.mult))
            assert n_const == REC_CONST, n_const

            n_step = 0

            def step(ins):
                nonlocal n_step
                ins.then_inc(S["dve_step"], 1)
                n_step += 1

            def steps_done():
                dve.wait_ge(S["dve_step"], n_step)

            def variance(b):
                for i in range(NT):
                    last = dve.bn_stats(stats[:, b, i, :], xs[:, b, i, :])
                step(last)
                steps_done()
                for i in range(NT):
                    last = dve.bn_aggr(meanvar[:, b, i, :], stats[:, b, i, :])
                last.then_inc(S["ln_var"], 1)

            def normalise(k, b, dst=xn, scales=0, signal=True):
                if signal:
                    dve.wait_ge(S["ln_rstd"], k * B + b + 1)
                for i in range(NT):
                    last = dve.tensor_scalar(dst[:, b, i, :], xs[:, b, i, :], meanvar[:, b, i, 0:1],
                                             rstd[:, b, scales + i:scales + i + 1], ALU.subtract, ALU.mult)
                    if signal:
                        last.then_inc(S["ln_norm"], 1)

            def residual(b, product, n, base):
                dve.wait_ge(S["res_psum"], product * B + b + 1)
                dve.tensor_tensor(xs[:, b], bank(4 + b).rearrange("p (i c) -> p i c", i=NT), base, ALU.add)\
                   .then_inc(S["res_done"], 1)
                dve.wait_ge(S["res_done"], n * B + b + 1)

            dve.wait_ge(S["ctx_loaded"], 32)
            step(dve.tensor_reduce(csum[:], ctxT_sb[:], AX.X, ALU.add))
            steps_done()
            for b in range(B):
                last = dve.tensor_scalar(csum_b[:, b, :], ones[:], csum[:, b:b + 1], 1.0 / CTX, ALU.mult, ALU.mult)
            last.then_inc(S["csum_ready"], 1)

            dve.wait_ge(S["av_norm"], B * NG + 1)
            for b in range(B + 1):
                if b < B:
                    dve.tensor_tensor(xs[:, b], xs[:, b], y[:, b], ALU.add).then_inc(S["res_done"], 1)
                    dve.wait_ge(S["res_done"], b + 1)
                    variance(b)
                if b >= 1:
                    normalise(XA, b - 1)
            dve.wait_ge(S["p2_psum"], 1)
            dve.tensor_copy(p2[:].rearrange("p b c -> p (b c)"), bank(0)).then_inc(S["p2_ready"], 1)
            for b in range(B):
                dve.wait_ge(S["xa_gelu"], b + 1)
                dve.tensor_tensor(xc[0:CTX, b % 2, b // 2, :], ps[0:CTX, b, :], gate_g[0:CTX, b % 2, b // 2, :],
                                  ALU.mult).then_inc(S["xa_prod"], 1)
            for b in range(B + 1):
                if b < B:
                    residual(b, 0, 1, xs[:, b])
                    variance(b)
                if b >= 1:
                    normalise(FFN, b - 1)
            for b in range(B):
                dve.wait_ge(S["gate_sum"], b + 1)
                dve.tensor_scalar(hsum_b[:, b, :], ones[:], hsum[:, b:b + 1], 1.0 / T, ALU.mult, ALU.mult)\
                   .then_inc(S["gate_bcast"], 1)
            tb1 = wr("Tb1").rearrange("p (f e) -> p f e", f=FC)
            dve.wait_ge(S["pool_const"], 7)

            def gate_vector(b):
                dve.wait_ge(S["g_psum"], b + 1)
                dve.tensor_tensor(gvec[:, b, :], ps[:, b, 0:NE], gb2_sb[:], ALU.add)
                dve.tensor_scalar(g9[0:NE, b, :], ps[0:NE, b, P:2 * P], wr("gb2"), None, ALU.add)\
                   .then_inc(S["g_ready"], 1)

            def mixed_bias(b):
                dve.wait_ge(S["g_ready"], b + 1)
                for f in range(FC):
                    last = dve.tensor_tensor(mb1_t[:, b, f, :], tb1[:, f, :], gvec[:, b, :], ALU.mult)
                step(last)
                steps_done()
                step(dve.tensor_reduce(mb1_s[:, b, :], mb1_t[:, b], AX.X, ALU.add))
                steps_done()
                dve.tensor_tensor(mb1_c[:, b, :], mb1_s[:, b, :], wr("b1"), ALU.add).then_inc(S["mb1_done"], 1)

            def mix_first(b):
                if b >= 2:
                    dve.wait_ge(S["u_psum"], FC * (b - 1))
                for e in range(NE):
                    last = dve.scalar_tensor_tensor(mw1[:, b % 2], tw1_sb[:, e, :], gvec[:, b, e:e + 1],
                                                    wr("W1T") if e == 0 else mw1[:, b % 2], ALU.mult, ALU.add)
                    if e < NE - 1:
                        step(last)
                        steps_done()
                last.then_inc(S["mix1_done"], 1)

            def mix_second(b):
                dve.wait_ge(S["mix2_half"], b + 1)
                for e in range(NE // 2, NE):
                    last = dve.scalar_tensor_tensor(mw2[:, b % 2], tw2_sb[:, e, :], gvec[:, b, e:e + 1],
                                                    mw2[:, b % 2], ALU.mult, ALU.add)
                    if e < NE - 1:
                        step(last)
                        steps_done()
                last.then_inc(S["mix2_done"], 1)

            for b in range(B):
                gate_vector(b)
            for b in range(B):
                mixed_bias(b)
                mix_first(b)
                mix_second(b)
            for b in range(B + 1):
                if b < B:
                    residual(b, 1, 2, xs[:, b])
                    variance(b)
                if b >= 1:
                    normalise(REC, b - 1, scales=NT)
                    normalise(REC, b - 1, dst=y, signal=False)

            def convolve(b):
                for c in range(HC):
                    dve.wait_ge(S["conv0"], HC * b + c + 1)
                    for k in range(1, KCONV):
                        last = dve.scalar_tensor_tensor(
                            xc[:, b % 2, c, k:T], ps[:, 2 + c, 0:T - k],
                            wr("convw")[:, c * KCONV + 3 - k:c * KCONV + 4 - k], xc[:, b % 2, c, k:T],
                            ALU.mult, ALU.add)
                        if k < KCONV - 1 or c < HC - 1:
                            step(last)
                            steps_done()
                last.then_inc(S["conv_done"], 1)

            def recurrence(b):
                dve.wait_ge(S["sx_done"], b + 1)
                dve.wait_ge(S["beta_done"], b + 1)
                step(dve.tensor_tensor(xc[:, b % 2], rec[:, b % 2], beta[:, b % 2], ALU.mult))
                steps_done()
                for c in range(HC):
                    last = dve.tensor_tensor_scan(rec[:, b % 2, c, :], alpha[:, b % 2, c, :], xc[:, b % 2, c, :],
                                                  0.0, ALU.mult, ALU.add)
                step(last)
                steps_done()
                dve.tensor_tensor(rec[:, b % 2], rec[:, b % 2], gate_g[:, b % 2], ALU.mult)\
                   .then_inc(S["hm_done"], 1)

            def inner_sum(b):
                dve.wait_ge(S["res_psum"], 2 * B + b + 1)
                dve.tensor_tensor(y[:, b], bank(7).rearrange("p (i c) -> p i c", i=NT), y[:, b], ALU.add)\
                   .then_inc(S["hx_done"], 1)
                dve.wait_ge(S["hx_done"], b + 1)
                for i in range(NT):
                    last = dve.scalar_tensor_tensor(sq[:], y[:, b, i, :], 1.0, y[:, b, i, :],
                                                    ALU.mult, ALU.mult, accum_out=sumsq[:, b, i:i + 1])
                    if i < NT - 1:
                        step(last)
                        steps_done()
                last.then_inc(S["ln_var"], 1)

            def scaled(b):
                dve.wait_ge(S["ln_rstd"], RMS * B + b + 1)
                for i in range(NT):
                    dve.tensor_scalar(xn[:, b, i, :], y[:, b, i, :], rstd[:, b, i:i + 1], None, ALU.mult)\
                       .then_inc(S["ln_norm"], 1)

            convolve(0)
            convolve(1)
            recurrence(0)
            for b in range(1, B):
                inner_sum(b - 1)
                if b + 1 < B:
                    convolve(b + 1)
                if b >= 3:
                    scaled(b - 3)
                recurrence(b)
            inner_sum(B - 1)
            for b in range(1, B):
                scaled(b)
            for b in range(B):
                dve.wait_ge(S["mg_gelu"], b + 1)
                dve.wait_ge(S["grow_psum"], 4 * b + 4)
                if b >= 2:
                    dve.wait_ge(S["res_psum"], 3 * B + b - 1)
                dve.tensor_tensor(rec[:, b % 2], bank(2, 2), gate_g[:, b % 2], ALU.mult).then_inc(S["mm_done"], 1)
            for b in range(B + 1):
                if b < B:
                    dve.wait_ge(S["hx_side"], b + 1)
                    residual(b, 3, 3, side[:, b])
                    variance(b)
                if b >= 1:
                    normalise(XA2, b - 1)
            for b in range(B + 1):
                if b < B:
                    dve.wait_ge(S["p2_side"], b + 1)
                    residual(b, 4, 4, side[:, b])
                    variance(b)
                if b >= 1:
                    normalise(EXPERT, b - 1)
            for b in range(B + 1):
                if b < B:
                    dve.wait_ge(S["b2_side"], b + 1)
                    dve.wait_ge(S["beta_side"], b + 1)
                    residual(b, 5, 5, y[:, b])
                    variance(b)
                if b >= 1:
                    normalise(LAST, b - 1)
                    dve.wait_ge(S["ln_norm"], NT * (LAST * B + b))
                    for i in range(NT):
                        last = dve.tensor_tensor(xn[:, b - 1, i, :], xn[:, b - 1, i, :], rows[:, P:2 * P], ALU.mult)
                    last.then_inc(S["gain_done"], 1)
                    dve.wait_ge(S["gain_done"], b)
                    dve.tensor_tensor(xn[:, b - 1], xn[:, b - 1], side[:, b - 1], ALU.add)\
                       .then_inc(S["out_ready"], 1)

        @block.tensor
        def _(pe):
            pe.wait_ge(S["attnw_loaded"], 16)

            def fold(n, lhsT, rhs, r, after):
                if after:
                    pe.wait_ge(S["fold_copied"], after)
                pe.matmul(ps[0:r, n, 0:P], lhsT, rhs, start=True, stop=True).then_inc(S["fold_psum"], 1)

            fold(0, wa("wuqT"), wa("wdq"), P, 0)
            fold(1, wa("wdq"), wa("wuqT"), P, 0)
            fold(2, wa("wuk"), fold_a, LAT, 1)
            fold(3, wa("wuv"), wa("woT"), LAT, 0)
            fold(4, wa("wdkv"), fold_b, P, 3)
            fold(5, wa("wdkv"), fold_c, P, 4)

            def norm_piece(b, dst):
                for i in range(NT):
                    pe.wait_ge(S["a_ln_norm"], b * NT + i + 1)
                    last = pe.transpose(bank(dst)[:, i * P:(i + 1) * P], a_xn[:, i, :], wa("ident"))
                last.then_inc(S["a_lnT_psum"], 1)

            def q_piece(b, dst):
                pe.wait_ge(S["a_lnT_ready"], b + 1)
                pe.matmul(bank(dst), wq_T[:], a_xT[:], start=True, stop=True).then_inc(S["q_psum"], 1)

            def k_piece(b, dst):
                pe.matmul(bank(dst), wk_T[:], a_xT[:], start=True, stop=True).then_inc(S["k_psum"], 1)

            def v_piece(b, dst):
                for i in range(NT):
                    last = pe.matmul(bank(dst)[:, i * P:(i + 1) * P], a_xT[:, i * P:(i + 1) * P], wv_T[:],
                                     start=True, stop=True)
                last.then_inc(S["v_psum"], 1)

            def k_stack(b, g, dst):
                pe.wait_ge(S["k_lo"], b + 1)
                pe.matmul(bank(dst), sel_r[:, 2, g, :], qk_hi[:, b, 1, :], start=True, stop=False)
                pe.matmul(bank(dst), sel_r[:, 3, g, :], qk_lo[:, b, 1, :], start=False, stop=True)\
                  .then_inc(S["kstack_psum"], 1)

            def q_parts(b, g, dst, stop):
                pe.matmul(bank(dst), sel_r[:, 0, g, :], qk_hi[:, b, 0, :], start=True, stop=False)
                return pe.matmul(bank(dst), sel_r[:, 1, g, :], qk_lo[:, b, 0, :], start=False, stop=stop)

            def q_stack(b, g, dst):
                q_parts(b, g, dst, True).then_inc(S["qstack_psum"], 1)

            def s_unit(G, g, u, at):
                s = bank(2 * at, 2).rearrange("p a n -> p (a n)")
                for j, rank, c, w in segments(u):
                    i = NT - 1 - rank
                    if u < 2:
                        pe.wait_ge(S["kmask_ready"], G * HG + j + 1)
                    pe.matmul(s[:, c:c + w], qstack[:, g % 2, i * P:(i + 1) * P], km[:, (g % 2) * HG + j, 0:w],
                              start=True, stop=False)
                    last = pe.matmul(s[:, c + w - P:c + w], ident_b[:], mask_b[:], start=False, stop=True)
                last.then_inc(S["s_psum"], 1)

            def t_unit(g, u, at):
                s = bank(2 * at, 2).rearrange("p a n -> p (a n)")
                for j, i, c, w in segments(u):
                    last = pe.matmul(s[:, c:c + w], km[:, (g % 2) * HG + j, i * P:(i + 1) * P],
                                     mstack[:, g % 2, T - w:T], start=True, stop=True)
                last.then_inc(S["e_psum"], 1)

            def max_rows(b, g, G):
                pe.wait_ge(S["max_done"], (G + 1) * NU)
                q_parts(b, g, 6, False)
                for i in range(NT):
                    last = pe.matmul(bank(6)[:, i * P:(i + 1) * P], negmax[:, g % 2, i, :], ident_r[:],
                                     start=False, stop=(i == NT - 1))
                last.then_inc(S["m_psum"], 1)

            def values(b, g, G):
                pe.wait_ge(S["av_norm"], G + 1)
                if g == 0:
                    pe.wait_ge(S["vx_ready"], b + 1)
                for i, units in ((0, (0, 1)), (1, (2, 3)), (3, (2, 3)), (2, (4,))):
                    pe.wait_ge(S["sel_done"], G * NU + units[-1] + 1)
                    for j in range(HG):
                        u, c, w = next((u, c, w) for u in units for jj, r, c, w in segments(u) if jj == j and r == i)
                        last = pe.matmul(ps[j * VW:(j + 1) * VW, 7, T - w:T], vx[:, i, g * HG + j, :],
                                         probs[:, g % 2, u * UNIT + c:u * UNIT + c + w],
                                         start=(i == 0), stop=(i == 2), tile_position=(0, j * VW))
                last.then_inc(S["av_psum"], 1)

            def tokens_first(G):
                pe.wait_ge(S["av_ready"], G + 1)
                for i in range(NT):
                    last = pe.transpose(bank(7)[:, i * P:(i + 1) * P], av_sb[:, i * P:(i + 1) * P], wa("ident"))
                last.then_inc(S["avT_psum"], 1)

            norm_piece(0, 6)
            pe.wait_ge(S["fold_copied"], 6)
            q_piece(0, 0)
            k_piece(0, 1)
            v_piece(0, 2)
            pe.wait_ge(S["act_const"], 7)
            pe.wait_ge(S["q_lo"], 1)
            k_stack(0, 0, 3)
            q_stack(0, 0, 4)
            k_stack(0, 1, 5)
            q_stack(0, 1, 7)
            pe.wait_ge(S["v_ready"], 1)
            pe.wait_ge(S["kstack_ready"], 2)
            pe.wait_ge(S["qstack_ready"], 1)
            for u in range(NU):
                if u >= 3:
                    pe.wait_ge(S["max_done"], u - 2)
                s_unit(0, 0, u, u % 3)
            max_rows(0, 0, 0)

            def batch(b, last):
                for g in range(NG):
                    G = b * NG + g
                    nb, ng = (b, g + 1) if g + 1 < NG else (b + 1, 0)
                    ab, ag = (b, g + 2) if g + 2 < NG else (b + 1, g + 2 - NG)
                    has_next = not (last and g == NG - 1)
                    has_after = not (last and g >= NG - 2)
                    pe.wait_ge(S["mstack_ready"], G + 1)
                    if has_next:
                        pe.wait_ge(S["qstack_ready"], G + 2)
                    for u in range(NU):
                        for kind in ("queries", "keys"):
                            n = g * 2 * NU + 2 * u + (kind == "keys")
                            if not has_next and kind == "queries":
                                continue
                            if not has_next and u > 0:
                                if u >= 3:
                                    pe.wait_ge(S["exp_done"], G * NU + u - 2)
                            elif n < 3:
                                pe.wait_ge(S["max_done"], (G + 1) * NU)
                            elif (n - 3) % 2 == 0:
                                m = n - 3
                                pe.wait_ge(S["max_done"], (b * NG + m // (2 * NU) + 1) * NU + m % (2 * NU) // 2 + 1)
                            else:
                                m = n - 3
                                pe.wait_ge(S["exp_done"], (b * NG + m // (2 * NU)) * NU + m % (2 * NU) // 2 + 1)
                            if kind == "keys":
                                t_unit(g, u, slot(kind, g, u))
                            else:
                                s_unit(G + 1, g + 1, u, slot(kind, g, u))
                        if has_after and u == 0:
                            k_stack(ab, ag, 6)
                        if has_after and u == 1:
                            pe.wait_ge(S["kstack_ready"], G + 3)
                            q_stack(ab, ag, 6)
                        if not last:
                            if (g, u) == (0, 3):
                                pe.wait_ge(S["qstack_ready"], G + 3)
                                norm_piece(b + 1, 6)
                            if (g, u) == (1, 2):
                                pe.wait_ge(S["qstack_ready"], G + 3)
                                q_piece(b + 1, 6)
                            if (g, u) == (1, 3):
                                pe.wait_ge(S["q_lo"], b + 2)
                                k_piece(b + 1, 6)
                            if (g, u) == (2, 2):
                                pe.wait_ge(S["qstack_ready"], G + 3)
                                v_piece(b + 1, 6)
                    values(b, g, G)
                    tokens_first(G)
                    if has_next:
                        if has_after:
                            pe.wait_ge(S["qstack_ready"], G + 3)
                        if not last and g == 0:
                            pe.wait_ge(S["a_lnT_ready"], b + 2)
                        if not last and g == 1:
                            pe.wait_ge(S["k_lo"], b + 2)
                        if not last and g == 2:
                            pe.wait_ge(S["v_ready"], b + 2)
                        max_rows(nb, ng, G + 1)

            with pe.Fori(0, B - 1) as b:
                batch(b, False)
            batch(B - 1, True)

            def norm_T(k, b):
                for i in range(NT):
                    pe.wait_ge(S["ln_norm"], (k * B + b) * NT + i + 1)
                    last = pe.transpose(bank(4 + b)[:, i * P:(i + 1) * P], xn[:, b, i, :], wa("ident"))
                last.then_inc(S["lnT_psum"], 1)

            def natural(dst, terms):
                for i in range(NT):
                    these = terms(slice(i * P, (i + 1) * P))
                    for m, (lhsT, rhs) in enumerate(these):
                        last = pe.matmul(bank(dst)[:, i * P:(i + 1) * P], lhsT, rhs,
                                         start=(m == 0), stop=(m == len(these) - 1))
                last.then_inc(S["res_psum"], 1)

            pe.wait_ge(S["csum_ready"], 1)
            for b in range(B):
                pe.matmul(bank(0)[:, b * P:(b + 1) * P], csum_b[:, b, :], wr("x2T"), start=True, stop=False)
                last = pe.matmul(bank(0)[:, b * P:(b + 1) * P], ones[0:1, :], wr("xb"), start=False, stop=True)
            last.then_inc(S["p2_psum"], 1)
            for b in range(B):
                norm_T(XA, b)
            pe.wait_ge(S["p2_ready"], 1)
            for b in range(B):
                pe.wait_ge(S["lnT_ready"], XA * B + b + 1)
                pe.matmul(ps[0:CTX, b, :], ctxT_sb[:, b, :], xT[:, b, :], start=True, stop=True)\
                  .then_inc(S["xa_psum"], 1)
            for b in range(B):
                pe.wait_ge(S["xa_prod"], b + 1)
                natural(4 + b, lambda t: [(xc[0:CTX, b % 2, b // 2, t], ctxn_sb[:, b, :])])
            for b in range(B):
                norm_T(FFN, b)
            for b in range(B):
                pe.wait_ge(S["lnT_ready"], FFN * B + b + 1)
                pe.matmul(bank(b), wr("gw1T"), xT[:, b, :], start=True, stop=True).then_inc(S["gate_psum"], 1)
            for b in range(B):
                pe.wait_ge(S["gate_bcast"], b + 1)
                pe.matmul(ps[:, b, 0:NE], hsum_b[:, b, :], wr("gw2T"), start=True, stop=True)
                pe.matmul(ps[0:NE, b, P:2 * P], wr("gw2T"), hsum_b[:, b, :], start=True, stop=True)\
                  .then_inc(S["g_psum"], 1)

            def ffn_product(b):
                pe.wait_ge(S["mix2_done"], b + 1)
                pe.wait_ge(S["u_ready"], FC * (b + 1))
                natural(4 + b, lambda t: [(hid[:, b % 2, f, t], mw2[:, b % 2, f * P:(f + 1) * P])
                                          for f in range(FC)] + [(g9[:, b, :], wr("tb2x"))])

            pe.wait_ge(S["g_ready"], B)
            for b in range(B):
                pe.wait_ge(S["mix1_done"], b + 1)
                for f in range(FC):
                    if b:
                        pe.wait_ge(S["u_ready"], FC * (b - 1) + f + 1)
                    pe.matmul(bank(f), mw1[:, b % 2, f * P:(f + 1) * P], xT[:, b, :], start=True, stop=True)\
                      .then_inc(S["u_psum"], 1)
                ffn_product(b)
            for b in range(B):
                norm_T(REC, b)
            wg = wr("wgT").rearrange("p (c n) -> p c n", c=HC)

            def inputs(b):
                pe.wait_ge(S["lnT_ready"], REC * B + b + 1)
                if b == 0:
                    pe.wait_ge(S["u_ready"], FC * B)
                for n in range(4):
                    if b and n == 0:
                        pe.wait_ge(S["zg_gelu"], b)
                    if b and n == 2:
                        pe.wait_ge(S["conv_done"], b)
                    pe.matmul(bank(n), wr("winT")[:, n * P:(n + 1) * P], xT[:, b, :], start=True, stop=True)\
                      .then_inc(S["z_psum"], 1)

            def gates(b):
                pe.wait_ge(S["conv_done"], b + 1)
                for n in range(4):
                    m = 4 * b + n
                    if m >= 3:
                        pe.wait_ge(S["gates_sig"], m - 2)
                    for c in range(HC):
                        last = pe.matmul(bank(4 + m % 3), wg[:, c, n * P:(n + 1) * P], xc[:, b % 2, c, :],
                                         start=(c == 0), stop=(c == HC - 1))
                    last.then_inc(S["gates_psum"], 1)

            def recurrent_product(b):
                pe.wait_ge(S["hm_done"], b + 1)
                if b:
                    pe.wait_ge(S["hx_done"], b)
                natural(7, lambda t: [(rec[:, b % 2, c, t], wr("woutT")[:, c * P:(c + 1) * P]) for c in range(HC)])

            inputs(0)
            inputs(1)
            pe.wait_ge(S["lnT_ready"], (REC + 1) * B)
            gates(0)
            recurrent_product(0)
            for b in range(1, B):
                if b + 1 < B:
                    inputs(b + 1)
                gates(b)
                recurrent_product(b)
            pe.wait_ge(S["hx_done"], B)
            pe.wait_ge(S["gates_sig"], 4 * B)
            for b in range(B):
                norm_T(RMS, b)

            def shrink_product(b):
                pe.wait_ge(S["mm_done"], b + 1)
                natural(4 + b, lambda t: [(rec[:, b % 2, c, t], wr("shrinkT")[:, c * P:(c + 1) * P])
                                          for c in range(HC)])

            for b in range(B):
                pe.wait_ge(S["lnT_ready"], RMS * B + b + 1)
                for n in range(4):
                    if b and n == 0:
                        pe.wait_ge(S["mg_gelu"], b)
                    if b and n == 2:
                        pe.wait_ge(S["mm_done"], b)
                    pe.matmul(bank(n), wr("growT")[:, n * P:(n + 1) * P], xT[:, b, :], start=True, stop=True)\
                      .then_inc(S["grow_psum"], 1)
                if b:
                    shrink_product(b - 1)
            shrink_product(B - 1)
            for b in range(B):
                norm_T(XA2, b)
            for b in range(B):
                pe.wait_ge(S["lnT_ready"], XA2 * B + b + 1)
                natural(4 + b, lambda t: [(xT[:, b, t], wr("x1T"))])
            for b in range(B):
                norm_T(EXPERT, b)

            def expert_product(b):
                pe.wait_ge(S["h_ready"], FC * (b + 1))
                natural(4 + b, lambda t: [(hid[:, b % 2, f, t], wr("m2")[:, f * P:(f + 1) * P])
                                          for f in range(FC)])

            for b in range(B):
                pe.wait_ge(S["lnT_ready"], EXPERT * B + b + 1)
                for f in range(FC):
                    if b:
                        pe.wait_ge(S["h_ready"], FC * (b - 1) + f + 1)
                    pe.matmul(bank(f), wr("m1")[:, f * P:(f + 1) * P], xT[:, b, :], start=True, stop=True)\
                      .then_inc(S["h_psum"], 1)
                if b:
                    expert_product(b - 1)
            expert_product(B - 1)


REC_CONST = 18


def kernel(**inputs):
    import numpy as _np
    import concourse.bacc as _bacc
    from concourse.bass_utils import run_bass_kernel_spmd as _run

    a = {k: _np.asarray(v) for k, v in inputs.items()}

    def chunked(w):
        n = w.shape[0] // P
        return w.reshape(n, P, w.shape[1]).transpose(1, 0, 2).reshape(P, -1)

    def per_chunk(v):
        return v.reshape(-1, P).T

    part = {"selqh": (0, 2), "selql": (1,), "selkh": (0, 1), "selkl": (2,)}
    sel = {n: _np.zeros((P, NG, HG, 4, HS), _np.float32) for n in part}
    for n, places in part.items():
        for h in range(NH):
            for d in range(HS):
                for pl in places:
                    sel[n][h * HS + d, h // HG, h % HG, pl, d] = 1.0
    row = _np.arange(P)
    attn = {
        "wdq": a["L0_attn_W_dq"], "wuqT": a["L0_attn_W_uq"].T, "wdkv": a["L0_attn_W_dkv"],
        "wuk": a["L0_attn_W_uk"], "wuv": a["L0_attn_W_uv"], "woT": a["L0_attn_W_o"].T,
        "ident": _np.eye(P, dtype=_np.float32),
        "mask": _np.where(row[None, :] > row[:, None], NEG, 0.0).astype(_np.float32),
        "kone": (row % 32 == 24).astype(_np.float32)[:, None],
        "headcol": (row[:, None] // 32 == _np.arange(HG)[None, :]).astype(_np.float32),
    }
    rest = {
        "gw1T": a["L0_ffn_gate_w1"].T, "gb1": a["L0_ffn_gate_b1"][:, None], "gw2T": a["L0_ffn_gate_w2"].T,
        "gb2": a["L0_ffn_gate_b2"][:, None], "W1T": a["L0_ffn_W1"].T, "b1": per_chunk(a["L0_ffn_b1"]),
        "W2T": chunked(a["L0_ffn_W2"].T),
        "tb2x": _np.concatenate([a["L0_ffn_Tb2"], a["L0_ffn_b2"][None]], 0),
        "Tb1": a["L0_ffn_Tb1"].reshape(NE, FC, P).transpose(2, 1, 0).reshape(P, -1),
        "winT": a["L1_attn_W_in"].T, "gamma1": a["L1_attn_gamma1"][:, None],
        "convw": a["L1_attn_conv_w"].reshape(HC, P, KCONV).transpose(1, 0, 2).reshape(P, -1),
        "convb": per_chunk(a["L1_attn_conv_b"]), "wgT": chunked(a["L1_attn_W_gates"].T),
        "bg": per_chunk(a["L1_attn_b_gates"]), "fb": per_chunk(a["L1_attn_forget_base"]),
        "woutT": chunked(a["L1_attn_W_out"].T), "gamma2": a["L1_attn_gamma2"][:, None],
        "growT": a["L1_attn_W_grow"].T, "shrinkT": chunked(a["L1_attn_W_shrink"].T),
        "x1T": a["L1_xattn_W"][:, :P].T, "x2T": a["L1_xattn_W"][:, P:].T, "xb": a["L1_xattn_b"][None],
        "m1": a["L1_ffn_w1"][0], "mb1": per_chunk(a["L1_ffn_b1"][0]), "m2": chunked(a["L1_ffn_w2"][0]),
    }

    def packed(parts, at, width, values):
        m = _np.zeros((P, width), _np.float32)
        for name, r, w in parts:
            c = at[name][0]
            assert values[name].shape == (r, w), (name, values[name].shape)
            m[0:r, c:c + w] = values[name]
        return m

    arrays = {
        "x": a["x"], "ctxn": _np.ascontiguousarray(a["ctx_1024"].transpose(1, 0, 2)),
        "ctxT": _np.ascontiguousarray(a["ctx_1024"].transpose(2, 0, 1)),
        "attnw": packed(ATTN_PARTS, ATTN_AT, ATTN_W, attn),
        "selw": _np.concatenate([sel[n].reshape(P, -1) for n in SELECTIONS], 1),
        "restw": packed(REST_PARTS, REST_AT, REST_W, rest),
        "rowsw": _np.concatenate([a["L1_ffn_b2"][0], a["L1_ffn_gamma"], a["L1_ffn_beta"]])[None],
        "tw1": _np.ascontiguousarray(a["L0_ffn_TW1"].transpose(2, 0, 1)),
        "tw2": _np.ascontiguousarray(a["L0_ffn_TW2"].reshape(NE, P, FC, P).transpose(3, 0, 2, 1).reshape(P, NE, -1)),
        "gb2row": a["L0_ffn_gate_b2"][None],
    }
    nc = _bacc.Bacc("TRN2", target_bir_lowering=False, num_devices=1)
    args, sent = [], {}
    for name, v in arrays.items():
        v = _np.ascontiguousarray(v)
        sent["in_" + name] = v
        args.append(nc.dram_tensor("in_" + name, v.shape, mybir.dt.from_np(v.dtype), kind="ExternalInput").ap())
    args.append(nc.dram_tensor("out_0", (B, T, P), F32, kind="ExternalOutput").ap())
    decoder_kernel(nc, *args)
    r = _run(nc, [sent], core_ids=[0])
    return r.results[0]["out_0"]
```

```python
import numpy as np
from contextlib import ExitStack

import concourse.bass as bass
from concourse import mybir

P = 128
B = 4
T = 512
NT = T // P
NH = 16
HS = P // NH
NG = 4
HG = NH // NG
LAT = 32
VW = 32
CTX = 77
NE = 8
FC = 4
HC = 2
KCONV = 4
GW = HG * (T + 384 + 256 + 128)
UNIT = 1024
NU = GW // UNIT
EPS = 1e-5
NEG = -1e30

F32 = mybir.dt.float32
F32R = mybir.dt.float32r
BF16 = mybir.dt.bfloat16
ALU = mybir.AluOpType
ACT = mybir.ActivationFunctionType
AX = mybir.AxisListType

ATTN_PARTS = [("wdq", LAT, P), ("wuqT", LAT, P), ("wdkv", LAT, P), ("wuk", P, LAT), ("wuv", P, LAT),
              ("woT", P, P), ("ident", P, P), ("mask", P, P), ("kone", P, 1), ("headcol", P, HG)]
SELECTIONS = ("selqh", "selql", "selkh", "selkl")
REST_PARTS = [("gw1T", P, P), ("gb1", P, 1), ("gw2T", P, NE), ("gb2", NE, 1), ("W1T", P, FC * P),
              ("b1", P, FC), ("W2T", P, FC * P), ("tb2x", NE + 1, P), ("Tb1", P, FC * NE),
              ("winT", P, 4 * P), ("gamma1", P, 1), ("convw", P, HC * KCONV), ("convb", P, HC),
              ("wgT", P, HC * 4 * P), ("bg", P, 4), ("fb", P, HC), ("woutT", P, HC * P),
              ("gamma2", P, 1), ("growT", P, 4 * P), ("shrinkT", P, HC * P),
              ("x1T", P, P), ("x2T", P, P), ("xb", 1, P),
              ("m1", P, FC * P), ("mb1", P, FC), ("m2", P, FC * P)]


def columns(parts):
    at, out = 0, {}
    for name, rows, width in parts:
        out[name] = (at, rows, width)
        at += width
    return out, at


ATTN_AT, ATTN_W = columns(ATTN_PARTS)
REST_AT, REST_W = columns(REST_PARTS)

def segments(unit):
    width = [512, 384, 256, 128]
    if unit < 2:
        return [(j, 0, 512 * (j % 2), width[0]) for j in (2 * unit, 2 * unit + 1)]
    if unit < 4:
        return [(j, r, 512 * (j % 2) + c, width[r])
                for j in (2 * unit - 4, 2 * unit - 3) for r, c in ((1, 0), (3, 384))]
    return [(j, 2, 256 * j, width[2]) for j in range(HG)]


TURNS = (("queries", 0), ("queries", 1), ("keys", 0), ("queries", 2), ("keys", 1), ("queries", 3), ("keys", 2),
         ("queries", 4), ("keys", 3), ("keys", 4))


def slot(kind, g, u):
    return (g * len(TURNS) + TURNS.index((kind, u))) % 3


def decoder_kernel(nc, x, ctxn, ctxT, attnw, selw, restw, rowsw, tw1, tw2, gb2row, out):
    es = ExitStack()
    with es:
        def sb(name, shape, dt=F32, stack=es):
            return stack.enter_context(nc.sbuf_tensor(name, shape, dt))

        aw = sb("aw", [P, ATTN_W])
        rw = sb("rw", [P, REST_W])
        rows = sb("rows", [P, 3 * P])
        tw1_sb = sb("tw1_sb", [P, NE, FC * P])
        tw2_sb = sb("tw2_sb", [P, NE, FC * P])
        gb2_sb = sb("gb2_sb", [P, NE])

        def wa(name):
            c, r, w = ATTN_AT[name]
            return aw[0:r, c:c + w]

        def wr(name):
            c, r, w = REST_AT[name]
            return rw[0:r, c:c + w]

        ones = sb("ones", [P, P])
        halfpow = sb("halfpow", [P, 4 * NT])
        decay = sb("decay", [P, 7, HC])
        hdecay = sb("hdecay", [P, HC])
        hbg = sb("hbg", [P, 4])
        sqrt_bias = sb("sqrt_bias", [P, 1])
        flag = sb("flag", [P, 1])

        xs = sb("xs", [P, B, NT, P])
        y = sb("y", [P, B, NT, P])
        ctxn_sb = sb("ctxn_sb", [CTX, B, P])
        ctxT_sb = sb("ctxT_sb", [P, B, CTX])

        stats = sb("stats", [P, B, NT, 6])
        meanvar = sb("meanvar", [P, B, NT, 2])
        vareps = sb("vareps", [P, B, 2 * NT])
        rstd = sb("rstd", [P, B, 2 * NT])

        att = ExitStack()
        ident_r = sb("ident_r", [P, P], F32R, att)
        ident_b = sb("ident_b", [P, P], BF16, att)
        mask_b = sb("mask_b", [P, 2, P], BF16, att)
        sel_r = sb("sel_r", [P, 4, NG, P], F32R, att)
        wq_T = sb("wq_T", [P, P], F32, att)
        wk_T = sb("wk_T", [P, P], F32, att)
        wv_T = sb("wv_T", [P, P], F32, att)
        a_stats = sb("a_stats", [P, NT, 6], F32, att)
        sum_meanvar = sb("sum_meanvar", [P, NT, 2], F32, att)
        a_xn = sb("a_xn", [P, NT, P], F32, att)
        a_xT = sb("a_xT", [P, T], F32, att)
        qk_hi = sb("qk_hi", [P, B, 2, T], F32R, att)
        qk_lo = sb("qk_lo", [P, B, 2, T], F32R, att)
        v_all = sb("v_all", [P, T], F32, att)
        vx = sb("vx", [P, NT, NH, VW], F32, att)
        kstack = sb("kstack", [P, T], F32, att)
        qstack = sb("qstack", [P, 2, T], F32R, att)
        mstack = sb("mstack", [P, 2, T], F32R, att)
        km = sb("km", [P, 2 * HG, T], F32R, att)
        negmax = sb("negmax", [P, 2, NT, P], F32R, att)
        probs = sb("probs", [P, 2, GW], F32, att)
        av_sb = sb("av_sb", [P, T], F32, att)
        fold_a = av_sb[:, 0:P]
        fold_b = av_sb[0:LAT, P:2 * P]
        fold_c = av_sb[0:LAT, 2 * P:3 * P]
        rden = sb("rden", [P, NT * HG], F32, att)
        att.close()

        tiles = sb("tiles", [P, B, 2, T])
        side = sb("side", [P, B, NT, P])
        hsum = sb("hsum", [P, B])
        hsum_b = sb("hsum_b", [P, B, P])
        gvec = sb("gvec", [P, B, NE])
        g9 = sb("g9", [NE + 1, B, P])
        mb1_t = sb("mb1_t", [P, B, FC, NE])
        mb1_s = sb("mb1_s", [P, B, FC])
        mb1_c = sb("mb1_c", [P, B, FC])
        hid = sb("hid", [P, B, FC, T])
        gate_g = sb("gate_g", [P, B, HC, T])
        xc = sb("xc", [P, B, HC, T])
        sumsq = sb("sumsq", [P, B, NT])
        csum = sb("csum", [P, B])
        csum_b = sb("csum_b", [P, B, P])
        p2 = sb("p2", [P, B, P])

        def xn(b, i):
            return tiles[:, b, 0, i * P:(i + 1) * P]

        def xT(b):
            return tiles[:, b, 1, :]

        beta = tiles
        alpha = hid[:, :, 0:HC, :]
        rec = hid[:, :, HC:2 * HC, :]

        def mixed_term(b, e):
            return hid[:, b, e, :] if e < FC else xc[:, b, e - FC, :]

        def mw1(b):
            return gate_g[:, b, 0, :]

        def mw2(b):
            return gate_g[:, b, 1, :]

        ps = es.enter_context(nc.psum_tensor("ps", [P, 8, 512], F32))

        def bank(i, n=1):
            return ps[:, i, :] if n == 1 else ps[:, i:i + n, :]

        names = """x_loaded xs_loaded attnw_loaded selw_loaded restw_loaded ctx_loaded fold_psum fold_copied
            att_sum att_stats att_aggr att_var act_const pool_const dve_const pool_step dve_step a_ln_var
            a_ln_rstd a_ln_norm a_lnT_psum a_lnT_ready a_stats_done a_eps_done q_psum k_psum v_psum q_hi
            k_hi q_lo k_lo v_ready vx_ready kstack_psum qstack_psum kstack_ready qstack_ready kmask_ready
            s_psum max_done e_psum exp_done sel_done m_psum mstack_ready av_psum av_ready avT_psum av_den
            av_norm xa_psum xa_gelu xa_prod gate_psum gate_sum gate_bcast g_psum g_ready mix1_done mix2_done
            mixed_terms mix2_half mb1_done u_psum u_ready z_psum zg_gelu conv0 conv_done gates_psum
            gates_sig alpha_sq alpha_done beta_done sx_half sx_done hm_done hx_done hx_side y_ready
            grow_psum mg_gelu mm_done h_psum h_ready p2_psum p2_ready csum_ready p2_side b2_side beta_side
            gain_done out_ready out_stored""".split()
        S = {n: es.enter_context(nc.semaphore(n)) for n in names}
        of_batch = "eps_done ln_var ln_rstd ln_norm lnT_psum lnT_ready res_psum res_done".split()
        SB = {n: [es.enter_context(nc.semaphore(n + str(b))) for b in range(B)] for n in of_batch}

        block = es.enter_context(nc.Block())

        x_v = x.rearrange("b (i p) c -> b p i c", p=P)
        out_v = out.rearrange("b (i p) c -> b p i c", p=P)

        XA, FFN, REC, RMS, XA2, EXPERT, LAST = range(7)

        def in_order(places):
            steps = sorted((place + LAGS[b], b, n) for n, place in places.items() for b in range(B))
            return [(n, b) for place, b, n in steps]

        @block.sync
        def _(sp):
            sp.dma_start(xs[:, 0], x_v[0]).then_inc(S["x_loaded"], 16)
            sp.dma_start(aw[:], attnw).then_inc(S["attnw_loaded"], 16)
            sp.dma_start(probs[:, 0, 0:4 * NG * P], selw).then_inc(S["selw_loaded"], 16)
            for b in range(1, B):
                sp.dma_start(xs[:, b], x_v[b]).then_inc(S["xs_loaded"], 16)
            sp.dma_start(rw[:], restw).then_inc(S["restw_loaded"], 16)
            sp.dma_start(ctxT_sb[:], ctxT).then_inc(S["ctx_loaded"], 16)
            sp.dma_start(ctxn_sb[:], ctxn).then_inc(S["ctx_loaded"], 16)
            sp.dma_start(gb2_sb[:], gb2row.broadcast_to([P, NE])).then_inc(S["restw_loaded"], 16)
            sp.dma_start(rows[:], rowsw.broadcast_to([P, 3 * P])).then_inc(S["restw_loaded"], 16)
            sp.dma_start(tw1_sb[:], tw1).then_inc(S["restw_loaded"], 16)
            sp.dma_start(tw2_sb[:], tw2).then_inc(S["restw_loaded"], 16)
            for b in range(B):
                sp.wait_ge(S["out_ready"], b + 1)
                result = tiles[:, b, 0, :].rearrange("p (i c) -> p i c", i=NT)
                sp.dma_start(out_v[b], result).then_inc(S["out_stored"], 16)
            sp.wait_ge(S["out_stored"], 16 * B)

        @block.gpsimd
        def _(pool):
            spare = pool.alloc_register("pool_spare")

            def wait_apart(sem, value):
                if isinstance(value, int):
                    pool.wait_ge(sem, value)
                    return
                pool.reg_mov(spare, value)
                value = pool.snap(spare)
                pool.wait_ge(S["pool_const"], 6)
                pool.wait_ge(sem, value)

            pool.memset(ones[:], 1.0).then_inc(S["pool_const"], 1)
            pool.memset(halfpow[:], -0.5).then_inc(S["pool_const"], 1)
            pool.memset(vx[:], 0.0).then_inc(S["pool_const"], 1)
            pool.memset(negmax[:].bitcast(F32), 0.0).then_inc(S["pool_const"], 1)
            pool.memset(sqrt_bias[:], 0.25 * (1.0 + 1e-6)).then_inc(S["pool_const"], 1)
            pool.wait_ge(S["pool_const"], 5)
            pool.memset(vx[:, :, :, HS:HS + 1], 1.0).then_inc(S["pool_const"], 1)
            pool.wait_ge(S["pool_const"], 6)

            def attention_rstd(b):
                pool.wait_ge(S["a_ln_var"], b + 1)
                pool.tensor_scalar(vareps[:, b, 0:NT], meanvar[:, b, :, 1], 1.0, EPS, ALU.mult, ALU.add)\
                    .then_inc(S["a_eps_done"], 1)
                pool.wait_ge(S["a_eps_done"], b + 1)
                pool.tensor_tensor(rstd[:, b, 0:NT], vareps[:, b, 0:NT], halfpow[:, 0:NT], ALU.pow)\
                    .then_inc(S["a_ln_rstd"], 1)

            def value_operand(b):
                wait_apart(S["v_ready"], b + 1)
                pool.tensor_copy(vx[:].rearrange("p i h d -> p (i h) d")[:, :, 0:HS],
                                 v_all[:].rearrange("p (n d) -> p n d", d=HS)).then_inc(S["vx_ready"], 1)

            def causal(G, g, u):
                wait_apart(S["exp_done"], G * NU + u + 1)
                seg = probs[:, g % 2, u * UNIT:(u + 1) * UNIT]
                n = 4 if u == 4 else 2
                v = seg.rearrange("p (j t) -> p j t", j=n)
                if u in (2, 3):
                    pool.affine_select(out=v[:, :, 384:512], in_=v[:, :, 384:512], pattern=[[0, 2], [1, P]],
                                       compare_op=ALU.is_ge, fill=0.0, base=0, channel_multiplier=-1)
                pool.affine_select(out=v[:, :, 0:P], in_=v[:, :, 0:P], pattern=[[0, n], [1, P]],
                                   compare_op=ALU.is_ge, fill=0.0, base=0, channel_multiplier=-1)\
                    .then_inc(S["sel_done"], 1)

            def norm_rstd(k, b, both=False):
                if k == XA:
                    pool.wait_ge(S["att_var"], b + 1)
                else:
                    pool.wait_ge(SB["ln_var"][b], k)
                n = NT
                if k == RMS:
                    last = pool.tensor_scalar(vareps[:, b, 0:NT], sumsq[:, b, :], 1.0 / P, 0.0, ALU.mult, ALU.add)
                else:
                    last = pool.tensor_scalar(vareps[:, b, 0:NT], meanvar[:, b, :, 1], 1.0, EPS, ALU.mult, ALU.add)
                if both:
                    n = 2 * NT
                    last = pool.tensor_scalar(vareps[:, b, NT:n], meanvar[:, b, :, 1], 1.0, 0.0, ALU.mult, ALU.add)
                last.then_inc(SB["eps_done"][b], 1)
                pool.wait_ge(SB["eps_done"][b], k + 1)
                pool.tensor_tensor(rstd[:, b, 0:n], vareps[:, b, 0:n], halfpow[:, 0:n], ALU.pow)\
                    .then_inc(SB["ln_rstd"][b], 1)

            def attention_sum(b):
                wait_apart(S["av_norm"], (b + 1) * NG + 1)
                pool.tensor_tensor(xs[:, b], xs[:, b], y[:, b], ALU.add).then_inc(S["att_sum"], 1)

            def group(b, g, last=False):
                if g == 0:
                    if not (isinstance(b, int) and b == 0):
                        pool.wait_ge(S["av_psum"], b * NG)
                    value_operand(b)
                    if isinstance(b, int):
                        for later in range(1, B):
                            attention_rstd(later)
                for u in range(NU):
                    causal(b * NG + g, g, u)
                    if g == 0 and u == 2 and not (isinstance(b, int) and b == 0):
                        attention_sum(b - 1)
                    if last and g == 2 and u < B - 1:
                        norm_rstd(XA, u)

            attention_rstd(0)
            group(0, 0)
            with pool.Fori(0, B - 1) as b:
                for g in (1, 2, 3):
                    group(b, g)
                group(b + 1, 0)
            for g in (1, 2, 3):
                group(B - 1, g, last=True)
            attention_sum(B - 1)

            pool.wait_ge(S["avT_psum"], B * NG)
            pool.memset(g9[:], 1.0).then_inc(S["pool_const"], 1)

            n_step = 0

            def pool_step(n, b):
                nonlocal n_step
                if n == SUM:
                    if b == B - 1:
                        norm_rstd(XA, b)
                elif n == FFN_VAR:
                    norm_rstd(FFN, b)
                elif n == MIX:
                    for e in range(MIXED):
                        pool.wait_ge(S["mixed_terms"], b * MIXED + e + 1)
                        if e:
                            pool.wait_ge(S["pool_step"], n_step)
                        last = pool.tensor_tensor(mw2(b), wr("W2T") if e == 0 else mw2(b),
                                                  mixed_term(b, e), ALU.add)
                        if e < MIXED - 1:
                            last.then_inc(S["pool_step"], 1)
                            n_step += 1
                    last.then_inc(S["mix2_half"], 1)
                elif n == REC_VAR:
                    norm_rstd(REC, b, both=True)
                elif n == REC_IN:
                    pool.wait_ge(SB["ln_rstd"][b], REC + 1)
                    for i in range(NT):
                        last = pool.tensor_scalar(y[:, b, i, :], xs[:, b, i, :], meanvar[:, b, i, 0:1],
                                                  rstd[:, b, i:i + 1], ALU.subtract, ALU.mult)
                    last.then_inc(S["y_ready"], 1)
                elif n == DECAY:
                    pool.wait_ge(S["gates_sig"], 4 * b + 4)
                    pool.wait_ge(S["conv_done"], b + 1)
                    pool.tensor_scalar(rec[:, b], rec[:, b], 1.0, 1.0, ALU.add, ALU.mult).then_inc(S["sx_half"], 1)
                    pool.wait_ge(S["sx_half"], b + 1)
                    pool.tensor_tensor(rec[:, b], rec[:, b], xc[:, b], ALU.mult).then_inc(S["sx_done"], 1)
                elif n == INNER_SUM:
                    norm_rstd(RMS, b)
                    pool.wait_ge(S["hx_done"], b + 1)
                    pool.tensor_tensor(side[:, b], xs[:, b], y[:, b], ALU.add).then_inc(S["hx_side"], 1)
                elif n == XA2_VAR:
                    norm_rstd(XA2, b)
                    pool.wait_ge(S["p2_ready"], 1)
                    pool.wait_ge(SB["res_done"][b], 3)
                    for i in range(NT):
                        last = pool.tensor_tensor(side[:, b, i, :], xs[:, b, i, :], p2[:, b, :], ALU.add)
                    last.then_inc(S["p2_side"], 1)
                elif n == EXPERT_VAR:
                    norm_rstd(EXPERT, b)
                elif n == EXPERT_IN:
                    pool.wait_ge(SB["ln_norm"][b], NT * (EXPERT + 1))
                    for i in range(NT):
                        last = pool.tensor_tensor(y[:, b, i, :], xn(b, i), rows[:, 0:P], ALU.add)
                    last.then_inc(S["b2_side"], 1)
                    pool.wait_ge(SB["res_done"][b], 4)
                    for i in range(NT):
                        last = pool.tensor_tensor(side[:, b, i, :], xs[:, b, i, :], rows[:, 2 * P:3 * P], ALU.add)
                    last.then_inc(S["beta_side"], 1)
                elif n == LAST_VAR:
                    norm_rstd(LAST, b)

            for n, b in in_order(POOL_STEPS):
                pool_step(n, b)

        @block.scalar
        def _(act):
            act.wait_ge(S["attnw_loaded"], 16)
            act.activation(ident_b[:], wa("ident"), ACT.Copy).then_inc(S["act_const"], 1)
            for n in range(2):
                last = act.activation(mask_b[:, n, :], wa("mask"), ACT.Copy)
            last.then_inc(S["act_const"], 1)
            act.activation(ident_r[:], wa("ident"), ACT.Copy).then_inc(S["act_const"], 1)
            act.wait_ge(S["selw_loaded"], 16)
            for n in range(4):
                act.activation(sel_r[:, n, :, :],
                               probs[:, 0, n * NG * P:(n + 1) * NG * P].rearrange("p (g c) -> p g c", g=NG),
                               ACT.Copy).then_inc(S["act_const"], 1)

            def norm_piece(b, src):
                act.wait_ge(S["a_lnT_psum"], b + 1)
                act.activation(a_xT[:], bank(src), ACT.Copy).then_inc(S["a_lnT_ready"], 1)

            def q_piece(b, src):
                act.wait_ge(S["q_psum"], b + 1)
                act.activation(qk_hi[:, b, 0, :], bank(src), ACT.Copy).then_inc(S["q_hi"], 1)

            def k_piece(b, src):
                act.wait_ge(S["k_psum"], b + 1)
                act.activation(qk_hi[:, b, 1, :], bank(src), ACT.Copy).then_inc(S["k_hi"], 1)

            def v_piece(b, src):
                act.wait_ge(S["v_psum"], b + 1)
                act.activation(v_all[:], bank(src), ACT.Copy).then_inc(S["v_ready"], 1)

            def k_stack(G, g, src):
                act.wait_ge(S["kstack_psum"], G + 1)
                if not (isinstance(G, int) and G == 0):
                    act.wait_ge(S["kmask_ready"], G * HG)
                act.activation(kstack[:], bank(src), ACT.Identity, bias=wa("kone"))\
                   .then_inc(S["kstack_ready"], 1)

            def q_stack(G, g, src):
                act.wait_ge(S["qstack_psum"], G + 1)
                act.activation(qstack[:, g % 2, :], bank(src), ACT.Copy).then_inc(S["qstack_ready"], 1)

            def m_stack(G, g):
                act.wait_ge(S["m_psum"], G + 1)
                act.activation(mstack[:, g % 2, :], bank(6), ACT.Copy).then_inc(S["mstack_ready"], 1)

            norm_piece(0, 6)
            k_piece(0, 1)
            q_piece(0, 0)
            k_stack(0, 0, 3)
            q_stack(0, 0, 4)
            v_piece(0, 2)
            k_stack(1, 1, 6)
            q_stack(1, 1, 7)
            m_stack(0, 0)

            def forget_base_exp():
                act.wait_ge(S["restw_loaded"], 80)
                act.activation(decay[:, 0, :], wr("fb"), ACT.Abs).then_inc(S["act_const"], 1)
                act.wait_ge(S["act_const"], 8)
                act.activation(decay[:, 1, :], decay[:, 0, :], ACT.Exp, scale=-1.0).then_inc(S["act_const"], 1)

            def group(b, g, last=False):
                G = b * NG + g
                if last and g == NG - 2:
                    forget_base_exp()
                for u in range(NU):
                    act.wait_ge(S["e_psum"], G * NU + u + 1)
                    act.activation(probs[:, g % 2, u * UNIT:(u + 1) * UNIT].rearrange("p (a n) -> p a n", a=2),
                                   bank(2 * slot("keys", g, u), 2), ACT.Exp, scale=float(HS) ** -0.5)\
                       .then_inc(S["exp_done"], 1)
                    if not (last and g >= NG - 2):
                        if u == 0:
                            k_stack(G + 2, g, 6)
                        if u == 1:
                            q_stack(G + 2, g, 6)
                    if not last:
                        if (g, u) == (1, 1):
                            norm_piece(b + 1, 7)
                        if (g, u) == (1, 2):
                            q_piece(b + 1, 6)
                        if (g, u) == (1, 3):
                            k_piece(b + 1, 6)
                        if (g, u) == (2, 2):
                            v_piece(b + 1, 6)
                if not (last and g == NG - 1):
                    m_stack(G + 1, g + 1)
                act.wait_ge(S["av_psum"], G + 1)
                act.activation(av_sb[:], bank(7), ACT.Copy).then_inc(S["av_ready"], 1)

            group(0, 0)
            with act.Fori(0, B - 1) as b:
                for g in (1, 2, 3):
                    group(b, g)
                group(b + 1, 0)
            for g in (1, 2, 3):
                group(B - 1, g, last=True)

            def norm_T(k, b):
                act.wait_ge(SB["lnT_psum"][b], k + 1)
                act.activation(xT(b), bank(4 + b), ACT.Copy).then_inc(SB["lnT_ready"][b], 1)

            def scalar_step(n, b):
                if n >= T_OF:
                    norm_T(NORM_STEPS.index(n - T_OF), b)
                elif n == XA_IN:
                    act.wait_ge(S["xa_psum"], b + 1)
                    act.activation(gate_g[0:CTX, b, 0, :], ps[0:CTX, 4 + b, :], ACT.Gelu).then_inc(S["xa_gelu"], 1)
                elif n == FFN_IN:
                    act.wait_ge(S["gate_psum"], b + 1)
                    act.activation(hid[:, b, 0, :], bank(4 + b), ACT.Relu, bias=wr("gb1"),
                                   accum_out=hsum[:, b:b + 1]).then_inc(S["gate_sum"], 1)
                elif n == MIX:
                    act.wait_ge(S["g_ready"], b + 1)
                    for e in range(MIXED):
                        act.activation(mixed_term(b, e), tw2_sb[:, e, :], ACT.Copy, scale=gvec[:, b, e:e + 1])\
                           .then_inc(S["mixed_terms"], 1)
                elif n == HIDDEN:
                    act.wait_ge(S["mb1_done"], b + 1)
                    act.wait_ge(S["mix2_half"], b + 1)
                    for f in range(FC):
                        act.wait_ge(S["u_psum"], b * FC + f + 1)
                        act.activation(hid[:, b, f, :], bank(f % 2), ACT.Gelu_apprx_tanh, bias=mb1_c[:, b, f:f + 1])\
                           .then_inc(S["u_ready"], 1)
                elif n == REC_IN:
                    for c in range(HC):
                        act.wait_ge(S["z_psum"], 4 * b + c + 1)
                        act.activation(gate_g[:, b, c, :], bank(c), ACT.Gelu).then_inc(S["zg_gelu"], 1)
                    for c in range(HC):
                        act.wait_ge(S["z_psum"], 4 * b + 3 + c)
                        act.activation(xc[:, b, c, :], bank(2 + c), ACT.Identity, bias=wr("convb")[:, c:c + 1],
                                       scale=wr("convw")[:, c * KCONV + 3:c * KCONV + 4]).then_inc(S["conv0"], 1)
                elif n == GATES:
                    if b == 0:
                        act.wait_ge(S["dve_const"], REC_CONST)
                    for m in range(4):
                        act.wait_ge(S["gates_psum"], 4 * b + m + 1)
                        act.activation(hid[:, b, m, :], bank(m % 2), ACT.Tanh, scale=0.5,
                                       bias=hbg[:, m:m + 1]).then_inc(S["gates_sig"], 1)
                elif n == DECAY:
                    act.wait_ge(S["gates_sig"], 4 * b + 4)
                    for c in range(HC):
                        last = act.activation(alpha[:, b, c, :], alpha[:, b, c, :], ACT.Exp, scale=hdecay[:, c:c + 1],
                                              bias=hdecay[:, c:c + 1])
                    last.then_inc(S["alpha_done"], 1)
                    act.wait_ge(S["alpha_done"], b + 1)
                    act.activation(beta[:, b], alpha[:, b], ACT.Square).then_inc(S["alpha_sq"], 1)
                elif n == SCAN:
                    act.wait_ge(S["alpha_sq"], b + 1)
                    act.activation(beta[:, b], beta[:, b], ACT.Sqrt, scale=-0.25, bias=sqrt_bias[:])\
                       .then_inc(S["beta_done"], 1)
                elif n == GROW:
                    for c in range(HC):
                        act.wait_ge(S["grow_psum"], 4 * b + c + 1)
                        act.activation(gate_g[:, b, c, :], bank(c), ACT.Gelu).then_inc(S["mg_gelu"], 1)
                elif n == EXPERT_HIDDEN:
                    for f in range(FC):
                        act.wait_ge(S["h_psum"], b * FC + f + 1)
                        act.activation(hid[:, b, f, :], bank(f % 2), ACT.Relu, bias=wr("mb1")[:, f:f + 1])\
                           .then_inc(S["h_ready"], 1)

            for n, b in in_order(SCALAR_STEPS):
                scalar_step(n, b)

        @block.vector
        def _(dve):
            spare = dve.alloc_register("vector_spare")

            def own_wait(name, value):
                if isinstance(value, int):
                    dve.wait_ge(S[name], value)
                    return
                dve.reg_mov(spare, value)
                done = dve.snap(spare)
                dve.wait_ge(S["fold_copied"], 6)
                dve.wait_ge(S[name], done)

            def attention_stats(b):
                for i in range(NT):
                    last = dve.bn_stats(stats[:, b, i, :], xs[:, b, i, :])
                last.then_inc(S["a_stats_done"], 1)
                dve.wait_ge(S["a_stats_done"], b + 1)
                for i in range(NT):
                    last = dve.bn_aggr(meanvar[:, b, i, :], stats[:, b, i, :])
                last.then_inc(S["a_ln_var"], 1)

            def attention_norm(b):
                if not isinstance(b, int):
                    dve.wait_ge(S["a_lnT_psum"], b)
                else:
                    dve.wait_ge(S["a_ln_rstd"], b + 1)
                for i in range(NT):
                    dve.tensor_scalar(a_xn[:, i, :], xs[:, b, i, :], meanvar[:, b, i, 0:1], rstd[:, b, i:i + 1],
                                      ALU.subtract, ALU.mult).then_inc(S["a_ln_norm"], 1)

            def low_part(b, n, src):
                dve.wait_ge(S["qk"[n] + "_hi"], b + 1)
                dve.tensor_tensor(qk_lo[:, b, n, :], bank(src), qk_hi[:, b, n, :].bitcast(F32), ALU.subtract)\
                   .then_inc(S["qk"[n] + "_lo"], 1)

            def head_keys(G, g):
                dve.wait_ge(S["kstack_ready"], G + 1)
                if not (isinstance(G, int) and G < 2):
                    dve.wait_ge(S["e_psum"], (G - 1) * NU)
                for j in range(HG):
                    dve.tensor_scalar(km[:, (g % 2) * HG + j, :], kstack[:], wa("headcol")[:, j:j + 1],
                                      None, ALU.mult).then_inc(S["kmask_ready"], 1)

            def maxima(G, g, u, at):
                dve.wait_ge(S["s_psum"], G * NU + u + 1)
                s = bank(2 * at, 2)
                neg = negmax[:, g % 2, :, :].rearrange("p i (j r) -> p i j r", j=HG)
                if u < 2:
                    last = dve.tensor_reduce(neg[:, 3, 2 * u:2 * u + 2, 24], s, AX.X, ALU.max, negate=True)
                elif u < 4:
                    j = 2 * u - 4
                    dve.tensor_reduce(neg[:, 2, j:j + 2, 24], s[:, :, 0:384], AX.X, ALU.max, negate=True)
                    last = dve.tensor_reduce(neg[:, 0, j:j + 2, 24], s[:, :, 384:512], AX.X, ALU.max, negate=True)
                else:
                    last = dve.tensor_reduce(neg[:, 1, :, 24], s.rearrange("p a (h n) -> p (a h) n", h=2),
                                             AX.X, ALU.max, negate=True)
                last.then_inc(S["max_done"], 1)

            def divide(b, g):
                dve.wait_ge(S["avT_psum"], b * NG + g + 1)
                v = bank(7).rearrange("p (i j r) -> p (i j) r", i=NT, j=HG)
                dve.reciprocal(rden[:], v[:, :, HS]).then_inc(S["av_den"], 1)
                dve.wait_ge(S["av_den"], b * NG + g + 1)
                for i in range(NT):
                    last = dve.tensor_tensor(
                        y[:, b, i, g * HG * HS:(g + 1) * HG * HS].rearrange("p (j d) -> p j d", j=HG),
                        v[:, i * HG:(i + 1) * HG, 0:HS],
                        rden[:, i * HG:(i + 1) * HG].unsqueeze(2).broadcast_to([P, HG, HS]), ALU.mult)
                last.then_inc(S["av_norm"], 1)

            dve.wait_ge(S["x_loaded"], 16)
            attention_stats(0)
            for n, (dst, r) in enumerate(((fold_a, P), (wq_T, P), (fold_b, LAT), (fold_c, LAT), (wk_T, P), (wv_T, P))):
                dve.wait_ge(S["fold_psum"], n + 1)
                dve.tensor_copy(dst if n in (0, 2, 3) else dst[:], ps[0:r, n, 0:P]).then_inc(S["fold_copied"], 1)
            attention_norm(0)
            dve.wait_ge(S["xs_loaded"], 16 * (B - 1))
            dve.wait_ge(S["pool_const"], 6)
            low_part(0, 1, 1)
            low_part(0, 0, 0)
            dve.tensor_copy(flag[:], ones[:, 0:1]).then_inc(S["av_norm"], 1)
            head_keys(0, 0)
            for u in range(NU):
                maxima(0, 0, u, u % 3)
                if u == 1:
                    head_keys(1, 1)

            n_step = 0

            def step(ins):
                nonlocal n_step
                ins.then_inc(S["dve_step"], 1)
                n_step += 1

            def steps_done():
                dve.wait_ge(S["dve_step"], n_step)

            def y_tile(b, i):
                return y[:, b, i, :]

            def variance(b):
                for i in range(NT):
                    last = dve.bn_stats(stats[:, b, i, :], xs[:, b, i, :])
                step(last)
                steps_done()
                for i in range(NT):
                    last = dve.bn_aggr(meanvar[:, b, i, :], stats[:, b, i, :])
                last.then_inc(SB["ln_var"][b], 1)

            def normalise(k, b, dst=xn, scales=0):
                dve.wait_ge(SB["ln_rstd"][b], k + 1)
                for i in range(NT):
                    last = dve.tensor_scalar(dst(b, i), xs[:, b, i, :], meanvar[:, b, i, 0:1],
                                             rstd[:, b, scales + i:scales + i + 1], ALU.subtract, ALU.mult)
                    last.then_inc(SB["ln_norm"][b], 1)

            def residual(b, n, base):
                dve.wait_ge(SB["res_psum"][b], n)
                dve.tensor_tensor(xs[:, b], bank(4 + b).rearrange("p (i c) -> p i c", i=NT), base, ALU.add)\
                   .then_inc(SB["res_done"][b], 1)
                dve.wait_ge(SB["res_done"][b], n if n < 3 else n - 1)

            def later_weights():
                dve.wait_ge(S["restw_loaded"], 80)
                dve.wait_ge(S["act_const"], 9)
                n_const = 0

                def const(ins):
                    nonlocal n_const
                    ins.then_inc(S["dve_const"], 1)
                    n_const += 1
                    dve.wait_ge(S["dve_const"], n_const)

                e, d2, z, z2, acc = (decay[:, n, :] for n in (1, 2, 3, 4, 5))
                const(dve.tensor_scalar(d2, e, 2.0, None, ALU.add))
                const(dve.reciprocal(d2, d2))
                const(dve.tensor_tensor(z, e, d2, ALU.mult))
                const(dve.tensor_tensor(z2, z, z, ALU.mult))
                const(dve.tensor_scalar(acc, z2, 1.0 / 19, None, ALU.mult))
                for k in range(17, 1, -2):
                    const(dve.scalar_tensor_tensor(acc, acc, 1.0 / k, z2, ALU.add, ALU.mult))
                const(dve.scalar_tensor_tensor(acc, acc, 1.0, z, ALU.add, ALU.mult))
                const(dve.tensor_scalar(decay[:, 6, :], wr("fb"), 0.0, -4.0, ALU.max, ALU.mult))
                const(dve.tensor_scalar(hbg[:], wr("bg"), 0.5, None, ALU.mult))
                const(dve.scalar_tensor_tensor(hdecay[:], acc, -8.0, decay[:, 6, :], ALU.mult, ALU.add))
                const(dve.tensor_scalar(wr("winT"), wr("winT"), wr("gamma1"), None, ALU.mult))
                const(dve.tensor_scalar(wr("growT"), wr("growT"), wr("gamma2"), None, ALU.mult))
                assert n_const == REC_CONST, n_const

            def context_sums():
                dve.wait_ge(S["ctx_loaded"], 32)
                step(dve.tensor_reduce(csum[:], ctxT_sb[:], AX.X, ALU.add))
                steps_done()
                for b in range(B):
                    last = dve.tensor_scalar(csum_b[:, b, :], ones[:], csum[:, b:b + 1], 1.0 / CTX, ALU.mult, ALU.mult)
                last.then_inc(S["csum_ready"], 1)

            def attention_variance(b):
                own_wait("att_sum", b + 1)
                for i in range(NT):
                    last = dve.bn_stats(a_stats[:, i, :], xs[:, b, i, :])
                last.then_inc(S["att_stats"], 1)
                own_wait("att_stats", b + 1)
                for i in range(NT):
                    last = dve.bn_aggr(sum_meanvar[:, i, :], a_stats[:, i, :])
                last.then_inc(S["att_aggr"], 1)
                dve.wait_ge(S["att_aggr"], b + 1)
                dve.tensor_copy(meanvar[:, b], sum_meanvar[:]).then_inc(S["att_var"], 1)

            def group(b, g, last=False):
                G = b * NG + g
                for u in range(NU):
                    if not (last and g == NG - 1):
                        maxima(G + 1, g + 1, u, slot("queries", g, u))
                    if g > 0 and u == 1:
                        divide(b, g - 1)
                    if g == 0 and u == 1 and not (isinstance(b, int) and b == 0):
                        divide(b - 1, NG - 1)
                    if g == 0 and u == 4 and not (isinstance(b, int) and b == 0):
                        attention_variance(b - 1)
                    if last and g == NG - 1 and u == 1:
                        later_weights()
                        context_sums()
                        for early in range(B - 1):
                            normalise(XA, early, dst=y_tile)
                    if not last:
                        if g == 0 and isinstance(b, int):
                            if u < B - 1:
                                attention_stats(u + 1)
                            if u == NU - 1:
                                dve.wait_ge(S["a_ln_rstd"], B)
                        if (g, u) == (1, 0):
                            attention_norm(b + 1)
                        if (g, u) == (1, 3):
                            low_part(b + 1, 0, 6)
                        if (g, u) == (1, 4):
                            low_part(b + 1, 1, 6)
                if not (last and g >= NG - 2):
                    head_keys(G + 2, g)

            group(0, 0)
            with dve.Fori(0, B - 1) as b:
                for g in (1, 2, 3):
                    group(b, g)
                group(b + 1, 0)
            for g in (1, 2, 3):
                group(B - 1, g, last=True)
            divide(B - 1, NG - 1)
            attention_variance(B - 1)

            tb1 = wr("Tb1").rearrange("p (f e) -> p f e", f=FC)
            dve.wait_ge(S["pool_const"], 7)

            def gate_vector(b):
                dve.wait_ge(S["g_psum"], b + 1)
                dve.tensor_tensor(gvec[:, b, :], ps[:, 4 + b, 0:NE], gb2_sb[:], ALU.add)
                dve.tensor_scalar(g9[0:NE, b, :], ps[0:NE, 4 + b, P:2 * P], wr("gb2"), None, ALU.add)\
                   .then_inc(S["g_ready"], 1)

            def mixed_bias(b):
                dve.wait_ge(S["g_ready"], b + 1)
                for f in range(FC):
                    last = dve.tensor_tensor(mb1_t[:, b, f, :], tb1[:, f, :], gvec[:, b, :], ALU.mult)
                step(last)
                steps_done()
                step(dve.tensor_reduce(mb1_s[:, b, :], mb1_t[:, b], AX.X, ALU.add))
                steps_done()
                dve.tensor_tensor(mb1_c[:, b, :], mb1_s[:, b, :], wr("b1"), ALU.add).then_inc(S["mb1_done"], 1)

            def mix_first(b):
                for e in range(NE):
                    last = dve.scalar_tensor_tensor(mw1(b), tw1_sb[:, e, :], gvec[:, b, e:e + 1],
                                                    wr("W1T") if e == 0 else mw1(b), ALU.mult, ALU.add)
                    if e < NE - 1:
                        step(last)
                        steps_done()
                last.then_inc(S["mix1_done"], 1)

            def mix_second(b):
                dve.wait_ge(S["mix2_half"], b + 1)
                for e in range(MIXED, NE):
                    last = dve.scalar_tensor_tensor(mw2(b), tw2_sb[:, e, :], gvec[:, b, e:e + 1],
                                                    mw2(b), ALU.mult, ALU.add)
                    if e < NE - 1:
                        step(last)
                        steps_done()
                last.then_inc(S["mix2_done"], 1)

            def convolve(b):
                for c in range(HC):
                    dve.wait_ge(S["conv0"], HC * b + c + 1)
                    for k in range(1, KCONV):
                        last = dve.scalar_tensor_tensor(
                            xc[:, b, c, k:T], ps[:, 2 + c, 0:T - k],
                            wr("convw")[:, c * KCONV + 3 - k:c * KCONV + 4 - k], xc[:, b, c, k:T],
                            ALU.mult, ALU.add)
                        if k < KCONV - 1 or c < HC - 1:
                            step(last)
                            steps_done()
                last.then_inc(S["conv_done"], 1)

            def recurrence(b):
                dve.wait_ge(S["sx_done"], b + 1)
                dve.wait_ge(S["beta_done"], b + 1)
                step(dve.tensor_tensor(xc[:, b], rec[:, b], beta[:, b], ALU.mult))
                steps_done()
                for c in range(HC):
                    last = dve.tensor_tensor_scan(rec[:, b, c, :], alpha[:, b, c, :], xc[:, b, c, :],
                                                  0.0, ALU.mult, ALU.add)
                step(last)
                steps_done()
                dve.tensor_tensor(rec[:, b], rec[:, b], gate_g[:, b], ALU.mult)\
                   .then_inc(S["hm_done"], 1)

            def inner_sum(b):
                dve.wait_ge(SB["res_psum"][b], 3)
                dve.wait_ge(S["y_ready"], b + 1)
                dve.tensor_tensor(y[:, b], bank(4 + b).rearrange("p (i c) -> p i c", i=NT), y[:, b], ALU.add)\
                   .then_inc(S["hx_done"], 1)
                dve.wait_ge(S["hx_done"], b + 1)
                for i in range(NT):
                    last = dve.scalar_tensor_tensor(xn(b, i), y[:, b, i, :], 1.0, y[:, b, i, :],
                                                    ALU.mult, ALU.mult, accum_out=sumsq[:, b, i:i + 1])
                last.then_inc(SB["ln_var"][b], 1)

            def scaled(b):
                dve.wait_ge(SB["ln_rstd"][b], RMS + 1)
                for i in range(NT):
                    dve.tensor_scalar(xn(b, i), y[:, b, i, :], rstd[:, b, i:i + 1], None, ALU.mult)\
                       .then_inc(SB["ln_norm"][b], 1)

            def vector_step(n, b):
                if n == XA_IN:
                    if b == B - 1:
                        normalise(XA, b, dst=y_tile)
                    if b == 0:
                        dve.wait_ge(S["p2_psum"], 1)
                        dve.tensor_copy(p2[:].rearrange("p b c -> p (b c)"), bank(2)).then_inc(S["p2_ready"], 1)
                elif n == XA_OUT:
                    dve.wait_ge(S["xa_gelu"], b + 1)
                    dve.tensor_tensor(xc[0:CTX, b, 0, :], ps[0:CTX, 4 + b, :], gate_g[0:CTX, b, 0, :],
                                      ALU.mult).then_inc(S["xa_prod"], 1)
                elif n == FFN_VAR:
                    residual(b, 1, xs[:, b])
                    variance(b)
                elif n == FFN_IN:
                    normalise(FFN, b)
                elif n == GATE_MEAN:
                    dve.wait_ge(S["gate_sum"], b + 1)
                    dve.tensor_scalar(hsum_b[:, b, :], ones[:], hsum[:, b:b + 1], 1.0 / T, ALU.mult, ALU.mult)\
                       .then_inc(S["gate_bcast"], 1)
                elif n == MIX:
                    gate_vector(b)
                    mixed_bias(b)
                    mix_first(b)
                elif n == HIDDEN:
                    mix_second(b)
                elif n == REC_VAR:
                    residual(b, 2, xs[:, b])
                    variance(b)
                elif n == REC_IN:
                    normalise(REC, b, scales=NT)
                elif n == GATES:
                    convolve(b)
                elif n == SCAN:
                    recurrence(b)
                elif n == INNER_SUM:
                    inner_sum(b)
                elif n == GROW:
                    scaled(b)
                elif n == SHRINK:
                    dve.wait_ge(S["mg_gelu"], HC * (b + 1))
                    dve.wait_ge(S["grow_psum"], 4 * b + 4)
                    dve.tensor_tensor(rec[:, b], bank(2, 2), gate_g[:, b], ALU.mult).then_inc(S["mm_done"], 1)
                elif n == XA2_VAR:
                    dve.wait_ge(S["hx_side"], b + 1)
                    residual(b, 4, side[:, b])
                    variance(b)
                elif n == XA2_OUT:
                    normalise(XA2, b)
                elif n == EXPERT_VAR:
                    dve.wait_ge(S["p2_side"], b + 1)
                    residual(b, 5, side[:, b])
                    variance(b)
                elif n == EXPERT_IN:
                    normalise(EXPERT, b)
                elif n == LAST_VAR:
                    dve.wait_ge(S["b2_side"], b + 1)
                    dve.wait_ge(S["beta_side"], b + 1)
                    residual(b, 6, y[:, b])
                    variance(b)
                elif n == LAST_OUT:
                    dve.wait_ge(SB["ln_var"][b], LAST)
                    for i in range(NT):
                        last = dve.scalar_tensor_tensor(xn(b, i), xs[:, b, i, :], meanvar[:, b, i, 0:1],
                                                        rows[:, P:2 * P], ALU.subtract, ALU.mult)
                    last.then_inc(S["gain_done"], 1)
                    dve.wait_ge(S["gain_done"], b + 1)
                    dve.wait_ge(SB["ln_rstd"][b], LAST + 1)
                    for i in range(NT):
                        last = dve.scalar_tensor_tensor(xn(b, i), xn(b, i), rstd[:, b, i:i + 1], side[:, b, i, :],
                                                        ALU.mult, ALU.add)
                    last.then_inc(S["out_ready"], 1)

            for n, b in in_order(VECTOR_STEPS):
                vector_step(n, b)

        @block.tensor
        def _(pe):
            def keep_warm(n):
                for _ in range(n):
                    pe.matmul(bank(7)[:, 0:P], ones[:], ones[:], start=True, stop=True)

            pe.wait_ge(S["pool_const"], 1)
            keep_warm(9)
            pe.wait_ge(S["attnw_loaded"], 16)

            def fold(n, lhsT, rhs, r, after):
                if after:
                    keep_warm(1)
                    pe.wait_ge(S["fold_copied"], after)
                pe.matmul(ps[0:r, n, 0:P], lhsT, rhs, start=True, stop=True).then_inc(S["fold_psum"], 1)

            fold(0, wa("wuqT"), wa("wdq"), P, 0)
            fold(1, wa("wdq"), wa("wuqT"), P, 0)
            fold(2, wa("wuk"), fold_a, LAT, 1)
            fold(3, wa("wuv"), wa("woT"), LAT, 0)
            fold(4, wa("wdkv"), fold_b, P, 3)
            fold(5, wa("wdkv"), fold_c, P, 4)

            def norm_piece(b, dst):
                for i in range(NT):
                    pe.wait_ge(S["a_ln_norm"], b * NT + i + 1)
                    last = pe.transpose(bank(dst)[:, i * P:(i + 1) * P], a_xn[:, i, :], wa("ident"))
                last.then_inc(S["a_lnT_psum"], 1)

            def q_piece(b, dst):
                pe.wait_ge(S["a_lnT_ready"], b + 1)
                pe.matmul(bank(dst), wq_T[:], a_xT[:], start=True, stop=True).then_inc(S["q_psum"], 1)

            def k_piece(b, dst):
                pe.matmul(bank(dst), wk_T[:], a_xT[:], start=True, stop=True).then_inc(S["k_psum"], 1)

            def v_piece(b, dst):
                for i in range(NT):
                    last = pe.matmul(bank(dst)[:, i * P:(i + 1) * P], a_xT[:, i * P:(i + 1) * P], wv_T[:],
                                     start=True, stop=True)
                last.then_inc(S["v_psum"], 1)

            def k_stack(b, g, dst):
                pe.wait_ge(S["k_lo"], b + 1)
                pe.matmul(bank(dst), sel_r[:, 2, g, :], qk_hi[:, b, 1, :], start=True, stop=False)
                pe.matmul(bank(dst), sel_r[:, 3, g, :], qk_lo[:, b, 1, :], start=False, stop=True)\
                  .then_inc(S["kstack_psum"], 1)

            def q_stack(b, g, dst):
                pe.matmul(bank(dst), sel_r[:, 0, g, :], qk_hi[:, b, 0, :], start=True, stop=False)
                pe.matmul(bank(dst), sel_r[:, 1, g, :], qk_lo[:, b, 0, :], start=False, stop=True)\
                  .then_inc(S["qstack_psum"], 1)

            def s_unit(G, g, u, at):
                s = bank(2 * at, 2).rearrange("p a n -> p (a n)")
                parts = segments(u)
                for at_bank in (0, 1):
                    here = [(j, rank, c, w) for j, rank, c, w in parts if c // 512 == at_bank]
                    for j, rank, c, w in here:
                        i = NT - 1 - rank
                        if u < 2:
                            pe.wait_ge(S["kmask_ready"], G * HG + j + 1)
                        pe.matmul(s[:, c:c + w], qstack[:, g % 2, i * P:(i + 1) * P], km[:, (g % 2) * HG + j, 0:w],
                                  start=(c % 512 == 0), stop=False)
                    ends = [c + w - P for j, rank, c, w in here]
                    if len(ends) == 1:
                        last = pe.matmul(s[:, ends[0]:ends[0] + P], ident_b[:], mask_b[:, 0, :],
                                         start=False, stop=True)
                    else:
                        row = s[:, 512 * at_bank:512 * (at_bank + 1)]
                        both = row[:, 2 * P:] if here[0][3] == 3 * P else row
                        both = both.rearrange("p (a n) -> p a n", a=2)[:, :, -P:]
                        last = pe.matmul(both, ident_b[:], mask_b[:], start=False, stop=True)
                last.then_inc(S["s_psum"], 1)

            def t_unit(g, u, at):
                s = bank(2 * at, 2).rearrange("p a n -> p (a n)")
                for j, i, c, w in segments(u):
                    last = pe.matmul(s[:, c:c + w], km[:, (g % 2) * HG + j, i * P:(i + 1) * P],
                                     mstack[:, g % 2, T - w:T], start=True, stop=True)
                last.then_inc(S["e_psum"], 1)

            def max_rows(b, g, G):
                pe.wait_ge(S["max_done"], (G + 1) * NU)
                pe.matmul(bank(6), ident_r[:], qstack[:, g % 2, :], start=True, stop=False)
                for i in range(NT):
                    last = pe.matmul(bank(6)[:, i * P:(i + 1) * P], negmax[:, g % 2, i, :], ident_r[:],
                                     start=False, stop=(i == NT - 1))
                last.then_inc(S["m_psum"], 1)

            VALUE_TILES = ((0, (0, 1)), (1, (2, 3)), (3, (2, 3)), (2, (4,)))

            def values(g, G, tiles):
                g = g % NG
                if tiles[0][0] == 0:
                    pe.wait_ge(S["av_norm"], G + 1)
                for i, units in tiles:
                    pe.wait_ge(S["sel_done"], G * NU + units[-1] + 1)
                    for j in range(HG):
                        u, c, w = next((u, c, w) for u in units for jj, r, c, w in segments(u) if jj == j and r == i)
                        last = pe.matmul(ps[j * VW:(j + 1) * VW, 7, T - w:T], vx[:, i, g * HG + j, :],
                                         probs[:, g % 2, u * UNIT + c:u * UNIT + c + w],
                                         start=(i == 0), stop=(i == 2), tile_position=(0, j * VW))
                return last

            def tokens_first(G):
                pe.wait_ge(S["av_ready"], G + 1)
                for i in range(NT):
                    last = pe.transpose(bank(7)[:, i * P:(i + 1) * P], av_sb[:, i * P:(i + 1) * P], wa("ident"))
                last.then_inc(S["avT_psum"], 1)

            keep_warm(1)
            norm_piece(0, 6)
            keep_warm(3)
            pe.wait_ge(S["fold_copied"], 6)
            pe.wait_ge(S["a_lnT_ready"], 1)
            k_piece(0, 1)
            q_piece(0, 0)
            pe.wait_ge(S["act_const"], 7)
            k_stack(0, 0, 3)
            pe.wait_ge(S["q_lo"], 1)
            q_stack(0, 0, 4)
            v_piece(0, 2)
            pe.wait_ge(S["qstack_ready"], 1)
            s_unit(0, 0, 0, 0)
            k_stack(0, 1, 6)
            pe.wait_ge(S["v_ready"], 1)
            s_unit(0, 0, 1, 1)
            q_stack(0, 1, 7)
            s_unit(0, 0, 2, 2)
            for u in range(3, NU):
                pe.wait_ge(S["max_done"], u - 2)
                s_unit(0, 0, u, u % 3)
            pe.wait_ge(S["kstack_ready"], 2)
            max_rows(0, 0, 0)

            def group(b, g, last=False):
                G = b * NG + g
                nb, ng = (b, g + 1) if g + 1 < NG else (b + 1, 0)
                ab, ag = (b, g + 2) if g + 2 < NG else (b + 1, g + 2 - NG)
                has_next = not (last and g == NG - 1)
                has_after = not (last and g >= NG - 2)
                if has_next:
                    pe.wait_ge(S["qstack_ready"], G + 2)
                for turn, (kind, u) in enumerate(TURNS):
                    n = g * len(TURNS) + turn
                    before, used = divmod(n - 3, len(TURNS))
                    if turn == 1 and not (g == 0 and isinstance(b, int) and b == 0):
                        values(g - 1, G - 1, VALUE_TILES[3:]).then_inc(S["av_psum"], 1)
                    if not has_next and kind == "queries":
                        continue
                    if not has_next and u > 0:
                        if u >= 3:
                            pe.wait_ge(S["exp_done"], G * NU + (1 if u == 3 else 3))
                    elif n < 3:
                        pe.wait_ge(S["max_done"], (G + 1) * NU)
                        if not isinstance(b, int):
                            pe.wait_ge(S["exp_done"], G * NU)
                    elif TURNS[used][0] == "queries":
                        pe.wait_ge(S["max_done"], (b * NG + before + 1) * NU + TURNS[used][1] + 1)
                    else:
                        pe.wait_ge(S["exp_done"], (b * NG + before) * NU + TURNS[used][1] + 1)
                    if kind == "queries":
                        s_unit(G + 1, g + 1, u, slot(kind, g, u))
                    else:
                        if u == 0:
                            if not (g == 0 and isinstance(b, int) and b == 0):
                                tokens_first(G - 1)
                            pe.wait_ge(S["mstack_ready"], G + 1)
                        t_unit(g, u, slot(kind, g, u))
                    if kind == "queries":
                        continue
                    if has_after and u == 0:
                        k_stack(ab, ag, 6)
                    if has_after and u == 1:
                        pe.wait_ge(S["kstack_ready"], G + 3)
                        q_stack(ab, ag, 6)
                    if not last:
                        if (g, u) == (1, 1):
                            pe.wait_ge(S["av_norm"], G + 1)
                            norm_piece(b + 1, 7)
                        if (g, u) == (1, 2):
                            pe.wait_ge(S["qstack_ready"], G + 3)
                            q_piece(b + 1, 6)
                        if (g, u) == (1, 3):
                            pe.wait_ge(S["q_lo"], b + 2)
                            k_piece(b + 1, 6)
                        if (g, u) == (2, 2):
                            pe.wait_ge(S["qstack_ready"], G + 3)
                            v_piece(b + 1, 6)
                if g == 0:
                    pe.wait_ge(S["vx_ready"], b + 1)
                values(g, G, VALUE_TILES[:1])
                if has_next:
                    if has_after:
                        pe.wait_ge(S["qstack_ready"], G + 3)
                    if not last and g == 1:
                        pe.wait_ge(S["k_lo"], b + 2)
                    if not last and g == 2:
                        pe.wait_ge(S["v_ready"], b + 2)
                    max_rows(nb, ng, G + 1)
                values(g, G, VALUE_TILES[1:3])

            group(0, 0)
            with pe.Fori(0, B - 1) as b:
                for g in (1, 2, 3):
                    group(b, g)
                group(b + 1, 0)
            for g in (1, 2, 3):
                group(B - 1, g, last=True)
            values(NG - 1, B * NG - 1, VALUE_TILES[3:]).then_inc(S["av_psum"], 1)
            tokens_first(B * NG - 1)

            read = {}

            def wide(n, *products):
                if n in read:
                    pe.wait_ge(*read[n])
                for m, (lhsT, rhs) in enumerate(products):
                    last = pe.matmul(bank(n), lhsT, rhs, start=(m == 0), stop=(m == len(products) - 1))
                return last

            def norm_T(k, b):
                for i in range(NT):
                    pe.wait_ge(SB["ln_norm"][b], k * NT + i + 1)
                    last = pe.transpose(bank(4 + b)[:, i * P:(i + 1) * P], y[:, b, i, :] if k == XA else xn(b, i),
                                        wa("ident"))
                last.then_inc(SB["lnT_psum"][b], 1)

            def natural(b, terms):
                for i in range(NT):
                    these = terms(slice(i * P, (i + 1) * P))
                    for m, (lhsT, rhs) in enumerate(these):
                        last = pe.matmul(bank(4 + b)[:, i * P:(i + 1) * P], lhsT, rhs,
                                         start=(m == 0), stop=(m == len(these) - 1))
                last.then_inc(SB["res_psum"][b], 1)

            pe.wait_ge(S["csum_ready"], 1)
            for b in range(B):
                pe.matmul(bank(2)[:, b * P:(b + 1) * P], csum_b[:, b, :], wr("x2T"), start=True, stop=False)
                last = pe.matmul(bank(2)[:, b * P:(b + 1) * P], ones[0:1, :], wr("xb"), start=False, stop=True)
            last.then_inc(S["p2_psum"], 1)
            read[2] = (S["p2_ready"], 1)
            wg = wr("wgT").rearrange("p (c n) -> p c n", c=HC)

            def tensor_step(n, b):
                if n >= T_OF:
                    norm_T(NORM_STEPS.index(n - T_OF), b)
                    return
                if n in NORM_STEPS:
                    pe.wait_ge(SB["lnT_ready"][b], NORM_STEPS.index(n) + 1)
                if n == XA_OUT:
                    pe.wait_ge(S["xa_prod"], b + 1)
                    natural(b, lambda t: [(xc[0:CTX, b, 0, t], ctxn_sb[:, b, :])])
                elif n == GATE_MEAN:
                    pe.wait_ge(S["gate_bcast"], b + 1)
                    pe.matmul(ps[:, 4 + b, 0:NE], hsum_b[:, b, :], wr("gw2T"), start=True, stop=True)
                    pe.matmul(ps[0:NE, 4 + b, P:2 * P], wr("gw2T"), hsum_b[:, b, :], start=True, stop=True)\
                      .then_inc(S["g_psum"], 1)
                elif n == FFN_OUT:
                    pe.wait_ge(S["mix2_done"], b + 1)
                    pe.wait_ge(S["u_ready"], FC * (b + 1))
                    natural(b, lambda t: [(hid[:, b, f, t], mw2(b)[:, f * P:(f + 1) * P])
                                          for f in range(FC)] + [(g9[:, b, :], wr("tb2x"))])
                elif n == SCAN:
                    pe.wait_ge(S["hm_done"], b + 1)
                    natural(b, lambda t: [(rec[:, b, c, t], wr("woutT")[:, c * P:(c + 1) * P]) for c in range(HC)])
                elif n == SHRINK:
                    pe.wait_ge(S["mm_done"], b + 1)
                    natural(b, lambda t: [(rec[:, b, c, t], wr("shrinkT")[:, c * P:(c + 1) * P])
                                          for c in range(HC)])
                elif n == XA_IN:
                    pe.matmul(ps[0:CTX, 4 + b, :], ctxT_sb[:, b, :], xT(b), start=True, stop=True)\
                      .then_inc(S["xa_psum"], 1)
                elif n == FFN_IN:
                    pe.matmul(bank(4 + b), wr("gw1T"), xT(b), start=True, stop=True).then_inc(S["gate_psum"], 1)
                elif n == HIDDEN:
                    pe.wait_ge(S["mix1_done"], b + 1)
                    for f in range(FC):
                        wide(f % 2, (mw1(b)[:, f * P:(f + 1) * P], xT(b))).then_inc(S["u_psum"], 1)
                        read[f % 2] = (S["u_ready"], FC * b + f + 1)
                elif n == REC_IN:
                    for m in range(4):
                        wide(m, (wr("winT")[:, m * P:(m + 1) * P], xT(b))).then_inc(S["z_psum"], 1)
                        read[m] = (S["zg_gelu"], HC * b + m + 1) if m < HC else (S["conv_done"], b + 1)
                elif n == GATES:
                    pe.wait_ge(S["conv_done"], b + 1)
                    for m in range(4):
                        wide(m % 2, *[(wg[:, c, m * P:(m + 1) * P], xc[:, b, c, :]) for c in range(HC)])\
                            .then_inc(S["gates_psum"], 1)
                        read[m % 2] = (S["gates_sig"], 4 * b + m + 1)
                elif n == GROW:
                    for m in range(4):
                        wide(m, (wr("growT")[:, m * P:(m + 1) * P], xT(b))).then_inc(S["grow_psum"], 1)
                        read[m] = (S["mg_gelu"], HC * b + m + 1) if m < HC else (S["mm_done"], b + 1)
                elif n == XA2_OUT:
                    natural(b, lambda t: [(xT(b)[:, t], wr("x1T"))])
                elif n == EXPERT_HIDDEN:
                    pe.wait_ge(SB["lnT_ready"][b], EXPERT + 1)
                    for f in range(FC):
                        wide(f % 2, (wr("m1")[:, f * P:(f + 1) * P], xT(b))).then_inc(S["h_psum"], 1)
                        read[f % 2] = (S["h_ready"], FC * b + f + 1)
                elif n == LAST_VAR:
                    pe.wait_ge(S["h_ready"], FC * (b + 1))
                    natural(b, lambda t: [(hid[:, b, f, t], wr("m2")[:, f * P:(f + 1) * P])
                                          for f in range(FC)])

            for n, b in in_order(TENSOR_STEPS):
                tensor_step(n, b)


REC_CONST = 19
(SUM, XA_IN, XA_OUT, FFN_VAR, FFN_IN, GATE_MEAN, MIX, HIDDEN, FFN_OUT, REC_VAR, REC_IN, GATES, DECAY, SCAN, INNER_SUM,
 GROW, SHRINK, XA2_VAR, XA2_OUT, EXPERT_VAR, EXPERT_IN, EXPERT_HIDDEN, LAST_VAR, LAST_OUT) = range(24)
T_OF = 100
NORM_STEPS = (XA_IN, FFN_IN, REC_IN, GROW, XA2_OUT, EXPERT_IN)
MIXED = 6
LAGS = (0, 5.8, 11.8, 18.2)
POOL_STEPS = {SUM: 0, FFN_VAR: 21.3, MIX: 28.8, REC_VAR: 41.6, REC_IN: 48.1, DECAY: 67.1, INNER_SUM: 79.6,
              XA2_VAR: 95.8, EXPERT_VAR: 102.7, EXPERT_IN: 115.2, LAST_VAR: 124.6}
VECTOR_STEPS = {XA_IN: 7.3, XA_OUT: 19.6, FFN_VAR: 19.6, FFN_IN: 20.8, GATE_MEAN: 26.3, MIX: 27.1, HIDDEN: 34,
                REC_VAR: 42.6, REC_IN: 46.1, GATES: 59, SCAN: 75, INNER_SUM: 80.4, GROW: 81.3, SHRINK: 89.2,
                XA2_VAR: 93.1, XA2_OUT: 96.2, EXPERT_VAR: 102.3, EXPERT_IN: 102.9, LAST_VAR: 122.3,
                LAST_OUT: 124}
SCALAR_STEPS = {T_OF + XA_IN: 13.3, XA_IN: 14.7, T_OF + FFN_IN: 22.8, FFN_IN: 24.8, MIX: 27.5, HIDDEN: 35,
                T_OF + REC_IN: 50, REC_IN: 52.6, GATES: 62.3, DECAY: 70.1, SCAN: 73.3, T_OF + GROW: 83.6,
                GROW: 86.3, T_OF + XA2_OUT: 99.2, T_OF + EXPERT_IN: 107, EXPERT_HIDDEN: 109.1}
TENSOR_STEPS = {T_OF + XA_IN: 12.5, XA_IN: 14.5, XA_OUT: 17, T_OF + FFN_IN: 21.9, FFN_IN: 23.8, GATE_MEAN: 25.1,
                HIDDEN: 33.9, FFN_OUT: 38.4, T_OF + REC_IN: 48.3, REC_IN: 51, GATES: 60.8, SCAN: 76.1,
                T_OF + GROW: 82.8, GROW: 84.9, SHRINK: 90.3, T_OF + XA2_OUT: 97.1, XA2_OUT: 99.8,
                T_OF + EXPERT_IN: 104.3, EXPERT_HIDDEN: 107, LAST_VAR: 113.3}


def kernel(**inputs):
    import numpy as _np
    import concourse.bacc as _bacc
    from concourse.bass_utils import run_bass_kernel_spmd as _run

    a = {k: _np.asarray(v) for k, v in inputs.items()}

    def chunked(w):
        n = w.shape[0] // P
        return w.reshape(n, P, w.shape[1]).transpose(1, 0, 2).reshape(P, -1)

    def per_chunk(v):
        return v.reshape(-1, P).T

    part = {"selqh": (0, 2), "selql": (1,), "selkh": (0, 1), "selkl": (2,)}
    sel = {n: _np.zeros((P, NG, HG, 4, HS), _np.float32) for n in part}
    for n, places in part.items():
        for h in range(NH):
            for d in range(HS):
                for pl in places:
                    sel[n][h * HS + d, h // HG, h % HG, pl, d] = 1.0
    row = _np.arange(P)
    attn = {
        "wdq": a["L0_attn_W_dq"], "wuqT": a["L0_attn_W_uq"].T, "wdkv": a["L0_attn_W_dkv"],
        "wuk": a["L0_attn_W_uk"], "wuv": a["L0_attn_W_uv"], "woT": a["L0_attn_W_o"].T,
        "ident": _np.eye(P, dtype=_np.float32),
        "mask": _np.where(row[None, :] > row[:, None], NEG, 0.0).astype(_np.float32),
        "kone": (row % 32 == 24).astype(_np.float32)[:, None],
        "headcol": (row[:, None] // 32 == _np.arange(HG)[None, :]).astype(_np.float32),
    }
    rest = {
        "gw1T": a["L0_ffn_gate_w1"].T, "gb1": a["L0_ffn_gate_b1"][:, None], "gw2T": a["L0_ffn_gate_w2"].T,
        "gb2": a["L0_ffn_gate_b2"][:, None], "W1T": a["L0_ffn_W1"].T, "b1": per_chunk(a["L0_ffn_b1"]),
        "W2T": chunked(a["L0_ffn_W2"].T),
        "tb2x": _np.concatenate([a["L0_ffn_Tb2"], a["L0_ffn_b2"][None]], 0),
        "Tb1": a["L0_ffn_Tb1"].reshape(NE, FC, P).transpose(2, 1, 0).reshape(P, -1),
        "winT": a["L1_attn_W_in"].T, "gamma1": a["L1_attn_gamma1"][:, None],
        "convw": a["L1_attn_conv_w"].reshape(HC, P, KCONV).transpose(1, 0, 2).reshape(P, -1),
        "convb": per_chunk(a["L1_attn_conv_b"]), "wgT": chunked(a["L1_attn_W_gates"].T),
        "bg": per_chunk(a["L1_attn_b_gates"]), "fb": per_chunk(a["L1_attn_forget_base"]),
        "woutT": chunked(a["L1_attn_W_out"].T), "gamma2": a["L1_attn_gamma2"][:, None],
        "growT": a["L1_attn_W_grow"].T, "shrinkT": chunked(a["L1_attn_W_shrink"].T),
        "x1T": a["L1_xattn_W"][:, :P].T, "x2T": a["L1_xattn_W"][:, P:].T, "xb": a["L1_xattn_b"][None],
        "m1": a["L1_ffn_w1"][0], "mb1": per_chunk(a["L1_ffn_b1"][0]), "m2": chunked(a["L1_ffn_w2"][0]),
    }

    def packed(parts, at, width, values):
        m = _np.zeros((P, width), _np.float32)
        for name, r, w in parts:
            c = at[name][0]
            assert values[name].shape == (r, w), (name, values[name].shape)
            m[0:r, c:c + w] = values[name]
        return m

    arrays = {
        "x": a["x"], "ctxn": _np.ascontiguousarray(a["ctx_1024"].transpose(1, 0, 2)),
        "ctxT": _np.ascontiguousarray(a["ctx_1024"].transpose(2, 0, 1)),
        "attnw": packed(ATTN_PARTS, ATTN_AT, ATTN_W, attn),
        "selw": _np.concatenate([sel[n].reshape(P, -1) for n in SELECTIONS], 1),
        "restw": packed(REST_PARTS, REST_AT, REST_W, rest),
        "rowsw": _np.concatenate([a["L1_ffn_b2"][0], a["L1_ffn_gamma"], a["L1_ffn_beta"]])[None],
        "tw1": _np.ascontiguousarray(a["L0_ffn_TW1"].transpose(2, 0, 1)),
        "tw2": _np.ascontiguousarray(a["L0_ffn_TW2"].reshape(NE, P, FC, P).transpose(3, 0, 2, 1).reshape(P, NE, -1)),
        "gb2row": a["L0_ffn_gate_b2"][None],
    }
    nc = _bacc.Bacc("TRN2", target_bir_lowering=False, num_devices=1)
    args, sent = [], {}
    for name, v in arrays.items():
        v = _np.ascontiguousarray(v)
        sent["in_" + name] = v
        args.append(nc.dram_tensor("in_" + name, v.shape, mybir.dt.from_np(v.dtype), kind="ExternalInput").ap())
    args.append(nc.dram_tensor("out_0", (B, T, P), F32, kind="ExternalOutput").ap())
    decoder_kernel(nc, *args)
    r = _run(nc, [sent], core_ids=[0])
    return r.results[0]["out_0"]
```
